# Optimizing a Trainium2 kernel written in Bass

```python
import numpy as np
import jax
import jax.numpy as jnp

def _softmax(x, axis=-1):
    return jax.nn.softmax(x, axis=axis)

def _gelu(x):
    return jax.nn.gelu(x, approximate=True)

def _silu(x):
    return jax.nn.silu(x)

def _sigmoid(x):
    return jax.nn.sigmoid(x)

def _layernorm(x, axis=-1, eps=1e-05):
    m = jnp.mean(x, axis=axis, keepdims=True)
    v = jnp.var(x, axis=axis, keepdims=True)
    return (x - m) / jnp.sqrt(v + eps)

def _scatter_add(tgt, idx, src, axis=0):
    return tgt.at[idx].add(src)

def _segment_sum(src, seg, n):
    return jax.ops.segment_sum(src, seg, n)
kernel_name = 'mk_gnn_preln_d4_gnn_r64_1dd719'

def setup_inputs(seed: int=0):
    np.random.seed(seed)
    _w = jnp.asarray

    def _rec_inputs():
        import jax
        import jax.numpy as jnp
        _gk = jax.random.key(seed)
        x = -0.0005121 + 1.001 * jax.random.normal(jax.random.fold_in(_gk, 1), (100000, 64), jnp.float32)
        src = jax.random.randint(jax.random.fold_in(_gk, 2), (50000,), 0, 100000, jnp.int32)
        dst = jax.random.randint(jax.random.fold_in(_gk, 3), (50000,), 0, 100000, jnp.int32)
        _o = jnp.argsort(dst, stable=True)
        src = src[_o]
        dst = dst[_o]
        return (x, src, dst)
    x, src, dst = _rec_inputs()

    def _L0_gnn_setup():
        import jax, jax.numpy as jnp
        import numpy as np
        N, E, D = (50000, 12500, 64)
        key = jax.random.key(seed)
        ks = jax.random.split(key, 8)
        s = 1.0 / np.sqrt(2 * D)
        inp = {'node_emb': jax.random.normal(ks[0], (N, D), dtype=jnp.float32), 'edge_index': jax.random.randint(ks[1], (2, E), 0, N, dtype=jnp.int64), 'W1': jax.random.normal(ks[2], (2 * D, D), dtype=jnp.float32) * s, 'b1': jnp.zeros((D,), dtype=jnp.float32), 'W2': jax.random.normal(ks[3], (D, D), dtype=jnp.float32) * (1.0 / np.sqrt(D)), 'b2': jnp.zeros((D,), dtype=jnp.float32), 'Wg': jax.random.normal(ks[4], (D, D), dtype=jnp.float32) * (1.0 / np.sqrt(D)), 'bg': jnp.zeros((D,), dtype=jnp.float32)}
        return inp
    _L0_gnn_all = _L0_gnn_setup()
    _L0_gnn_in = {k: v for k, v in _L0_gnn_all.items() if k in ('W1', 'b1', 'W2', 'b2', 'Wg', 'bg')}
    del _L0_gnn_all

    def _L1_gnn_setup():
        import jax, jax.numpy as jnp
        import numpy as np
        NUM_NODES = 100000
        EMBED_DIM = 64
        NUM_LAYERS = 3
        NUM_EDGES = 50000
        key = jax.random.key(seed)
        k1, k2 = jax.random.split(key)
        bound = float(np.sqrt(6.0 / (NUM_NODES + EMBED_DIM)))
        emb = jax.random.uniform(k1, (NUM_NODES, EMBED_DIM), dtype=jnp.float32, minval=-bound, maxval=bound)
        edge_index = jax.random.randint(k2, (2, NUM_EDGES), 0, NUM_NODES, dtype=jnp.int64)
        return {'emb': emb, 'edge_index': edge_index}
    _L1_gnn_all = _L1_gnn_setup()
    _L1_gnn_in = {k: v for k, v in _L1_gnn_all.items() if k in ()}
    del _L1_gnn_all

    def _L2_gnn_setup():
        import jax, jax.numpy as jnp
        import numpy as np
        N_NODES = 100000
        N_EDGES = 1250000
        D_FEAT = 64
        key = jax.random.key(seed)
        k1, k2 = jax.random.split(key)
        edge_index = jax.random.randint(k1, (2, N_EDGES), 0, N_NODES, dtype=jnp.int64)
        x = jax.random.normal(k2, (N_NODES, D_FEAT), dtype=jnp.float32)
        return {'edge_index': edge_index, 'x': x}
    _L2_gnn_all = _L2_gnn_setup()
    _L2_gnn_in = {k: v for k, v in _L2_gnn_all.items() if k in ()}
    del _L2_gnn_all

    def _L3_gnn_setup():
        import jax, jax.numpy as jnp
        import numpy as np
        N_NODES = 100000
        F_IN = 64
        F_OUT = 64
        SLOPE = 0.2
        key = jax.random.key(seed)
        k1, k2, k3, k4 = jax.random.split(key, 4)
        input_matrix = jax.random.normal(k1, (N_NODES, F_IN), dtype=jnp.float32)
        edge_index = jax.random.randint(k2, (2, 25000), 0, N_NODES, dtype=jnp.int64)
        lim_w = float(np.sqrt(6.0 / (F_IN + F_OUT)))
        W = jax.random.uniform(k3, (F_IN, F_OUT), minval=-lim_w, maxval=lim_w, dtype=jnp.float32)
        lim_a = float(np.sqrt(6.0 / (2 * F_OUT + 1)))
        a = jax.random.uniform(k4, (2 * F_OUT,), minval=-lim_a, maxval=lim_a, dtype=jnp.float32)
        return {'input_matrix': input_matrix, 'edge_index': edge_index, 'W': W, 'a': a}
    _L3_gnn_all = _L3_gnn_setup()
    _L3_gnn_in = {k: v for k, v in _L3_gnn_all.items() if k in ('W', 'a')}
    del _L3_gnn_all
    return {'x': x, 'src': src, 'dst': dst, 'L0_gnn_W1': _L0_gnn_in['W1'], 'L0_gnn_b1': _L0_gnn_in['b1'], 'L0_gnn_W2': _L0_gnn_in['W2'], 'L0_gnn_b2': _L0_gnn_in['b2'], 'L0_gnn_Wg': _L0_gnn_in['Wg'], 'L0_gnn_bg': _L0_gnn_in['bg'], 'L3_gnn_W': _L3_gnn_in['W'], 'L3_gnn_a': _L3_gnn_in['a']}

def reference(x, src, dst, L0_gnn_W1, L0_gnn_b1, L0_gnn_W2, L0_gnn_b2, L0_gnn_Wg, L0_gnn_bg, L3_gnn_W, L3_gnn_a):
    import jax
    import jax.numpy as jnp

    def _L0_gnn_ref(node_emb, edge_index, W1, b1, W2, b2, Wg, bg):
        import jax, jax.numpy as jnp
        import numpy as np
        src, dst = (edge_index[0], edge_index[1])
        pair_emb = jnp.concatenate([node_emb[src], node_emb[dst]], axis=-1)
        h = jax.nn.relu(pair_emb @ W1 + b1)
        interaction = h @ W2 + b2
        gate = jax.nn.sigmoid(interaction @ Wg + bg)
        gated = interaction * gate
        N = node_emb.shape[0]
        summed = jax.ops.segment_sum(gated, src, num_segments=N)
        counts = jax.ops.segment_sum(jnp.ones((src.shape[0],), dtype=gated.dtype), src, num_segments=N)
        pooled = summed / jnp.maximum(counts, 1.0)[:, None]
        return pooled

    def _L1_gnn_ref(emb, edge_index):
        import jax, jax.numpy as jnp
        import numpy as np
        NUM_NODES = 100000
        EMBED_DIM = 64
        NUM_LAYERS = 3
        NUM_EDGES = 50000
        n = emb.shape[0]
        row, col = (edge_index[0], edge_index[1])
        ones = jnp.ones(row.shape[0], dtype=emb.dtype)
        deg = jax.ops.segment_sum(ones, col, num_segments=n)
        dinv = jnp.where(deg > 0, jax.lax.rsqrt(jnp.where(deg > 0, deg, 1.0)), 0.0)
        norm = dinv[row] * dinv[col]
        x = emb
        acc = emb
        for _ in range(NUM_LAYERS):
            msgs = x[row] * norm[:, None]
            x = jax.ops.segment_sum(msgs, col, num_segments=n)
            acc = acc + x
        return acc / (NUM_LAYERS + 1)

    def _L2_gnn_ref(edge_index, x):
        import jax, jax.numpy as jnp
        import numpy as np
        N_NODES = 100000
        N_EDGES = 1250000
        D_FEAT = 64
        row, col = (edge_index[0], edge_index[1])
        messages = x[col]
        aggr_out = jax.ops.segment_sum(messages, row, num_segments=x.shape[0])
        return aggr_out

    def _L3_gnn_ref(input_matrix, edge_index, W, a):
        import jax, jax.numpy as jnp
        import numpy as np
        N_NODES = 100000
        F_IN = 64
        F_OUT = 64
        SLOPE = 0.2
        N = input_matrix.shape[0]
        loops = jnp.arange(N, dtype=edge_index.dtype)
        src = jnp.concatenate([edge_index[0], loops])
        dst = jnp.concatenate([edge_index[1], loops])
        h = input_matrix @ W
        F = h.shape[1]
        h_src = h[src]
        h_dst = h[dst]
        alpha = h_src @ a[:F] + h_dst @ a[F:]
        alpha = jnp.where(alpha >= 0, alpha, SLOPE * alpha)
        alpha = jnp.exp(alpha)
        denom = jax.ops.segment_sum(alpha, src, num_segments=N)
        alpha = alpha / denom[src]
        out = jax.ops.segment_sum(h_dst * alpha[:, None], src, num_segments=N)
        return out
    edge_index = jnp.stack([src, dst])
    h = jnp.maximum(_layernorm(x, axis=-1), 0.0)
    x = x + _L0_gnn_ref(h, edge_index, L0_gnn_W1, L0_gnn_b1, L0_gnn_W2, L0_gnn_b2, L0_gnn_Wg, L0_gnn_bg)
    h = jnp.maximum(_layernorm(x, axis=-1), 0.0)
    x = x + _L1_gnn_ref(h, edge_index)
    h = jnp.maximum(_layernorm(x, axis=-1), 0.0)
    x = x + _L2_gnn_ref(edge_index, h)
    h = jnp.maximum(_layernorm(x, axis=-1), 0.0)
    x = x + _L3_gnn_ref(h, edge_index, L3_gnn_W, L3_gnn_a)
    return x

_drawn_inputs = setup_inputs


def setup_inputs(seed=0):
    import zlib

    import numpy as np

    out = dict(_drawn_inputs(seed))
    spreads = {'L0_gnn_b1': (0.0, 0.327), 'L0_gnn_b2': (0.0, 0.1), 'L0_gnn_bg': (0.0, 0.8)}
    factors = {}
    for name, (base, spread) in spreads.items():
        noise = np.random.default_rng([zlib.crc32(name.encode()), seed]).standard_normal(out[name].shape)
        drawn = base * np.exp(spread * noise) if base else spread * noise
        out[name] = jnp.asarray(drawn.astype(out[name].dtype))
    for name, factor in factors.items():
        out[name] = (out[name] * factor).astype(out[name].dtype)
    return out
```

```python
import concourse.bass as bass
from concourse import mybir
from contextlib import ExitStack

P = 128
D = 64
J = 8
TILE = P * J
LANES = 128
CH = 4
GROUP = CH * LANES
R = 4
AHEAD = 2
IDX_AHEAD = 3
NR = 5
EPS = 1e-5
SLOPE = 0.2
HOPS = 3

fp32 = mybir.dt.float32
fp16 = mybir.dt.float16
i32 = mybir.dt.int32
ALU = mybir.AluOpType
ACT = mybir.ActivationFunctionType
AX_X = mybir.AxisListType.X


class Signal:

    def __init__(self, sem):
        self.sem, self.base = sem, 0

    def at(self, n):
        return n + self.base

    def end(self, n):
        self.base += n


def ring_cycle(eng, n, slots, step):
    turns = n // slots
    for g in range(min(slots, n)):
        step(g, g, 0)
    if turns > 1:
        with eng.Fori(1, turns) as turn:
            for s in range(slots):
                step(turn * slots + s, s, turn)
    for g in range(max(turns, 1) * slots, n):
        step(g, g % slots, g // slots)


def not_first(turn):
    return not (isinstance(turn, int) and turn == 0)


class Memory:

    def __init__(self, nc, name):
        self.nc, self.name, self.stack = nc, name, ExitStack()

    def __enter__(self):
        self.stack.__enter__()
        return self

    def __exit__(self, *why):
        return self.stack.__exit__(*why)

    def tile(self, name, shape, dt=fp32):
        return self.stack.enter_context(self.nc.sbuf_tensor(f"{self.name}_{name}", shape, dt))

    def ring(self, name, slots, shape, dt=fp32):
        return [self.tile(f"{name}{s}", shape, dt) for s in range(slots)]


def not_zero(g):
    return not (isinstance(g, int) and g == 0)


def gnn_kernel(nc, x, src, dst, W1, b1, W2, b2, Wg, bg, W3, a3, out):
    N = x.shape[0]
    E = src.shape[0]
    TILES = -(-N // TILE)
    NPAD = TILES * TILE
    LAST_P = (N - (TILES - 1) * TILE) // J
    assert (N - (TILES - 1) * TILE) % J == 0
    GROUPS = -(-E // GROUP)
    CHUNKS = GROUPS * CH
    assert GROUPS <= P and E > (CHUNKS - 2) * LANES
    HI = TILES * J
    ROWS = N + (1 + CH) * LANES
    FULL = E // LANES
    REST = E - FULL * LANES
    A = D + 1

    with ExitStack() as ctx:
        def sb(name, shape, dt=fp32):
            return ctx.enter_context(nc.sbuf_tensor(name, shape, dt))

        def ps(name, shape, dt=fp32):
            return ctx.enter_context(nc.psum_tensor(name, shape, dt))

        def signal(name):
            return Signal(ctx.enter_context(nc.semaphore(name)))

        def table(name, rows, width):
            return nc.dram_tensor(name, (rows, width), fp32, kind="Internal").ap()

        h_tab = table("h_tab", NPAD, D)
        y_tab = table("y_tab", NPAD, D)
        x1_tab = table("x1_tab", NPAD, D)
        x2_tab = table("x2_tab", ROWS, D)
        pool_tab = table("pool_tab", ROWS, D)
        hop_tab = [table(f"hop_tab{k}", ROWS, D) for k in range(HOPS)]
        hw_tab = table("hw_tab", NPAD, A)
        as_tab = table("as_tab", NPAD, 1)
        att_tab = table("att_tab", ROWS, A)
        x_end = table("x_end", TILE, D)
        src_row = nc.dram_tensor("src_row", (CHUNKS * LANES,), fp32, kind="Internal").ap()
        dst_row = nc.dram_tensor("dst_row", (CHUNKS * LANES,), fp32, kind="Internal").ap()

        def tile_of(tab, g):
            return tab[0:NPAD, :].rearrange("(g p j) d -> g p (j d)", p=P, j=J)[bass.ds(g, 1)].rearrange(
                "g p n -> p (g n)")

        ident = sb("ident", [P, P])
        zeros = sb("zeros", [P, 56 * D])
        eps = sb("eps", [P, 1])
        iota_hi = sb("iota_hi", [P, HI], fp16)
        iota_lo = sb("iota_lo", [P, P], fp16)
        earlier = sb("earlier", [P, CH, GROUP])
        dump = sb("dump", [P, CH])
        w1_sb = sb("w1_sb", [P, D])
        b1_sb = sb("b1_sb", [D, 1])
        w2_sb = sb("w2_sb", [A, 2 * D])
        w2T = sb("w2T", [D, A])
        wg_sb = sb("wg_sb", [D, D])
        bg_pad = sb("bg_pad", [A, D])
        w3_sb = sb("w3_sb", [P, 2 * (D + 2)])
        w3_in = sb("w3_in", [P, D])
        w3T = sb("w3T", [D, P])
        a3_sb = sb("a3_sb", [D, 2])

        class Ends:

            def __init__(self, name, dram, row):
                self.dram, self.row = dram, row
                self.col = sb(f"{name}_col", [P, CHUNKS])
                self.gather = sb(f"{name}_gather", [P, CHUNKS], i32)
                self.scatter = sb(f"{name}_scatter", [P, CHUNKS], i32)
                self.to_dump = sb(f"{name}_to_dump", [P, CHUNKS])
                self.hi = sb(f"{name}_hi", [P, CHUNKS])
                self.lo = sb(f"{name}_lo", [P, CHUNKS])

        S = Ends("src", src, src_row)
        T = Ends("dst", dst, dst_row)
        rcnt = sb("rcnt", [P, HI])
        dinv = sb("dinv", [P, HI])
        dinv2 = sb("dinv2", [P, HI])

        psum = ps("psum", [P, 8, 512])
        counts_out = psum[:, 4:6, :].rearrange("p b n -> p (b n)")
        counts_in = psum[:, 6:8, :].rearrange("p b n -> p (b n)")

        s_const = signal("s_const")
        s_iota = signal("s_iota")
        s_rows = signal("s_rows")
        s_wts = signal("s_wts")
        s_rowf = signal("s_rowf")
        s_pt = signal("s_pt")
        s_dc = signal("s_dc")
        s_zero = signal("s_zero")
        s_passed = signal("s_passed")
        s_row = [signal(f"s_row{s}") for s in range(R)]
        s_gidx = signal("s_gidx")
        s_sidx = signal("s_sidx")
        s_same = signal("s_same")
        s_before = signal("s_before")
        s_shift = signal("s_shift")
        s_snew = signal("s_snew")
        s_got = [signal(f"s_got{s}") for s in range(R)]
        s_vals = signal("s_vals")
        s_summed = signal("s_summed")
        s_sums = signal("s_sums")
        s_scat = signal("s_scat")
        s_tr = signal("s_tr")
        s_trc = signal("s_trc")
        s_m1 = signal("s_m1")
        s_m1c = signal("s_m1c")
        s_m2 = signal("s_m2")
        s_gate = signal("s_gate")
        s_ones = signal("s_ones")
        s_hot = signal("s_hot")
        s_cnt = signal("s_cnt")
        s_lin = signal("s_lin")
        s_leaky = signal("s_leaky")
        s_ex = signal("s_ex")
        s_in = [signal(f"s_in{s}") for s in range(NR)]
        s_out = [signal(f"s_out{s}") for s in range(NR)]
        s_pre = signal("s_pre")
        s_u = signal("s_u")
        s_v = signal("s_v")
        s_x = signal("s_x")
        s_sum = signal("s_sum")
        s_mean = signal("s_mean")
        s_cen = signal("s_cen")
        s_sqr = signal("s_sqr")
        s_ssq = signal("s_ssq")
        s_std = signal("s_std")
        s_rstd = signal("s_rstd")
        s_hn = signal("s_hn")
        s_ready = signal("s_ready")
        s_t3 = signal("s_t3")

        def passed(pool, n):
            if not isinstance(n, int):
                pool.sem_inc(s_passed.sem, 1)

        def zero_table(eng, tab, done):
            rows, n, at, step, width = ROWS, 0, 0, 56, D
            while rows - at >= P:
                k = min(step, (rows - at) // P)
                eng.dma_start(tab[at:at + P * k, :].rearrange("(p r) d -> p (r d)", p=P),
                              zeros[:, 0:k * width]).then_inc(done.sem, 16)
                at += P * k
                n += 1
            if rows > at:
                eng.dma_start(tab[at:rows, :], zeros[0:rows - at, 0:width]).then_inc(done.sem, 16)
                n += 1
            return n

        def bc(ap):
            return ap.unsqueeze(2).to_broadcast([P, ap.shape[1], D])

        def rows3(t, w=D):
            return t[:, :].rearrange("p (j d) -> p j d", d=w)

        with Memory(nc, "prep") as m, nc.Block() as block:
            bits = m.ring("bits", 4, [P, CHUNKS], i32)
            for e, name in ((S, "src"), (T, "dst")):
                e.rows_i = m.tile(f"{name}_rows_i", [GROUPS, CH, LANES], i32)
                e.rows_f = m.tile(f"{name}_rows_f", [GROUPS, CH, LANES])

            @block.gpsimd
            def _(pool):
                pool.iota(S.rows_i[:, :, :], [[0, CH], [1, LANES]], base=N, channel_multiplier=0).then_inc(s_iota.sem, 1)
                pool.iota(T.rows_i[:, :, :], [[0, CH], [1, LANES]], base=N, channel_multiplier=0).then_inc(s_iota.sem, 1)
                pool.memset(ident[:, :], 0.0).then_inc(s_const.sem, 1)
                pool.memset(bg_pad[:, :], 0.0).then_inc(s_const.sem, 1)
                pool.memset(w3_sb[:, :], 0.0).then_inc(s_const.sem, 1)
                pool.memset(earlier[:, :, :], 1.0).then_inc(s_const.sem, 1)
                pool.memset(zeros[:, :], 0.0).then_inc(s_const.sem, 1)
                pool.memset(eps[:, :], EPS).then_inc(s_const.sem, 1)
                pool.iota(iota_hi[:, :], [[1, HI]], base=0, channel_multiplier=0,
                          allow_small_or_imprecise_dtypes=True).then_inc(s_const.sem, 1)
                pool.iota(iota_lo[:, :], [[1, P]], base=0, channel_multiplier=0,
                          allow_small_or_imprecise_dtypes=True).then_inc(s_const.sem, 1)
                pool.iota(dump[:, :], [[LANES, CH]], base=N + LANES, channel_multiplier=1,
                          allow_small_or_imprecise_dtypes=True).then_inc(s_const.sem, 1)
                pool.wait_ge(s_const.sem, s_const.at(9))
                pool.affine_select(out=ident[:, :], in_=ident[:, :], compare_op=ALU.not_equal, fill=1.0,
                                   base=0, pattern=[[-1, P]], channel_multiplier=1).then_inc(s_const.sem, 1)
                for i in range(CH):
                    pool.affine_select(out=earlier[:, i, :], in_=earlier[:, i, :], compare_op=ALU.is_gt, fill=0.0,
                                       base=LANES * i, pattern=[[-1, GROUP]],
                                       channel_multiplier=1).then_inc(s_const.sem, 1)

            @block.sync
            def _(sp):
                sp.wait_ge(s_iota.sem, s_iota.at(2))
                for e in (S, T):
                    whole = FULL // GROUPS
                    sp.dma_start(e.rows_i[:, 0:whole, :], e.dram[0:whole * GROUPS * LANES].rearrange(
                        "(t c m) -> c t m", c=GROUPS, m=LANES)).then_inc(s_rows.sem, 16)
                    more = FULL - whole * GROUPS
                    sp.dma_start(e.rows_i[0:more, whole, :], e.dram[whole * GROUPS * LANES:FULL * LANES].rearrange(
                        "(c m) -> c m", m=LANES)).then_inc(s_rows.sem, 16)
                    sp.dma_start(e.rows_i[more:more + 1, whole, 0:REST], e.dram[FULL * LANES:E].rearrange(
                        "(c m) -> c m", c=1)).then_inc(s_rows.sem, 16)
                sp.wait_ge(s_const.sem, s_const.at(9))
                sp.dma_start(w1_sb[:, :], W1).then_inc(s_wts.sem, 16)
                sp.dma_start(b1_sb[:, :], b1.rearrange("(p o) -> p o", o=1)).then_inc(s_wts.sem, 16)
                sp.dma_start(w2_sb[0:D, 0:D], W2).then_inc(s_wts.sem, 16)
                sp.dma_start(w2_sb[D:A, 0:D], b2.rearrange("(o n) -> o n", o=1)).then_inc(s_wts.sem, 16)
                sp.dma_start(wg_sb[:, :], Wg).then_inc(s_wts.sem, 16)
                sp.dma_start(bg_pad[D:A, :], bg.rearrange("(o n) -> o n", o=1)).then_inc(s_wts.sem, 16)
                for k in range(2):
                    sp.dma_start(w3_in[k * D:(k + 1) * D, :], W3).then_inc(s_wts.sem, 16)
                    sp.dma_start(w3_sb[k * D:(k + 1) * D, k * (D + 2):k * (D + 2) + D], W3).then_inc(s_wts.sem, 16)
                for k in range(2):
                    sp.dma_start(a3_sb[:, k:k + 1], a3[(1 - k) * D:(2 - k) * D].rearrange(
                        "(p o) -> p o", o=1)).then_inc(s_wts.sem, 16)
                sp.wait_ge(s_dc.sem, s_dc.at(2))
                for e in (S, T):
                    sp.dma_start(e.row.rearrange("(t c m) -> c t m", c=GROUPS, m=LANES),
                                 e.rows_f[:, :, :]).then_inc(s_rowf.sem, 16)
                sp.dma_start(x_end.rearrange("(p j) d -> p (j d)", j=J), zeros[:, 0:J * D]).then_inc(s_rowf.sem, 16)
                sp.wait_ge(s_rowf.sem, s_rowf.at(48))
                sp.dma_start(x_end[0:N - (TILES - 1) * TILE, :], x[(TILES - 1) * TILE:N, :]).then_inc(s_rowf.sem, 16)
                sp.wait_ge(s_rowf.sem, s_rowf.at(64))

            @block.tensor
            def _(pe):
                pe.wait_ge(s_const.sem, s_const.at(10))
                pe.wait_ge(s_dc.sem, s_dc.at(2))
                for n, e in enumerate((S, T)):
                    for t in range(CH):
                        last = pe.transpose(psum[:, n, t * GROUPS:(t + 1) * GROUPS], e.rows_f[:, t, :],
                                            ident[0:GROUPS, 0:GROUPS])
                    last.then_inc(s_pt.sem, 1)
                pe.wait_ge(s_wts.sem, s_wts.at(16 * 12))
                pe.transpose(psum[0:D, 2, 0:A], w2_sb[:, 0:D], ident[0:A, 0:A]).then_inc(s_pt.sem, 1)
                pe.transpose(psum[0:D, 3, 0:P], w3_in[:, :], ident[:, :]).then_inc(s_pt.sem, 1)
                pe.wait_ge(s_trc.sem, s_trc.at(2))
                pe.matmul(psum[0:A, 4, 0:D], w2T[:, :], wg_sb[:, :], start=True, stop=True).then_inc(s_pt.sem, 1)
                pe.matmul(psum[:, 5, 0:2], w3T[:, :], a3_sb[:, :], start=True, stop=True).then_inc(s_pt.sem, 1)

            @block.scalar
            def _(act):
                act.wait_ge(s_pt.sem, s_pt.at(3))
                act.copy(w2T[:, :], psum[0:D, 2, 0:A]).then_inc(s_trc.sem, 1)
                act.wait_ge(s_pt.sem, s_pt.at(4))
                act.copy(w3T[:, :], psum[0:D, 3, 0:P]).then_inc(s_trc.sem, 1)
                act.wait_ge(s_pt.sem, s_pt.at(6))
                for k in range(2):
                    o = k * (D + 2) + D
                    act.copy(w3_sb[k * D:(k + 1) * D, o:o + 2], psum[k * D:(k + 1) * D, 5, 0:2])

            @block.vector
            def _(dve):
                dve.wait_ge(s_rows.sem, s_rows.at(16 * 6))
                for e in (S, T):
                    dve.tensor_copy(e.rows_f[:, :, :], e.rows_i[:, :, :]).then_inc(s_dc.sem, 1)
                n = 2
                dve.wait_ge(s_const.sem, s_const.at(14))
                for k, e in enumerate((S, T)):
                    dve.wait_ge(s_pt.sem, s_pt.at(k + 1))
                    dve.tensor_copy(e.col[:, :], psum[:, k, 0:CHUNKS])
                    dve.tensor_copy(e.gather[:, :], psum[:, k, 0:CHUNKS]).then_inc(s_dc.sem, 1)
                    n += 1
                    dve.wait_ge(s_dc.sem, s_dc.at(n))
                    dve.tensor_scalar(bits[0][:, :], e.gather[:, :], 10, 3, ALU.logical_shift_right,
                                      ALU.logical_shift_left)
                    dve.tensor_scalar(bits[1][:, :], e.gather[:, :], 7, None, ALU.bitwise_and)
                    dve.tensor_scalar(bits[2][:, :], e.gather[:, :], 3, P - 1, ALU.logical_shift_right,
                                      ALU.bitwise_and)
                    dve.tensor_tensor(e.to_dump[:, :].rearrange("p (g c) -> p g c", c=CH),
                                      dump[:, :].unsqueeze(1).to_broadcast([P, GROUPS, CH]),
                                      e.col[:, :].rearrange("p (g c) -> p g c", c=CH),
                                      ALU.subtract).then_inc(s_dc.sem, 1)
                    n += 1
                    dve.wait_ge(s_dc.sem, s_dc.at(n))
                    dve.tensor_tensor(bits[3][:, :], bits[0][:, :], bits[1][:, :], ALU.bitwise_or)
                    dve.tensor_copy(e.lo[:, :], bits[2][:, :]).then_inc(s_dc.sem, 1)
                    n += 1
                    dve.wait_ge(s_dc.sem, s_dc.at(n))
                    dve.tensor_copy(e.hi[:, :], bits[3][:, :]).then_inc(s_dc.sem, 1)
                    n += 1
                    dve.wait_ge(s_dc.sem, s_dc.at(n))
                dve.wait_ge(s_pt.sem, s_pt.at(5))
                dve.tensor_tensor(w2_sb[:, D:2 * D], psum[0:A, 4, 0:D], bg_pad[:, :], ALU.add)
        s_pt.end(6)
        s_trc.end(2)
        s_dc.end(10)

        LAG = 2

        def tiles_of(s):
            return -(-(TILES - s) // NR)

        def table_tile(tab, g):
            n = NPAD if tab.shape[0] >= NPAD else (TILES - 1) * TILE
            return tab[0:n, :].rearrange("(g p j) d -> g p (j d)", p=P, j=J)[bass.ds(g, 1)].rearrange(
                "g p n -> p (g n)")

        def tile_loads(sp, loads, used):
            def step(g, s, turn):
                if not_first(turn):
                    sp.wait_ge(used.sem, used.at(g - NR + 1))
                for tab, ring in loads:
                    if tab is x and isinstance(g, int) and g == TILES - 1:
                        part = x_end.rearrange("(p j) d -> p (j d)", j=J)
                    else:
                        part = table_tile(tab, g)
                    sp.dma_start(ring[s][:, :], part).then_inc(s_in[s].sem, 16)
            ring_cycle(sp, TILES - 1, NR, step)
            step(TILES - 1, (TILES - 1) % NR, (TILES - 1) // NR)

        def tile_stores(act, stores, g, s):
            for tab, ring in stores:
                if tab is out and isinstance(g, int) and g == TILES - 1:
                    act.dma_start(out[(TILES - 1) * TILE:N, :].rearrange("(p j) d -> p (j d)", j=J),
                                  ring[s][0:LAST_P, :]).then_inc(s_out[s].sem, 16)
                else:
                    act.dma_start(table_tile(tab, g), ring[s][:, :]).then_inc(s_out[s].sem, 16)

        def end_tiles(loads, stores, signals):
            for s in range(NR):
                s_in[s].end(16 * len(loads) * tiles_of(s))
                s_out[s].end(16 * len(stores) * tiles_of(s))
            for sig in signals:
                sig.end(TILES)

        def norm_phase(m, hn, loads, stores, resid, before=None, after=None, pool_first=None, zero=(), spare=None,
                       project=None, stored_resid=False):
            zeroed = []
            cen = m.ring("cen", NR, [P, J * D])
            sqr = m.ring("sqr", NR, [P, J * D])
            rowsum, mean, sumsq, std, rstd = (m.ring(name, NR, [P, J]) for name in (
                "rowsum", "mean", "sumsq", "std", "rstd"))
            if project:
                hT = m.tile("hT", [P, J * D])
                lin, leaky, ex = (m.ring(name, NR, [P, J]) for name in ("lin", "leaky", "ex"))
            ready = s_ready if after or project else s_hn

            with nc.Block() as block:
                @block.sync
                def _(sp):
                    tile_loads(sp, loads, ready)

                @block.gpsimd
                def _(pool):
                    def step(g, s, turn):
                        if pool_first:
                            pool.wait_ge(s_in[s].sem, s_in[s].at(16 * len(loads) * (turn + 1)))
                            if not_first(turn):
                                pool.wait_ge(s_x.sem, s_x.at(g - NR + 1))
                            pool_first(pool, g, s)
                        pool.wait_ge(s_mean.sem, s_mean.at(g + 1))
                        if not_first(turn):
                            pool.wait_ge(s_hn.sem, s_hn.at(g - NR + 1))
                        pool.tensor_tensor(rows3(cen[s]), rows3(resid[s]), bc(mean[s][:, :]),
                                           ALU.add).then_inc(s_cen.sem, 1)
                    ring_cycle(pool, TILES, NR, step)

                @block.vector
                def _(dve):
                    def part_a(g, s, turn):
                        dve.wait_ge(s_in[s].sem, s_in[s].at(16 * len(loads) * (turn + 1)))
                        if stored_resid and not_first(turn):
                            dve.wait_ge(s_out[s].sem, s_out[s].at(16 * len(stores) * turn))
                        if before:
                            before(dve, g, s)
                            dve.wait_ge(s_x.sem, s_x.at(g + 1))
                        dve.tensor_reduce(rowsum[s][:, :], rows3(resid[s]), AX_X, ALU.add).then_inc(s_sum.sem, 1)
                        dve.wait_ge(s_sum.sem, s_sum.at(g + 1))
                        dve.tensor_scalar(mean[s][:, :], rowsum[s][:, :], -1.0 / D, None,
                                          ALU.mult).then_inc(s_mean.sem, 1)

                    def squares_sum(g, s, turn):
                        dve.wait_ge(s_sqr.sem, s_sqr.at(g + 1))
                        dve.tensor_reduce(sumsq[s][:, :], rows3(sqr[s]), AX_X, ALU.add).then_inc(s_ssq.sem, 1)

                    def part_b(g, s, turn):
                        dve.wait_ge(s_std.sem, s_std.at(g + 1))
                        dve.reciprocal(rstd[s][:, :], std[s][:, :]).then_inc(s_rstd.sem, 1)
                        dve.wait_ge(s_rstd.sem, s_rstd.at(g + 1))
                        if not_first(turn):
                            dve.wait_ge(s_out[s].sem, s_out[s].at(16 * len(stores) * turn))
                        dve.scalar_tensor_tensor(rows3(hn[s]), rows3(cen[s]), 0.0, bc(rstd[s][:, :]),
                                                 ALU.max, ALU.mult).then_inc(s_hn.sem, 1)
                        if after:
                            dve.wait_ge(s_hn.sem, s_hn.at(g + 1))
                            after(dve, g, s)

                    def part_c(g, s, turn):
                        hw, as_, _ = project
                        dve.wait_ge(s_t3.sem, s_t3.at(g + 1))
                        dve.tensor_tensor(lin[s][:, :].unsqueeze(2), rows3(hw[s], A)[:, :, D:A],
                                          as_[s][:, :].unsqueeze(2), ALU.add).then_inc(s_lin.sem, 1)
                        dve.wait_ge(s_lin.sem, s_lin.at(g + 1))
                        dve.scalar_tensor_tensor(leaky[s][:, :], lin[s][:, :], SLOPE, lin[s][:, :],
                                                 ALU.mult, ALU.max).then_inc(s_leaky.sem, 1)

                    def part_d(g, s, turn):
                        hw, _, att = project
                        dve.wait_ge(s_ex.sem, s_ex.at(g + 1))
                        dve.tensor_tensor(rows3(att[s], A)[:, :, 0:D], rows3(hw[s], A)[:, :, 0:D], bc(ex[s][:, :]),
                                          ALU.mult)
                        dve.tensor_copy(rows3(att[s], A)[:, :, D:A],
                                        ex[s][:, :].unsqueeze(2)).then_inc(s_ready.sem, 1)

                    def behind(part, g, s, turn, n):
                        if not isinstance(turn, int) or g >= n:
                            part(g - n, (s - n) % NR, turn - (1 if s < n else 0))

                    def both(g, s, turn):
                        ahead = s + LAG
                        if not isinstance(turn, int) or g + LAG < TILES:
                            part_a(g + LAG, ahead % NR, turn + ahead // NR)
                        if not isinstance(turn, int) or g + 1 < TILES:
                            squares_sum(g + 1, (s + 1) % NR, turn)
                        part_b(g, s, turn)
                        if project:
                            behind(part_c, g, s, turn, 1)
                            behind(part_d, g, s, turn, 2)

                    for g in range(LAG):
                        part_a(g, g, 0)
                    squares_sum(0, 0, 0)
                    turns = (TILES - LAG) // NR
                    for g in range(NR):
                        both(g, g, 0)
                    with dve.Fori(1, turns) as turn:
                        for s in range(NR):
                            both(turn * NR + s, s, turn)
                    for g in range(turns * NR, TILES):
                        both(g, g % NR, g // NR)
                    if project:
                        part_c(TILES - 1, (TILES - 1) % NR, (TILES - 1) // NR)
                        part_d(TILES - 2, (TILES - 2) % NR, (TILES - 2) // NR)
                        part_d(TILES - 1, (TILES - 1) % NR, (TILES - 1) // NR)

                @block.tensor
                def _(pe):
                    def step(g, s, turn):
                        pe.wait_ge(s_hn.sem, s_hn.at(g + 1))
                        if not_zero(g):
                            pe.wait_ge(s_trc.sem, s_trc.at(g))
                        for k in range(J // 2):
                            last = pe.transpose(psum[:, 0, k * P:(k + 1) * P], hn[s][:, k * P:(k + 1) * P], ident[:, :])
                        last.then_inc(s_tr.sem, 1)
                        pe.wait_ge(s_trc.sem, s_trc.at(g + 1))
                        if not_zero(g):
                            pe.wait_ge(s_t3.sem, s_t3.at(g))
                        for k in range(J // 2):
                            o = (k % 2) * 2 * (D + 2)
                            last = pe.matmul(psum[:, 1 + k // 2, o:o + 2 * (D + 2)], hT[:, k * P:(k + 1) * P],
                                             w3_sb[:, :], start=True, stop=True)
                        last.then_inc(s_m1.sem, 1)
                    if project:
                        ring_cycle(pe, TILES, NR, step)

                @block.scalar
                def _(act):
                    n = 0
                    for tab in zero:
                        n += zero_table(act, tab, s_zero)
                    zeroed.append(n)
                    if spare is not None:
                        width = spare.shape[1]
                        act.dma_start(spare[NPAD:ROWS, :].rearrange("(p r) d -> p (r d)", r=4),
                                      zeros[0:(ROWS - NPAD) // 4, 0:4 * width]).then_inc(s_zero.sem, 16)
                        zeroed[0] += 1

                    def square(g, s, turn):
                        act.wait_ge(s_cen.sem, s_cen.at(g + 1))
                        if not_first(turn):
                            act.wait_ge(s_ssq.sem, s_ssq.at(g - NR + 1))
                        act.activation(sqr[s][:, :], cen[s][:, :], ACT.Square).then_inc(s_sqr.sem, 1)

                    def root(g, s, turn):
                        act.wait_ge(s_ssq.sem, s_ssq.at(g + 1))
                        act.activation(std[s][:, :], sumsq[s][:, :], ACT.Sqrt, bias=eps[:, :],
                                       scale=1.0 / D).then_inc(s_std.sem, 1)

                    def products(g, s, turn):
                        hw, as_, _ = project
                        act.wait_ge(s_tr.sem, s_tr.at(g + 1))
                        if not_zero(g):
                            act.wait_ge(s_m1.sem, s_m1.at(g))
                        act.copy(hT[:, :], psum[:, 0, :]).then_inc(s_trc.sem, 1)
                        if not_first(turn):
                            act.wait_ge(s_out[s].sem, s_out[s].at(16 * len(stores) * turn))
                        act.wait_ge(s_m1.sem, s_m1.at(g + 1))
                        for b in range(2):
                            got_b = psum[:, 1 + b, 0:4 * (D + 2)].rearrange("p (r w) -> p r w", w=D + 2)
                            act.copy(rows3(hw[s], A)[:, 4 * b:4 * b + 4, :], got_b[:, :, 0:A])
                            last = act.copy(as_[s][:, 4 * b:4 * b + 4].unsqueeze(2), got_b[:, :, A:A + 1])
                        last.then_inc(s_t3.sem, 1)

                    def exps(g, s, turn):
                        act.wait_ge(s_leaky.sem, s_leaky.at(g + 1))
                        act.activation(ex[s][:, :], leaky[s][:, :], ACT.Exp).then_inc(s_ex.sem, 1)

                    def store(g, s, turn):
                        act.wait_ge(ready.sem, ready.at(g + 1))
                        tile_stores(act, stores, g, s)

                    def behind(part, g, s, turn, n):
                        if not isinstance(turn, int) or g >= n:
                            part(g - n, (s - n) % NR, turn - (1 if s < n else 0))

                    def step(g, s, turn):
                        ahead = s + LAG
                        if not isinstance(g, int) or g + LAG < TILES:
                            square(g + LAG, ahead % NR, turn + ahead // NR)
                        if not isinstance(turn, int) or g + 1 < TILES:
                            root(g + 1, (s + 1) % NR, turn)
                        if project:
                            products(g, s, turn)
                            behind(exps, g, s, turn, 1)
                            behind(store, g, s, turn, 2)
                        else:
                            store(g, s, turn)
                    for g in range(LAG):
                        square(g, g, 0)
                    root(0, 0, 0)
                    turns = (TILES - LAG) // NR
                    for g in range(NR):
                        step(g, g, 0)
                    with act.Fori(1, turns) as turn:
                        for s in range(NR):
                            step(turn * NR + s, s, turn)
                    for g in range(turns * NR, TILES):
                        step(g, g % NR, g // NR)
                    if project:
                        exps(TILES - 1, (TILES - 1) % NR, 0)
                        for g in (TILES - 2, TILES - 1):
                            store(g, g % NR, 0)
                    if zeroed[0]:
                        act.wait_ge(s_zero.sem, s_zero.at(16 * zeroed[0]))
                    for s in range(NR):
                        act.wait_ge(s_out[s].sem, s_out[s].at(16 * len(stores) * tiles_of(s)))

            s_zero.end(16 * zeroed[0])
            end_tiles(loads, stores, [s_hn, s_sum, s_mean, s_cen, s_sqr, s_ssq, s_std, s_rstd]
                      + [s_ready] * bool(after or project) + [s_x] * bool(before)
                      + [s_pre] * bool(pool_first)
                      + [s_tr, s_trc, s_m1, s_t3, s_lin, s_leaky, s_ex] * bool(project))

        def plain_phase(loads, stores, compute, more=()):
            with nc.Block() as block:
                @block.sync
                def _(sp):
                    tile_loads(sp, loads, s_ready)

                @block.vector
                def _(dve):
                    def step(g, s, turn):
                        dve.wait_ge(s_in[s].sem, s_in[s].at(16 * len(loads) * (turn + 1)))
                        if not_first(turn):
                            dve.wait_ge(s_out[s].sem, s_out[s].at(16 * len(stores) * turn))
                        compute(dve, g, s)
                    ring_cycle(dve, TILES, NR, step)

                @block.scalar
                def _(act):
                    def step(g, s, turn):
                        act.wait_ge(s_ready.sem, s_ready.at(g + 1))
                        tile_stores(act, stores, g, s)
                    ring_cycle(act, TILES - 1, NR, step)
                    step(TILES - 1, (TILES - 1) % NR, (TILES - 1) // NR)
                    for s in range(NR):
                        act.wait_ge(s_out[s].sem, s_out[s].at(16 * len(stores) * tiles_of(s)))
            end_tiles(loads, stores, [s_ready, *more])


        def edges_of(s):
            return -(-(GROUPS - s) // R)

        def edge_phase(name, gathers, by, target, width, make=None, mark=False, count=False, zero=()):
            NG = len(gathers) * CH
            gwidth = max(c + w for _, _, c, w in gathers)
            zeroed = []

            with Memory(nc, name) as m:
                g_idx = m.ring("g_idx", R, [P, len(gathers), CH], i32)
                s_idx = m.ring("s_idx", R, [P, CH], i32)
                got = m.ring("got", R, [P, CH, gwidth])
                same = m.ring("same", R, [P, CH, GROUP])
                sums = m.ring("sums", R, [P, CH, width])
                rowb = m.ring("rowb", R, [P, GROUP])
                vals = m.ring("vals", R, [P, CH, width]) if make else got
                if mark:
                    junk = m.tile("junk", [P, CH, GROUP])
                    n_before = m.tile("n_before", [P, CH])
                    shift = m.tile("shift", [P, CH])
                if count:
                    hot_hi = m.ring("hot_hi", 2, [P, HI], fp16)
                    hot_lo = m.ring("hot_lo", 2, [P, P], fp16)
                    deg1, some, out1, rdeg, root, rroot = (m.tile(n, [P, HI]) for n in (
                        "deg1", "some", "out1", "rdeg", "root", "rroot"))
                if make == "mlp":
                    pairT = m.tile("pairT", [P, GROUP])
                    h1T = m.tile("h1T", [A, GROUP])
                    gate = m.tile("gate", [P, CH, D])
                if make == "attend":
                    lin, leaky, ex = (m.tile(n, [P, CH]) for n in ("lin", "leaky", "ex"))
                rows_used = s_vals if make else s_summed
                block = m.stack.enter_context(nc.Block())

                def cols(t, g):
                    return t[:, bass.ds(g * CH, CH)]

                def col(t, g, i):
                    return t[:, bass.ds(g * CH + i, 1)]

                @block.sync
                def _(sp):
                    def step(g, s, turn):
                        if not_first(turn):
                            sp.wait_ge(s_same.sem, s_same.at(g - R + 1))
                            if mark:
                                sp.wait_ge(s_snew.sem, s_snew.at(g - R + 1))
                        sp.dma_start(rowb[s][:, :], by.row.rearrange("(g e) -> g e", e=GROUP)[
                            bass.ds(g, 1), :].to_broadcast([P, GROUP])).then_inc(s_row[s].sem, 16)
                    ring_cycle(sp, GROUPS, R, step)

                @block.gpsimd
                def _(pool):
                    def gather(g, s, turn):
                        pool.wait_ge(s_gidx.sem, s_gidx.at(g + 1))
                        if not_first(turn):
                            pool.wait_ge(rows_used.sem, rows_used.at(g - R + 1))
                            if make == "mlp":
                                pool.wait_ge(s_tr.sem, s_tr.at(g - R + 1))
                        passed(pool, g)
                        for k, (ends, tab, c, w) in enumerate(gathers):
                            for i in range(CH):
                                pool.indirect_dma_start(got[s][:, i, c:c + w], None, tab,
                                                        bass.IndirectOffsetOnAxis(ap=g_idx[s][:, k, i:i + 1], axis=0)
                                                        ).then_inc(s_got[s].sem, 16)

                    def scatter(g, s, turn):
                        pool.wait_ge(s_sidx.sem, s_sidx.at(g + 1))
                        pool.wait_ge(s_sums.sem, s_sums.at(g + 1))
                        if not_zero(g):
                            pool.wait_ge(s_scat.sem, s_scat.at(16 * CH * g))
                        passed(pool, g)
                        for i in range(CH):
                            pool.indirect_dma_start(target, bass.IndirectOffsetOnAxis(ap=s_idx[s][:, i:i + 1], axis=0),
                                                    sums[s][:, i, :], None, compute_op=ALU.add
                                                    ).then_inc(s_scat.sem, 16)

                    def step(g, s, turn):
                        ahead = s + AHEAD
                        if not isinstance(g, int) or g + AHEAD < GROUPS:
                            gather(g + AHEAD, ahead % R, turn + ahead // R)
                        scatter(g, s, turn)
                    for g in range(AHEAD):
                        gather(g, g, 0)
                    turns = (GROUPS - AHEAD) // R
                    for g in range(R):
                        step(g, g, 0)
                    with pool.Fori(1, turns) as turn:
                        for s in range(R):
                            step(turn * R + s, s, turn)
                    for g in range(turns * R, GROUPS):
                        step(g, g % R, g // R)
                    pool.wait_ge(s_scat.sem, s_scat.at(16 * CH * GROUPS))

                @block.vector
                def _(dve):
                    def gather_index(g, s, turn):
                        if not_first(turn):
                            dve.wait_ge(s_got[s].sem, s_got[s].at(16 * NG * turn))
                        for k, (ends, _, _, _) in enumerate(gathers):
                            last = dve.tensor_scalar(g_idx[s][:, k, :], cols(ends.gather, g), 0.0, None, ALU.add)
                        last.then_inc(s_gidx.sem, 1)

                    def equal_ends(g, s, turn):
                        dve.wait_ge(s_row[s].sem, s_row[s].at(16 * (turn + 1)))
                        if not_first(turn):
                            dve.wait_ge(s_summed.sem, s_summed.at(g - R + 1))
                        for i in range(CH):
                            last = dve.tensor_scalar(same[s][:, i, :], rowb[s][:, :], col(by.col, g, i), None,
                                                     ALU.is_equal)
                        last.then_inc(s_same.sem, 1)

                    def scatter_index(g, s, turn):
                        if mark:
                            for i in range(CH):
                                last = dve.scalar_tensor_tensor(junk[:, i, :], rowb[s][:, :], col(by.col, g, i),
                                                                earlier[:, i, :], ALU.is_equal, ALU.mult,
                                                                accum_out=n_before[:, i:i + 1])
                            last.then_inc(s_before.sem, 1)
                            dve.wait_ge(s_before.sem, s_before.at(g + 1))
                            dve.scalar_tensor_tensor(shift[:, :], n_before[:, :], 1.0, cols(by.to_dump, g),
                                                     ALU.min, ALU.mult).then_inc(s_shift.sem, 1)
                            dve.wait_ge(s_shift.sem, s_shift.at(g + 1))
                            dve.tensor_tensor(cols(by.scatter, g), cols(by.col, g), shift[:, :],
                                              ALU.add).then_inc(s_snew.sem, 1)
                            dve.wait_ge(s_snew.sem, s_snew.at(g + 1))
                        if not_first(turn):
                            dve.wait_ge(s_scat.sem, s_scat.at(16 * CH * (g - R + 1)))
                        dve.tensor_scalar(s_idx[s][:, :], cols(by.scatter, g), 0.0, None, ALU.add).then_inc(s_sidx.sem, 1)

                    def one_hots(g):
                        for i in range(CH):
                            for k, ends in enumerate((S, T)):
                                if not_zero(g) or i:
                                    dve.wait_ge(s_cnt.sem, s_cnt.at(2 * CH * g + 2 * i + k - 1))
                                dve.tensor_scalar(hot_lo[k][:, :], iota_lo[:, :], col(ends.lo, g, i), None, ALU.is_equal)
                                dve.tensor_scalar(hot_hi[k][:, :], iota_hi[:, :], col(ends.hi, g, i), None,
                                                  ALU.is_equal).then_inc(s_hot.sem, 1)

                    def values(g, s, turn):
                        if not_first(turn):
                            dve.wait_ge(s_summed.sem, s_summed.at(g - R + 1))
                        if make == "mlp":
                            dve.wait_ge(s_gate.sem, s_gate.at(g + 1))
                            inter = psum[:, 2, :].rearrange("p (c w) -> p c w", c=CH)[:, :, 0:D]
                            dve.tensor_tensor(vals[s][:, :, :], inter, gate[:, :, :], ALU.mult).then_inc(s_vals.sem, 1)
                        if make == "attend":
                            dve.wait_ge(s_got[s].sem, s_got[s].at(16 * NG * (turn + 1)))
                            dve.tensor_tensor(lin[:, :].unsqueeze(2), got[s][:, :, D:A], got[s][:, :, A:A + 1],
                                              ALU.add).then_inc(s_lin.sem, 1)
                            dve.wait_ge(s_lin.sem, s_lin.at(g + 1))
                            dve.scalar_tensor_tensor(leaky[:, :], lin[:, :], SLOPE, lin[:, :],
                                                     ALU.mult, ALU.max).then_inc(s_leaky.sem, 1)
                            dve.wait_ge(s_ex.sem, s_ex.at(g + 1))
                            dve.tensor_tensor(vals[s][:, :, 0:D], got[s][:, :, 0:D],
                                              ex[:, :].unsqueeze(2).to_broadcast([P, CH, D]), ALU.mult)
                            dve.tensor_copy(vals[s][:, :, D:A], ex[:, :].unsqueeze(2)).then_inc(s_vals.sem, 1)

                    def step(g, s, turn):
                        ahead = s + IDX_AHEAD
                        if not isinstance(g, int) or g + IDX_AHEAD < GROUPS:
                            gather_index(g + IDX_AHEAD, ahead % R, turn + ahead // R)
                        equal_ends(g, s, turn)
                        scatter_index(g, s, turn)
                        if count:
                            one_hots(g)
                        if make:
                            values(g, s, turn)
                    if make == "mlp":
                        dve.memset(h1T[D:A, :], 1.0).then_inc(s_ones.sem, 1)
                    for g in range(IDX_AHEAD):
                        gather_index(g, g, 0)
                    turns = (GROUPS - IDX_AHEAD) // R
                    for g in range(R):
                        step(g, g, 0)
                    with dve.Fori(1, turns) as turn:
                        for s in range(R):
                            step(turn * R + s, s, turn)
                    for g in range(turns * R, GROUPS):
                        step(g, g % R, g // R)
                    if count:
                        dve.wait_ge(s_cnt.sem, s_cnt.at(2 * CH * GROUPS))
                        dve.tensor_scalar(out1[:, :], counts_out[:, 0:HI], 1.0, None, ALU.max)
                        dve.tensor_scalar(some[:, :], counts_in[:, 0:HI], 1.0, None, ALU.min)
                        dve.tensor_scalar(deg1[:, :], counts_in[:, 0:HI], 1.0, None, ALU.max).then_inc(s_lin.sem, 1)
                        dve.wait_ge(s_lin.sem, s_lin.at(1))
                        dve.reciprocal(rcnt[:, :], out1[:, :])
                        dve.reciprocal(rdeg[:, :], deg1[:, :])
                        dve.wait_ge(s_ex.sem, s_ex.at(1))
                        dve.reciprocal(rroot[:, :], root[:, :]).then_inc(s_lin.sem, 1)
                        dve.wait_ge(s_lin.sem, s_lin.at(2))
                        dve.tensor_tensor(dinv[:, :], rroot[:, :], some[:, :], ALU.mult)
                        dve.tensor_tensor(dinv2[:, :], rdeg[:, :], some[:, :], ALU.mult)

                @block.tensor
                def _(pe):
                    def mlp(g, s, turn):
                        pe.wait_ge(s_got[s].sem, s_got[s].at(16 * NG * (turn + 1)))
                        if not_zero(g):
                            pe.wait_ge(s_trc.sem, s_trc.at(g))
                        for i in range(CH):
                            last = pe.transpose(psum[:, 0, i * P:(i + 1) * P], got[s][:, i, :], ident[:, :])
                        last.then_inc(s_tr.sem, 1)
                        pe.wait_ge(s_trc.sem, s_trc.at(g + 1))
                        if not_zero(g):
                            pe.wait_ge(s_m1c.sem, s_m1c.at(g))
                        pe.matmul(psum[0:D, 1, :], w1_sb[:, :], pairT[:, :], start=True, stop=True).then_inc(s_m1.sem, 1)
                        pe.wait_ge(s_m1c.sem, s_m1c.at(g + 1))
                        if not not_zero(g):
                            pe.wait_ge(s_ones.sem, s_ones.at(1))
                        if not_zero(g):
                            pe.wait_ge(s_vals.sem, s_vals.at(g))
                        for i in range(CH):
                            last = pe.matmul(psum[:, 2, i * P:(i + 1) * P], h1T[:, i * P:(i + 1) * P], w2_sb[:, :],
                                             start=True, stop=True)
                        last.then_inc(s_m2.sem, 1)

                    def count_chunks(g):
                        for i in range(CH):
                            for k, counts in enumerate((counts_out, counts_in)):
                                pe.wait_ge(s_hot.sem, s_hot.at(2 * CH * g + 2 * i + k + 1))
                                first = not not_zero(g) and i == 0
                                end = isinstance(g, int) and g == GROUPS - 1 and i == CH - 1
                                pe.matmul(counts[:, 0:512], hot_lo[k][:, :], hot_hi[k][:, 0:512], start=first, stop=end)
                                pe.matmul(counts[:, 512:HI], hot_lo[k][:, :], hot_hi[k][:, 512:HI],
                                          start=first, stop=end).then_inc(s_cnt.sem, 1)

                    def step(g, s, turn):
                        if make == "mlp":
                            mlp(g, s, turn)
                        if count:
                            count_chunks(g)
                        if make:
                            pe.wait_ge(s_vals.sem, s_vals.at(g + 1))
                        else:
                            pe.wait_ge(s_got[s].sem, s_got[s].at(16 * NG * (turn + 1)))
                        pe.wait_ge(s_same.sem, s_same.at(g + 1))
                        if not_zero(g):
                            pe.wait_ge(s_sums.sem, s_sums.at(g))
                        for j in range(CH):
                            for i in range(CH):
                                last = pe.matmul(psum[:, 3, j * width:(j + 1) * width],
                                                 same[s][:, i, j * LANES:(j + 1) * LANES], vals[s][:, i, 0:width],
                                                 start=i == 0, stop=i == CH - 1)
                        last.then_inc(s_summed.sem, 1)
                    ring_cycle(pe, GROUPS, R, step)

                @block.scalar
                def _(act):
                    n = 0
                    for tab in zero:
                        n += zero_table(act, tab, s_zero)
                    zeroed.append(n)

                    def step(g, s, turn):
                        if make == "mlp":
                            act.wait_ge(s_tr.sem, s_tr.at(g + 1))
                            if not_zero(g):
                                act.wait_ge(s_m1.sem, s_m1.at(g))
                            act.copy(pairT[:, :], psum[:, 0, :]).then_inc(s_trc.sem, 1)
                            act.wait_ge(s_m1.sem, s_m1.at(g + 1))
                            if not_zero(g):
                                act.wait_ge(s_m2.sem, s_m2.at(g))
                            act.activation(h1T[0:D, :], psum[0:D, 1, :], ACT.Relu, bias=b1_sb[:, :]).then_inc(s_m1c.sem, 1)
                            act.wait_ge(s_m2.sem, s_m2.at(g + 1))
                            if not_zero(g):
                                act.wait_ge(s_vals.sem, s_vals.at(g))
                            pre = psum[:, 2, :].rearrange("p (c w) -> p c w", c=CH)[:, :, D:2 * D]
                            act.activation(gate[:, :, :], pre, ACT.Sigmoid).then_inc(s_gate.sem, 1)
                        if make == "attend":
                            act.wait_ge(s_leaky.sem, s_leaky.at(g + 1))
                            if not_zero(g):
                                act.wait_ge(s_vals.sem, s_vals.at(g))
                            act.activation(ex[:, :], leaky[:, :], ACT.Exp).then_inc(s_ex.sem, 1)
                        act.wait_ge(s_summed.sem, s_summed.at(g + 1))
                        if not_first(turn):
                            act.wait_ge(s_scat.sem, s_scat.at(16 * CH * (g - R + 1)))
                        act.copy(sums[s][:, :, :].rearrange("p c w -> p (c w)"),
                                 psum[:, 3, 0:CH * width]).then_inc(s_sums.sem, 1)
                    ring_cycle(act, GROUPS, R, step)
                    if count:
                        act.wait_ge(s_lin.sem, s_lin.at(1))
                        act.activation(root[:, :], deg1[:, :], ACT.Sqrt).then_inc(s_ex.sem, 1)
                    if n:
                        act.wait_ge(s_zero.sem, s_zero.at(16 * n))

            s_zero.end(16 * zeroed[0])
            for s in range(R):
                s_row[s].end(16 * edges_of(s))
                s_got[s].end(16 * NG * edges_of(s))
            s_scat.end(16 * CH * GROUPS)
            for sig in ([s_gidx, s_sidx, s_same, s_summed, s_sums] + [s_before, s_shift, s_snew] * bool(mark)
                        + [s_vals] * bool(make) + [s_tr, s_trc, s_m1, s_m1c, s_m2, s_gate] * (make == "mlp")
                        + [s_lin, s_leaky, s_ex] * (make == "attend")):
                sig.end(GROUPS)
            if count:
                s_hot.end(2 * CH * GROUPS)
                s_cnt.end(2 * CH * GROUPS)
                s_lin.end(2)
                s_ex.end(1)
            if make == "mlp":
                s_ones.end(1)

        def degrees(t, g):
            return bc(t[:, bass.ds(g * J, J)])

        with Memory(nc, "n0") as m:
            xt, hn = (m.ring(k, NR, [P, J * D]) for k in ("x", "h"))
            norm_phase(m, hn, [(x, xt)], [(h_tab, hn)], xt, zero=[pool_tab])

        edge_phase("e0", [(S, h_tab, 0, D), (T, h_tab, D, D)], S, pool_tab, D, make="mlp", mark=True, count=True,
                   zero=hop_tab)

        with Memory(nc, "n1") as m:
            xt, pt, scaled, x1, hn, x1h, y = (m.ring(k, NR, [P, J * D]) for k in (
                "x", "p", "scaled", "x1", "h", "x1h", "y"))

            def pool_first(pool, g, s):
                pool.tensor_tensor(rows3(scaled[s]), rows3(pt[s]), degrees(rcnt, g), ALU.mult).then_inc(s_pre.sem, 1)

            def before(dve, g, s):
                dve.wait_ge(s_pre.sem, s_pre.at(g + 1))
                dve.tensor_tensor(x1[s][:, :], xt[s][:, :], scaled[s][:, :], ALU.add).then_inc(s_x.sem, 1)

            def after(dve, g, s):
                dve.scalar_tensor_tensor(x1h[s][:, :], hn[s][:, :], 1.0 / (HOPS + 1), x1[s][:, :], ALU.mult, ALU.add)
                dve.tensor_tensor(rows3(y[s]), rows3(hn[s]), degrees(dinv, g), ALU.mult).then_inc(s_ready.sem, 1)

            norm_phase(m, hn, [(x, xt), (pool_tab, pt)], [(x1_tab, x1h), (y_tab, y)], x1, before, after, pool_first)

        for k in range(HOPS):
            edge_phase(f"e1{k}", [(S, y_tab, 0, D)], T, hop_tab[k], D, mark=k == 0)
            if k < HOPS - 1:
                with Memory(nc, f"n2{k}") as m:
                    hop, y = (m.ring(n, NR, [P, J * D]) for n in ("hop", "y"))

                    def compute(dve, g, s):
                        dve.tensor_tensor(rows3(y[s]), rows3(hop[s]), degrees(dinv2, g),
                                          ALU.mult).then_inc(s_ready.sem, 1)
                    plain_phase([(hop_tab[k], hop)], [(y_tab, y)], compute)

        with Memory(nc, "n3") as m:
            x1, h0, h1, h2, two, three, mixed, x2, hn = (m.ring(k, NR if k not in ("three", "mixed") else 2, [P, J * D])
                                                         for k in ("x1", "h0", "h1", "h2", "two", "three", "mixed", "x2", "h"))

            def pool_first(pool, g, s):
                pool.tensor_tensor(two[s][:, :], h0[s][:, :], h1[s][:, :], ALU.add).then_inc(s_pre.sem, 1)

            def before(dve, g, s):
                dve.wait_ge(s_pre.sem, s_pre.at(g + 1))
                dve.tensor_tensor(three[s % 2][:, :], two[s][:, :], h2[s][:, :], ALU.add).then_inc(s_u.sem, 1)
                dve.wait_ge(s_u.sem, s_u.at(g + 1))
                dve.scalar_tensor_tensor(rows3(mixed[s % 2]), rows3(three[s % 2]), 1.0 / (HOPS + 1), degrees(dinv, g),
                                         ALU.mult, ALU.mult).then_inc(s_v.sem, 1)
                dve.wait_ge(s_v.sem, s_v.at(g + 1))
                dve.tensor_tensor(x2[s][:, :], mixed[s % 2][:, :], x1[s][:, :], ALU.add).then_inc(s_x.sem, 1)

            norm_phase(m, hn, [(x1_tab, x1), (hop_tab[0], h0), (hop_tab[1], h1), (hop_tab[2], h2)],
                       [(x2_tab, x2), (h_tab, hn)], x2, before, pool_first=pool_first, spare=x2_tab, stored_resid=True)
            s_u.end(TILES)
            s_v.end(TILES)

        edge_phase("e2", [(T, h_tab, 0, D)], S, x2_tab, D)

        with Memory(nc, "n4") as m:
            x3, hn = (m.ring(k, NR, [P, J * D]) for k in ("x3", "h"))
            hw, att = (m.ring(k, NR, [P, J * A]) for k in ("hw", "att"))
            as_ = m.ring("as", NR, [P, J])
            norm_phase(m, hn, [(x2_tab, x3)], [(hw_tab, hw), (as_tab, as_), (att_tab, att)], x3,
                       project=(hw, as_, att), spare=att_tab)

        edge_phase("e3", [(T, hw_tab, 0, A), (S, as_tab, A, 1)], S, att_tab, A, make="attend")

        with Memory(nc, "n5") as m:
            x3, share, y = (m.ring(k, NR, [P, J * D]) for k in ("x3", "share", "y"))
            att = m.ring("att", NR, [P, J * A])
            rden = m.ring("rden", NR, [P, J])

            def compute(dve, g, s):
                dve.reciprocal(rden[s][:, :].unsqueeze(2), rows3(att[s], A)[:, :, D:A]).then_inc(s_u.sem, 1)
                dve.wait_ge(s_u.sem, s_u.at(g + 1))
                dve.tensor_tensor(rows3(share[s]), rows3(att[s], A)[:, :, 0:D], bc(rden[s][:, :]),
                                  ALU.mult).then_inc(s_v.sem, 1)
                dve.wait_ge(s_v.sem, s_v.at(g + 1))
                dve.tensor_tensor(y[s][:, :], x3[s][:, :], share[s][:, :], ALU.add).then_inc(s_ready.sem, 1)

            plain_phase([(x2_tab, x3), (att_tab, att)], [(out, y)], compute, more=[s_u, s_v])


_INS = ["x", "src", "dst", "L0_gnn_W1", "L0_gnn_b1", "L0_gnn_W2", "L0_gnn_b2", "L0_gnn_Wg", "L0_gnn_bg",
        "L3_gnn_W", "L3_gnn_a"]


def kernel(**inputs):
    import numpy as _np
    import concourse.bacc as _bacc
    from concourse import mybir as _mybir
    from concourse.bass_utils import run_bass_kernel_spmd as _run

    nc = _bacc.Bacc("TRN2", target_bir_lowering=False, num_devices=1)
    arrays, args = {}, []
    for name in _INS:
        a = _np.ascontiguousarray(inputs[name])
        arrays[f"in_{name}_dram"] = a
        args.append(nc.dram_tensor(f"in_{name}_dram", a.shape, _mybir.dt.from_np(a.dtype), kind="ExternalInput").ap())
    shape = _np.asarray(inputs["x"]).shape
    args.append(nc.dram_tensor("out_0_dram", shape, _mybir.dt.float32, kind="ExternalOutput").ap())
    gnn_kernel(nc, *args)
    r = _run(nc, [arrays], core_ids=[0])
    return r.results[0]["out_0_dram"]
```

```python
import concourse.bass as bass
from concourse import mybir
from contextlib import ExitStack

P = 128
D = 64
J = 8
TILE = P * J
LANES = 128
CH = 4
GROUP = CH * LANES
R = 4
AHEAD = 2
IDX_AHEAD = 3
WC = 5
WIN = WC * LANES
BINC = 28
WR = 4
NR = 6
EPS = 1e-5
SLOPE = 0.2
HOPS = 3

fp32 = mybir.dt.float32
fp16 = mybir.dt.float16
bf16 = mybir.dt.bfloat16
i32 = mybir.dt.int32
ALU = mybir.AluOpType
ACT = mybir.ActivationFunctionType
AX_X = mybir.AxisListType.X


class Signal:

    def __init__(self, sem):
        self.sem, self.base = sem, 0

    def at(self, n):
        return n + self.base

    def end(self, n):
        self.base += n


def ring_cycle(eng, n, slots, step):
    turns = n // slots
    for g in range(min(slots, n)):
        step(g, g, 0)
    if turns > 1:
        with eng.Fori(1, turns) as turn:
            for s in range(slots):
                step(turn * slots + s, s, turn)
    for g in range(max(turns, 1) * slots, n):
        step(g, g % slots, g // slots)


def not_first(turn):
    return not (isinstance(turn, int) and turn == 0)


class GeneralSignals:

    def __init__(self, signal):
        self.gidx = signal("g_gidx")
        self.sidx = signal("g_sidx")
        self.same = signal("g_same")
        self.before = signal("g_before")
        self.shift = signal("g_shift")
        self.snew = signal("g_snew")
        self.vals = signal("g_vals")
        self.summed = signal("g_summed")
        self.sums = signal("g_sums")
        self.scat = signal("g_scat")
        self.tr = signal("g_tr")
        self.trc = signal("g_trc")
        self.m1 = signal("g_m1")
        self.m1c = signal("g_m1c")
        self.m2 = signal("g_m2")
        self.gate = signal("g_gate")
        self.hot = signal("g_hot")
        self.cnt = signal("g_cnt")
        self.lin = signal("g_lin")
        self.leaky = signal("g_leaky")
        self.ex = signal("g_ex")
        self.ones = signal("g_ones")
        self.ready = signal("g_ready")
        self.zero = signal("g_zero")
        self.row = [signal(f"g_row{s}") for s in range(R)]
        self.got = [signal(f"g_got{s}") for s in range(R)]
        self.in_ = [signal(f"g_in_{s}") for s in range(NR)]
        self.out = [signal(f"g_out{s}") for s in range(NR)]


class FastSignals:

    def __init__(self, signal):
        self.gidx = signal("f_gidx")
        self.hot = signal("f_hot")
        self.vals = signal("f_vals")
        self.high = signal("f_high")
        self.rest = signal("f_rest")
        self.mid = signal("f_mid")
        self.pieces = signal("f_pieces")
        self.acc = signal("f_acc")
        self.red = signal("f_red")
        self.fin = signal("f_fin")
        self.tr = signal("f_tr")
        self.trc = signal("f_trc")
        self.m1 = signal("f_m1")
        self.m1c = signal("f_m1c")
        self.m2 = signal("f_m2")
        self.gate = signal("f_gate")
        self.onehot = signal("f_onehot")
        self.cnt = signal("f_cnt")
        self.lin = signal("f_lin")
        self.leaky = signal("f_leaky")
        self.ex = signal("f_ex")
        self.ones = signal("f_ones")
        self.got = [signal(f"f_got{s}") for s in range(WR)]
        self.base = [signal(f"f_base{s}") for s in range(WR)]
        self.out = [signal(f"f_out{s}") for s in range(WR)]


class Memory:

    def __init__(self, nc, name):
        self.nc, self.name, self.stack = nc, name, ExitStack()

    def __enter__(self):
        self.stack.__enter__()
        return self

    def __exit__(self, *why):
        return self.stack.__exit__(*why)

    def tile(self, name, shape, dt=fp32):
        return self.stack.enter_context(self.nc.sbuf_tensor(f"{self.name}_{name}", shape, dt))

    def ring(self, name, slots, shape, dt=fp32):
        return [self.tile(f"{name}{s}", shape, dt) for s in range(slots)]


def not_zero(g):
    return not (isinstance(g, int) and g == 0)


def gnn_kernel(nc, x, src, dst, W1, b1, W2, b2, Wg, bg, W3, a3, out):
    N = x.shape[0]
    E = src.shape[0]
    TILES = -(-N // TILE)
    NPAD = TILES * TILE
    LAST_P = (N - (TILES - 1) * TILE) // J
    assert (N - (TILES - 1) * TILE) % J == 0
    GROUPS = -(-E // GROUP)
    CHUNKS = GROUPS * CH
    assert GROUPS <= P and E > (CHUNKS - 2) * LANES
    HI = TILES * J
    EDGES = CHUNKS * LANES
    assert CHUNKS % BINC == 0 and TILES <= P and TILE == 1024 and E > (CHUNKS - 2) * LANES
    BINS = CHUNKS // BINC
    SPARE = N + 2 * LANES
    ROWS = SPARE + CH * LANES
    FULL = E // LANES
    REST = E - FULL * LANES
    A = D + 1

    with ExitStack() as ctx:
        def sb(name, shape, dt=fp32):
            return ctx.enter_context(nc.sbuf_tensor(name, shape, dt))

        def ps(name, shape, dt=fp32):
            return ctx.enter_context(nc.psum_tensor(name, shape, dt))

        def signal(name):
            return Signal(ctx.enter_context(nc.semaphore(name)))

        def table(name, rows, width):
            return nc.dram_tensor(name, (rows, width), fp32, kind="Internal").ap()

        h_tab = table("h_tab", NPAD, D)
        y_tab = [table(f"y_tab{k}", NPAD, D) for k in range(2)]
        x1_tab = table("x1_tab", NPAD, D)
        x2_tab = table("x2_tab", ROWS, D)
        pool_tab = table("pool_tab", ROWS, D)
        hop_tab = [table(f"hop_tab{k}", ROWS, D) for k in range(HOPS)]
        hw_tab = table("hw_tab", NPAD, A)
        as_tab = table("as_tab", NPAD, 1)
        att_tab = table("att_tab", ROWS, A)
        x_end = table("x_end", TILE, D)
        tile_rows = [nc.dram_tensor(f"{e}_tile_row", (CHUNKS * LANES,), fp16, kind="Internal").ap() for e in ("src", "dst")]
        src_pairs = nc.dram_tensor("src_pairs", (EDGES, 2), i32, kind="Internal").ap()
        dst_pairs = nc.dram_tensor("dst_pairs", (EDGES, 2), i32, kind="Internal").ap()
        src_row = nc.dram_tensor("src_row", (CHUNKS * LANES,), fp32, kind="Internal").ap()
        dst_row = nc.dram_tensor("dst_row", (CHUNKS * LANES,), fp32, kind="Internal").ap()

        def tile_of(tab, g):
            return tab[0:NPAD, :].rearrange("(g p j) d -> g p (j d)", p=P, j=J)[bass.ds(g, 1)].rearrange(
                "g p n -> p (g n)")

        ident = sb("ident", [P, P])
        zeros = sb("zeros", [P, 56 * D])
        eps = sb("eps", [P, 1])
        iota_hi = sb("iota_hi", [P, HI], fp16)
        iota_lo = sb("iota_lo", [P, P], fp16)
        earlier = sb("earlier", [P, CH, GROUP])
        dump = sb("dump", [P, CH])
        w1_sb = sb("w1_sb", [P, D])
        b1_sb = sb("b1_sb", [D, 1])
        w2_sb = sb("w2_sb", [A, 2 * D])
        w2T = sb("w2T", [D, A])
        wg_sb = sb("wg_sb", [D, D])
        bg_pad = sb("bg_pad", [A, D])
        w3_sb = sb("w3_sb", [P, 2 * (D + 2)])
        w3_in = sb("w3_in", [P, D])
        w3T = sb("w3T", [D, P])
        a3_sb = sb("a3_sb", [D, 2])

        class Ends:

            def __init__(self, name, dram, row):
                self.dram, self.row = dram, row
                self.col = sb(f"{name}_col", [P, CHUNKS])
                self.gather = sb(f"{name}_gather", [P, CHUNKS], i32)
                self.scatter = sb(f"{name}_scatter", [P, CHUNKS], i32)
                self.to_dump = sb(f"{name}_to_dump", [P, CHUNKS])
                self.hi = sb(f"{name}_hi", [P, CHUNKS])
                self.lo = sb(f"{name}_lo", [P, CHUNKS])
                self.rel = sb(f"{name}_rel", [P, TILES * WC])
                self.own = sb(f"{name}_own", [P, TILES * WC], i32)
                self.other = sb(f"{name}_other", [P, TILES * WC], i32)

        S = Ends("src", src, src_row)
        T = Ends("dst", dst, dst_row)
        base = sb("base", [P, CHUNKS])
        part = sb("part", [P, 1])
        tile_id = sb("tile_id", [P, CHUNKS])
        pairs = sb("pairs", [P, CHUNKS, 2], i32)
        first_edge = sb("first_edge", [1, 2, P], i32)
        is_fast = sb("is_fast", [1, 1], i32)
        iota_jp = sb("iota_jp", [P, J, P], fp16)
        rcnt = sb("rcnt", [P, HI])
        dinv = sb("dinv", [P, HI])
        dinv2 = sb("dinv2", [P, HI])

        psum = ps("psum", [P, 8, 512])
        counts_out = psum[:, 4:6, :].rearrange("p b n -> p (b n)")
        counts_in = psum[:, 6:8, :].rearrange("p b n -> p (b n)")

        s_const = signal("s_const")
        s_iota = signal("s_iota")
        s_rows = signal("s_rows")
        s_wts = signal("s_wts")
        s_rowf = signal("s_rowf")
        s_pt = signal("s_pt")
        s_dc = signal("s_dc")
        s_passed = signal("s_passed")
        s_bin = signal("s_bin")
        s_binld = [signal(f"s_binld{k}") for k in range(2)]
        s_sort = signal("s_sort")
        s_bpe = signal("s_bpe")
        s_tcnt = signal("s_tcnt")
        s_kept = signal("s_kept")
        s_onehot = signal("s_onehot")
        s_cnt = signal("s_cnt")
        s_deg = signal("s_deg")
        s_root = signal("s_root")
        s_eqt = signal("s_eqt")
        s_rank = signal("s_rank")
        s_base = signal("s_base")
        s_pos = signal("s_pos")
        s_place = [signal(f"s_place{s}") for s in range(R)]
        s_win = [signal(f"s_win{k}") for k in range(2)]
        s_trow = [signal(f"s_trow{s}") for s in range(R)]
        s_tr = signal("s_tr")
        s_trc = signal("s_trc")
        s_m1 = signal("s_m1")
        s_lin = signal("s_lin")
        s_leaky = signal("s_leaky")
        s_ex = signal("s_ex")
        s_in = [signal(f"s_in{s}") for s in range(NR)]
        s_out = [signal(f"s_out{s}") for s in range(NR)]
        s_pre = signal("s_pre")
        s_u = signal("s_u")
        s_v = signal("s_v")
        s_x = signal("s_x")
        s_sum = signal("s_sum")
        s_mean = signal("s_mean")
        s_cen = signal("s_cen")
        s_sqr = signal("s_sqr")
        s_ssq = signal("s_ssq")
        s_std = signal("s_std")
        s_rstd = signal("s_rstd")
        s_hn = signal("s_hn")
        s_ready = signal("s_ready")
        s_t3 = signal("s_t3")
        s_t3b = signal("s_t3b")

        def passed(pool, n):
            if not isinstance(n, int):
                pool.sem_inc(s_passed.sem, 1)

        def zero_table(eng, tab, done):
            rows, n, at, step, width = ROWS, 0, 0, 56, D
            while rows - at >= P:
                k = min(step, (rows - at) // P)
                eng.dma_start(tab[at:at + P * k, :].rearrange("(p r) d -> p (r d)", p=P),
                              zeros[:, 0:k * width]).then_inc(done.sem, 16)
                at += P * k
                n += 1
            if rows > at:
                eng.dma_start(tab[at:rows, :], zeros[0:rows - at, 0:width]).then_inc(done.sem, 16)
                n += 1
            return n

        def bc(ap):
            return ap.unsqueeze(2).to_broadcast([P, ap.shape[1], D])

        def rows3(t, w=D):
            return t[:, :].rearrange("p (j d) -> p j d", d=w)

        with Memory(nc, "prep") as m, nc.Block() as block:
            bits = m.ring("bits", 4, [P, CHUNKS], i32)
            for e, name in ((S, "src"), (T, "dst")):
                e.rows_i = m.tile(f"{name}_rows_i", [GROUPS, CH, LANES], i32)
                e.rows_f = m.tile(f"{name}_rows_f", [GROUPS, CH, LANES])

            @block.gpsimd
            def _(pool):
                pool.iota(S.rows_i[:, :, :], [[0, CH], [1, LANES]], base=N - (GROUPS - 2) * LANES,
                          channel_multiplier=LANES).then_inc(s_iota.sem, 1)
                pool.iota(T.rows_i[:, :, :], [[0, CH], [1, LANES]], base=N - (GROUPS - 2) * LANES,
                          channel_multiplier=LANES).then_inc(s_iota.sem, 1)
                pool.memset(ident[:, :], 0.0).then_inc(s_const.sem, 1)
                pool.memset(bg_pad[:, :], 0.0).then_inc(s_const.sem, 1)
                pool.memset(w3_sb[:, :], 0.0).then_inc(s_const.sem, 1)
                pool.memset(earlier[:, :, :], 1.0).then_inc(s_const.sem, 1)
                pool.memset(zeros[:, :], 0.0).then_inc(s_const.sem, 1)
                pool.iota(iota_jp[:, :, :], [[1, J], [J, P]], base=0, channel_multiplier=0,
                          allow_small_or_imprecise_dtypes=True).then_inc(s_const.sem, 1)
                pool.memset(eps[:, :], EPS).then_inc(s_const.sem, 1)
                pool.iota(iota_hi[:, :], [[1, HI]], base=0, channel_multiplier=0,
                          allow_small_or_imprecise_dtypes=True).then_inc(s_const.sem, 1)
                pool.iota(iota_lo[:, :], [[1, P]], base=0, channel_multiplier=0,
                          allow_small_or_imprecise_dtypes=True).then_inc(s_const.sem, 1)
                pool.iota(dump[:, :], [[LANES, CH]], base=SPARE, channel_multiplier=1,
                          allow_small_or_imprecise_dtypes=True).then_inc(s_const.sem, 1)
                pool.wait_ge(s_const.sem, s_const.at(10))
                pool.affine_select(out=ident[:, :], in_=ident[:, :], compare_op=ALU.not_equal, fill=1.0,
                                   base=0, pattern=[[-1, P]], channel_multiplier=1).then_inc(s_const.sem, 1)
                for i in range(CH):
                    pool.affine_select(out=earlier[:, i, :], in_=earlier[:, i, :], compare_op=ALU.is_gt, fill=0.0,
                                       base=LANES * i, pattern=[[-1, GROUP]],
                                       channel_multiplier=1).then_inc(s_const.sem, 1)

            tile_rows_i = m.ring("tile_rows_i", 2, [GROUPS, CH, LANES], i32)
            tile_rows_f = m.ring("tile_rows_f", 2, [GROUPS, CH, LANES], fp16)
            dst_pair_rows = m.tile("dst_pair_rows", [GROUPS, CH, LANES, 2], i32)
            tid_i = m.tile("tid_i", [P, CHUNKS], i32)

            @block.sync
            def _(sp):
                sp.wait_ge(s_iota.sem, s_iota.at(2))
                for e in (S, T):
                    whole = FULL // GROUPS
                    sp.dma_start(e.rows_i[:, 0:whole, :], e.dram[0:whole * GROUPS * LANES].rearrange(
                        "(t c m) -> c t m", c=GROUPS, m=LANES)).then_inc(s_rows.sem, 16)
                    more = FULL - whole * GROUPS
                    sp.dma_start(e.rows_i[0:more, whole, :], e.dram[whole * GROUPS * LANES:FULL * LANES].rearrange(
                        "(c m) -> c m", m=LANES)).then_inc(s_rows.sem, 16)
                    sp.dma_start(e.rows_i[more:more + 1, whole, 0:REST], e.dram[FULL * LANES:E].rearrange(
                        "(c m) -> c m", c=1)).then_inc(s_rows.sem, 16)
                sp.wait_ge(s_const.sem, s_const.at(10))
                sp.dma_start(w1_sb[:, :], W1).then_inc(s_wts.sem, 16)
                sp.dma_start(b1_sb[:, :], b1.rearrange("(p o) -> p o", o=1)).then_inc(s_wts.sem, 16)
                sp.dma_start(w2_sb[0:D, 0:D], W2).then_inc(s_wts.sem, 16)
                sp.dma_start(w2_sb[D:A, 0:D], b2.rearrange("(o n) -> o n", o=1)).then_inc(s_wts.sem, 16)
                sp.dma_start(wg_sb[:, :], Wg).then_inc(s_wts.sem, 16)
                sp.dma_start(bg_pad[D:A, :], bg.rearrange("(o n) -> o n", o=1)).then_inc(s_wts.sem, 16)
                for k in range(2):
                    sp.dma_start(w3_in[k * D:(k + 1) * D, :], W3).then_inc(s_wts.sem, 16)
                    sp.dma_start(w3_sb[k * D:(k + 1) * D, k * (D + 2):k * (D + 2) + D], W3).then_inc(s_wts.sem, 16)
                for k in range(2):
                    sp.dma_start(a3_sb[:, k:k + 1], a3[(1 - k) * D:(2 - k) * D].rearrange(
                        "(p o) -> p o", o=1)).then_inc(s_wts.sem, 16)
                sp.wait_ge(s_dc.sem, s_dc.at(2))
                for e in (S, T):
                    sp.dma_start(e.row.rearrange("(t c m) -> c t m", c=GROUPS, m=LANES),
                                 e.rows_f[:, :, :]).then_inc(s_rowf.sem, 16)
                sp.wait_ge(s_bin.sem, s_bin.at(2))
                for k in range(2):
                    sp.dma_start(tile_rows[k].rearrange("(t c m) -> c t m", c=GROUPS, m=LANES),
                                 tile_rows_f[k][:, :, :]).then_inc(s_rowf.sem, 16)
                sp.dma_start(dst_pairs.rearrange("(t c m) w -> c t (m w)", c=GROUPS, m=LANES),
                             dst_pair_rows[:, :, :, :].rearrange("c t m w -> c t (m w)")).then_inc(s_rowf.sem, 16)
                sp.dma_start(x_end.rearrange("(p j) d -> p (j d)", j=J), zeros[:, 0:J * D]).then_inc(s_rowf.sem, 16)
                sp.wait_ge(s_rowf.sem, s_rowf.at(96))
                sp.dma_start(x_end[0:N - (TILES - 1) * TILE, :], x[(TILES - 1) * TILE:N, :]).then_inc(s_rowf.sem, 16)
                sp.wait_ge(s_rowf.sem, s_rowf.at(112))

            @block.tensor
            def _(pe):
                pe.wait_ge(s_const.sem, s_const.at(11))
                pe.wait_ge(s_dc.sem, s_dc.at(2))
                for n, e in enumerate((S, T)):
                    for t in range(CH):
                        last = pe.transpose(psum[:, n, t * GROUPS:(t + 1) * GROUPS], e.rows_f[:, t, :],
                                            ident[0:GROUPS, 0:GROUPS])
                    last.then_inc(s_pt.sem, 1)
                pe.wait_ge(s_wts.sem, s_wts.at(16 * 12))
                pe.transpose(psum[0:D, 2, 0:A], w2_sb[:, 0:D], ident[0:A, 0:A]).then_inc(s_pt.sem, 1)
                pe.transpose(psum[0:D, 3, 0:P], w3_in[:, :], ident[:, :]).then_inc(s_pt.sem, 1)
                pe.wait_ge(s_trc.sem, s_trc.at(2))
                pe.matmul(psum[0:A, 4, 0:D], w2T[:, :], wg_sb[:, :], start=True, stop=True).then_inc(s_pt.sem, 1)
                pe.matmul(psum[:, 5, 0:2], w3T[:, :], a3_sb[:, :], start=True, stop=True).then_inc(s_pt.sem, 1)

            @block.scalar
            def _(act):
                act.wait_ge(s_pt.sem, s_pt.at(3))
                act.copy(w2T[:, :], psum[0:D, 2, 0:A]).then_inc(s_trc.sem, 1)
                act.wait_ge(s_pt.sem, s_pt.at(4))
                act.copy(w3T[:, :], psum[0:D, 3, 0:P]).then_inc(s_trc.sem, 1)
                act.wait_ge(s_pt.sem, s_pt.at(6))
                for k in range(2):
                    o = k * (D + 2) + D
                    act.copy(w3_sb[k * D:(k + 1) * D, o:o + 2], psum[k * D:(k + 1) * D, 5, 0:2])

            @block.vector
            def _(dve):
                dve.wait_ge(s_rows.sem, s_rows.at(16 * 6))
                for e in (S, T):
                    dve.tensor_copy(e.rows_f[:, :, :], e.rows_i[:, :, :]).then_inc(s_dc.sem, 1)
                n = 2
                dve.wait_ge(s_const.sem, s_const.at(15))
                for k, e in enumerate((S, T)):
                    dve.wait_ge(s_pt.sem, s_pt.at(k + 1))
                    dve.tensor_copy(e.col[:, :], psum[:, k, 0:CHUNKS])
                    dve.tensor_copy(e.gather[:, :], psum[:, k, 0:CHUNKS]).then_inc(s_dc.sem, 1)
                    n += 1
                    dve.wait_ge(s_dc.sem, s_dc.at(n))
                    dve.tensor_scalar(bits[0][:, :], e.gather[:, :], 10, 3, ALU.logical_shift_right,
                                      ALU.logical_shift_left)
                    dve.tensor_scalar(bits[1][:, :], e.gather[:, :], 7, None, ALU.bitwise_and)
                    dve.tensor_scalar(bits[2][:, :], e.gather[:, :], 3, P - 1, ALU.logical_shift_right,
                                      ALU.bitwise_and)
                    dve.tensor_tensor(e.to_dump[:, :].rearrange("p (g c) -> p g c", c=CH),
                                      dump[:, :].unsqueeze(1).to_broadcast([P, GROUPS, CH]),
                                      e.col[:, :].rearrange("p (g c) -> p g c", c=CH),
                                      ALU.subtract).then_inc(s_dc.sem, 1)
                    n += 1
                    dve.wait_ge(s_dc.sem, s_dc.at(n))
                    dve.tensor_tensor(bits[3][:, :], bits[0][:, :], bits[1][:, :], ALU.bitwise_or)
                    dve.tensor_copy(e.lo[:, :], bits[2][:, :]).then_inc(s_dc.sem, 1)
                    n += 1
                    dve.wait_ge(s_dc.sem, s_dc.at(n))
                    dve.tensor_copy(e.hi[:, :], bits[3][:, :]).then_inc(s_dc.sem, 1)
                    n += 1
                    dve.wait_ge(s_dc.sem, s_dc.at(n))
                for k, e in enumerate((S, T)):
                    dve.tensor_scalar(tile_rows_i[k][:, :, :], e.rows_i[:, :, :], 10, None, ALU.logical_shift_right)
                dve.tensor_scalar(tid_i[:, :], S.gather[:, :], 10, None, ALU.logical_shift_right)
                dve.tensor_copy(pairs[:, :, 0:1], S.gather[:, :].unsqueeze(2))
                dve.tensor_copy(pairs[:, :, 1:2], T.gather[:, :].unsqueeze(2))
                dve.tensor_copy(dst_pair_rows[:, :, :, 0], T.rows_i[:, :, :])
                dve.tensor_copy(dst_pair_rows[:, :, :, 1], S.rows_i[:, :, :]).then_inc(s_bin.sem, 1)
                dve.wait_ge(s_bin.sem, s_bin.at(1))
                dve.tensor_copy(tile_id[:, :], tid_i[:, :])
                for k in range(2):
                    last = dve.tensor_copy(tile_rows_f[k][:, :, :], tile_rows_i[k][:, :, :])
                last.then_inc(s_bin.sem, 1)
                dve.wait_ge(s_pt.sem, s_pt.at(5))
                dve.tensor_tensor(w2_sb[:, D:2 * D], psum[0:A, 4, 0:D], bg_pad[:, :], ALU.add)
        s_pt.end(6)
        s_trc.end(2)
        s_bin.end(2)
        s_const.end(15)
        s_dc.end(10)

        counts_m = Memory(nc, "counts")
        with counts_m as m:
            edge_b = m.ring("edge_b", 2, [P, BINC * LANES], fp16)
            is_tile = m.ring("is_tile", 2, [P, BINC, LANES], bf16)
            cnt_step = m.ring("cnt_step", 2, [P, BINC])
            is_less = m.ring("is_less", 2, [P, BINC * LANES], bf16)
            less = m.tile("less", [P, 2, BINS])
            less_step = m.ring("less_step", 2, [P, 2])
            cnt = m.tile("cnt", [P, CHUNKS])
            scan = m.ring("scan", 2, [P, CHUNKS])
            bound = m.tile("bound", [P, 2])
            before = m.tile("before", [P, P])
            totals = m.tile("totals", [P, 4])
            starts = m.tile("starts", [P, 2])
            clamped = m.tile("clamped", [P, 2])
            over = m.tile("over", [P, 4])
            worst = m.tile("worst", [P, 1])
            worst1 = m.tile("worst1", [1, 1])
            flag = m.tile("flag", [1, 1])
            edges_now = m.tile("edges_now", [GROUPS, GROUP])
            edges_next = m.tile("edges_next", [GROUPS, GROUP])
            rise = m.tile("rise", [GROUPS, GROUP])

            with nc.Block() as block:
                @block.gpsimd
                def _(pool):
                    pool.iota(part[:, :], [[0, 1]], base=0, channel_multiplier=1,
                              allow_small_or_imprecise_dtypes=True).then_inc(s_const.sem, 1)
                    pool.iota(bound[:, :], [[1, 2]], base=0, channel_multiplier=1,
                              allow_small_or_imprecise_dtypes=True).then_inc(s_const.sem, 1)
                    pool.memset(before[:, :], 1.0).then_inc(s_const.sem, 1)
                    pool.memset(over[:, :], 0.0).then_inc(s_const.sem, 1)
                    pool.memset(edges_next[:, :], 1e9).then_inc(s_const.sem, 1)
                    pool.wait_ge(s_const.sem, s_const.at(5))
                    pool.affine_select(out=before[:, :], in_=before[:, :], compare_op=ALU.is_gt, fill=0.0,
                                       base=0, pattern=[[1, P]], channel_multiplier=-1).then_inc(s_const.sem, 1)

                @block.sync
                def _(sp):
                    sp.dma_start(edges_now[:, :], dst_row.rearrange("(p m) -> p m", m=GROUP)).then_inc(s_sort.sem, 16)
                    sp.wait_ge(s_const.sem, s_const.at(5))
                    sp.dma_start(edges_next[0:GROUPS - 1, :], dst_row[1:1 + (GROUPS - 1) * GROUP].rearrange(
                        "(p m) -> p m", m=GROUP)).then_inc(s_sort.sem, 16)
                    sp.dma_start(edges_next[GROUPS - 1:GROUPS, 0:GROUP - 1], dst_row[1 + (GROUPS - 1) * GROUP:EDGES]
                                 .rearrange("(p m) -> p m", p=1)).then_inc(s_sort.sem, 16)

                    def step(b, s, turn, row, before_this):
                        if not (before_this == 0 and not not_first(turn)):
                            sp.wait_ge(s_tcnt.sem, s_tcnt.at(before_this + b - 1))
                        sp.dma_start(edge_b[s][:, :], row.rearrange("(g e) -> g e", e=BINC * LANES)[
                            bass.ds(b, 1), :].to_broadcast([P, BINC * LANES])).then_inc(s_binld[s].sem, 16)
                    ring_cycle(sp, BINS, 2, lambda b, s, turn: step(b, s, turn, tile_rows[0], 0))
                    ring_cycle(sp, BINS, 2, lambda b, s, turn: step(b, s, turn, tile_rows[1], BINS))

                @block.vector
                def _(dve):
                    dve.wait_ge(s_const.sem, s_const.at(6))

                    def count_src(b, s, turn):
                        dve.wait_ge(s_binld[s].sem, s_binld[s].at(16 * (turn + 1)))
                        dve.tensor_scalar(is_tile[s][:, :, :].rearrange("p c e -> p (c e)"), edge_b[s][:, :],
                                          part[:, :], None, ALU.is_equal).then_inc(s_tcnt.sem, 1)
                        dve.wait_ge(s_tcnt.sem, s_tcnt.at(b + 1))
                        dve.tensor_reduce(cnt_step[s][:, :], is_tile[s][:, :, :], AX_X, ALU.add).then_inc(s_bin.sem, 1)
                        dve.wait_ge(s_bin.sem, s_bin.at(b + 1))
                        dve.tensor_scalar(cnt[:, bass.ds(b * BINC, BINC)], cnt_step[s][:, :], 0.0, None,
                                          ALU.add).then_inc(s_kept.sem, 1)

                    def count_dst(b, s, turn):
                        dve.wait_ge(s_binld[s].sem, s_binld[s].at(16 * (turn + 1) + 16 * (BINS // 2)))
                        if not (isinstance(b, int) and b < 1):
                            dve.wait_ge(s_tcnt.sem, s_tcnt.at(BINS + b))
                        for k in range(2):
                            last = dve.tensor_scalar(is_less[k][:, :], edge_b[s][:, :], bound[:, k:k + 1], 0.0,
                                                     ALU.is_lt, ALU.add, accum_out=less_step[s][:, k:k + 1])
                        last.then_inc(s_tcnt.sem, 1)
                        dve.wait_ge(s_tcnt.sem, s_tcnt.at(BINS + b + 1))
                        dve.tensor_scalar(less[:, :, bass.ds(b, 1)], less_step[s][:, :].unsqueeze(2), 0.0, None,
                                          ALU.add).then_inc(s_kept.sem, 1)
                    ring_cycle(dve, BINS, 2, count_src)
                    ring_cycle(dve, BINS, 2, count_dst)

                    n = BINS
                    dve.wait_ge(s_sort.sem, s_sort.at(48))
                    dve.wait_ge(s_kept.sem, s_kept.at(2 * BINS))
                    dve.tensor_tensor(rise[:, :], edges_now[:, :], edges_next[:, :], ALU.subtract)
                    dve.tensor_scalar(scan[0][:, :], cnt[:, :], 0.0, None, ALU.add)
                    dve.tensor_reduce(totals[:, 0:1], cnt[:, :], AX_X, ALU.add)
                    dve.tensor_reduce(totals[:, 1:3].unsqueeze(2), less[:, :, :], AX_X, ALU.add).then_inc(s_bin.sem, 1)
                    n += 1
                    dve.wait_ge(s_bin.sem, s_bin.at(n))
                    dve.tensor_reduce(over[0:GROUPS, 2:3], rise[:, :], AX_X, ALU.max)
                    cur, d = 0, 1
                    while d < CHUNKS:
                        a, b = scan[cur], scan[1 - cur]
                        dve.tensor_scalar(b[:, 0:d], a[:, 0:d], 0.0, None, ALU.add)
                        dve.tensor_tensor(b[:, d:CHUNKS], a[:, d:CHUNKS], a[:, 0:CHUNKS - d],
                                          ALU.add).then_inc(s_bin.sem, 1)
                        n += 1
                        dve.wait_ge(s_bin.sem, s_bin.at(n))
                        cur, d = 1 - cur, 2 * d
                    dve.tensor_tensor(scan[1 - cur][:, :], scan[cur][:, :], cnt[:, :], ALU.subtract)
                    dve.tensor_scalar(over[:, 0:1], totals[:, 0:1], -float(WIN), None, ALU.add)
                    dve.scalar_tensor_tensor(over[:, 1:2], totals[:, 2:3], -float(WIN), totals[:, 1:2],
                                             ALU.add, ALU.subtract)
                    dve.wait_ge(s_bpe.sem, s_bpe.at(1))
                    dve.tensor_copy(starts[:, 0:1], psum[:, 0, 0:1])
                    dve.tensor_copy(starts[:, 1:2], totals[:, 1:2]).then_inc(s_bin.sem, 1)
                    n += 1
                    dve.wait_ge(s_bin.sem, s_bin.at(n))
                    dve.tensor_scalar(base[:, :], scan[1 - cur][:, :], starts[:, 0:1], None, ALU.add)
                    dve.tensor_scalar(clamped[:, :], starts[:, :], float(EDGES - WIN), None, ALU.min)
                    dve.tensor_reduce(worst[:, :], over[:, :], AX_X, ALU.max).then_inc(s_bin.sem, 1)
                    n += 1
                    dve.wait_ge(s_bpe.sem, s_bpe.at(2))
                    for k in range(2):
                        dve.tensor_copy(first_edge[0:1, k, :], psum[0:1, 1, k * P:(k + 1) * P])
                    dve.tensor_reduce(worst1[:, :], psum[0:1, 1, 2 * P:3 * P], AX_X, ALU.max).then_inc(s_bin.sem, 1)
                    n += 1
                    dve.wait_ge(s_bin.sem, s_bin.at(n))
                    dve.tensor_scalar(flag[:, :], worst1[:, :], 0.0, None, ALU.is_le).then_inc(s_bin.sem, 1)
                    n += 1
                    dve.wait_ge(s_bin.sem, s_bin.at(n))
                    dve.tensor_copy(is_fast[:, :], flag[:, :])
                    count_steps = n
                    s_bin.steps = n

                @block.tensor
                def _(pe):
                    pe.wait_ge(s_const.sem, s_const.at(6))
                    pe.wait_ge(s_bin.sem, s_bin.at(BINS + 1))
                    pe.matmul(psum[:, 0, 0:1], before[:, :], totals[:, 0:1], start=True, stop=True).then_inc(s_bpe.sem, 1)
                    steps = (CHUNKS - 1).bit_length()
                    pe.wait_ge(s_bin.sem, s_bin.at(BINS + 1 + steps + 2))
                    for k in range(2):
                        pe.matmul(psum[0:1, 1, k * P:(k + 1) * P], clamped[:, k:k + 1], ident[:, :], start=True, stop=True)
                    pe.matmul(psum[0:1, 1, 2 * P:3 * P], worst[:, :], ident[:, :], start=True,
                              stop=True).then_inc(s_bpe.sem, 1)
        s_const.end(6)
        s_sort.end(48)
        for k in range(2):
            s_binld[k].end(16 * BINS)
        s_tcnt.end(2 * BINS)
        s_kept.end(2 * BINS)
        s_bin.end(s_bin.steps)
        s_bpe.end(2)

        with Memory(nc, "place") as m:
            hot_hi = m.ring("hot_hi", CH, [P, HI], fp16)
            hot_lo = m.ring("hot_lo", CH, [P, P], fp16)
            deg1, some, rdeg, root, rroot = (m.tile(n, [P, HI]) for n in ("deg1", "some", "rdeg", "root", "rroot"))
            tile_b = m.ring("tile_b", R, [P, GROUP], fp16)
            is_mine = m.ring("is_mine", R, [P, GROUP])
            junk = m.ring("junk", 2, [P, CH, LANES])
            rank = m.ring("rank", R, [P, CH])
            base_now = m.ring("base_now", R, [P, CH])
            place = m.ring("place", R, [P, CH], i32)
            pair = m.ring("pair", R, [P, CH, 2], i32)
            windows = m.ring("windows", 2, [P, TILES * WC, 2], i32)
            own = m.ring("own", 2, [P, TILES * WC])
            tile_start = m.tile("tile_start", [P, TILES * WC])

            with nc.Block() as block:
                @block.sync
                def _(sp):
                    def step(g, s, turn):
                        if not_first(turn):
                            sp.wait_ge(s_rank.sem, s_rank.at(g - R + 1))
                        sp.dma_start(tile_b[s][:, :], tile_rows[0].rearrange("(g e) -> g e", e=GROUP)[
                            bass.ds(g, 1), :].to_broadcast([P, GROUP])).then_inc(s_trow[s].sem, 16)
                    ring_cycle(sp, GROUPS, R, step)

                @block.vector
                def _(dve):
                    def degree_rows(g):
                        for i in range(CH):
                            if not_zero(g):
                                dve.wait_ge(s_cnt.sem, s_cnt.at(CH * (g - 1) + i + 1))
                            dve.tensor_scalar(hot_lo[i][:, :], iota_lo[:, :], T.lo[:, bass.ds(g * CH + i, 1)], None,
                                              ALU.is_equal)
                            dve.tensor_scalar(hot_hi[i][:, :], iota_hi[:, :], T.hi[:, bass.ds(g * CH + i, 1)], None,
                                              ALU.is_equal).then_inc(s_onehot.sem, 1)

                    def step(g, s, turn):
                        degree_rows(g)
                        dve.wait_ge(s_trow[s].sem, s_trow[s].at(16 * (turn + 1)))
                        if not_first(turn):
                            dve.wait_ge(s_base.sem, s_base.at(g - R + 1))
                        dve.tensor_scalar(base_now[s][:, :], base[:, bass.ds(g * CH, CH)], 0.0, None, ALU.add)
                        dve.tensor_scalar(is_mine[s][:, :], tile_b[s][:, :], part[:, :], None,
                                          ALU.is_equal).then_inc(s_eqt.sem, 1)
                        for i in range(CH):
                            last = dve.scalar_tensor_tensor(junk[s % 2][:, i, :], tile_b[s][:, i * LANES:(i + 1) * LANES],
                                                            tile_id[:, bass.ds(g * CH + i, 1)], earlier[:, 0, 0:LANES],
                                                            ALU.is_equal, ALU.mult, accum_out=rank[s][:, i:i + 1])
                        last.then_inc(s_rank.sem, 1)
                        dve.wait_ge(s_rank.sem, s_rank.at(g + 1))
                        if not_first(turn):
                            dve.wait_ge(s_place[s].sem, s_place[s].at(16 * CH * turn))
                        dve.tensor_scalar(pair[s][:, :, :], pairs[:, bass.ds(g * CH, CH), :], 0.0, None, ALU.add)
                        dve.wait_ge(s_base.sem, s_base.at(g + 1))
                        dve.tensor_tensor(place[s][:, :], psum[:, s, 0:CH], rank[s][:, :], ALU.add).then_inc(s_pos.sem, 1)
                    ring_cycle(dve, GROUPS, R, step)
                    dve.wait_ge(s_cnt.sem, s_cnt.at(CH * GROUPS))
                    dve.tensor_scalar(some[:, :], counts_in[:, 0:HI], 1.0, None, ALU.min)
                    dve.tensor_scalar(deg1[:, :], counts_in[:, 0:HI], 1.0, None, ALU.max).then_inc(s_deg.sem, 1)
                    dve.wait_ge(s_deg.sem, s_deg.at(1))
                    dve.reciprocal(rdeg[:, :], deg1[:, :])
                    dve.wait_ge(s_root.sem, s_root.at(1))
                    dve.reciprocal(rroot[:, :], root[:, :]).then_inc(s_deg.sem, 1)
                    dve.wait_ge(s_deg.sem, s_deg.at(2))
                    dve.tensor_tensor(dinv[:, :], rroot[:, :], some[:, :], ALU.mult)
                    dve.tensor_tensor(dinv2[:, :], rdeg[:, :], some[:, :], ALU.mult)

                @block.tensor
                def _(pe):
                    def step(g, s, turn):
                        for i in range(CH):
                            pe.wait_ge(s_onehot.sem, s_onehot.at(CH * g + i + 1))
                            first = not not_zero(g) and i == 0
                            end = isinstance(g, int) and g == GROUPS - 1 and i == CH - 1
                            pe.matmul(counts_in[:, 0:512], hot_lo[i][:, :], hot_hi[i][:, 0:512], start=first,
                                      stop=end)
                            pe.matmul(counts_in[:, 512:HI], hot_lo[i][:, :], hot_hi[i][:, 512:HI], start=first,
                                      stop=end).then_inc(s_cnt.sem, 1)
                        pe.wait_ge(s_eqt.sem, s_eqt.at(g + 1))
                        if not_first(turn):
                            pe.wait_ge(s_pos.sem, s_pos.at(g - R + 1))
                        for i in range(CH):
                            last = pe.matmul(psum[:, s, i:i + 1], is_mine[s][:, i * LANES:(i + 1) * LANES],
                                             base_now[s][:, i:i + 1], start=True, stop=True)
                        last.then_inc(s_base.sem, 1)
                    ring_cycle(pe, GROUPS, R, step)

                @block.gpsimd
                def _(pool):
                    pool.iota(tile_start[:, :], [[TILE, TILES], [0, WC]], base=0, channel_multiplier=0,
                              allow_small_or_imprecise_dtypes=True).then_inc(s_const.sem, 1)

                    def step(g, s, turn):
                        pool.wait_ge(s_pos.sem, s_pos.at(g + 1))
                        passed(pool, g)
                        for i in range(CH):
                            pool.indirect_dma_start(src_pairs, bass.IndirectOffsetOnAxis(ap=place[s][:, i:i + 1], axis=0),
                                                    pair[s][:, i, :], None).then_inc(s_place[s].sem, 16)
                    ring_cycle(pool, GROUPS, R, step)
                    for s in range(R):
                        pool.wait_ge(s_place[s].sem, s_place[s].at(16 * CH * -(-(GROUPS - s) // R)))

                @block.scalar
                def _(act):
                    with act.Fori(0, TILES) as t:
                        at = act.value_load(first_edge[0:1, 1, bass.ds(t, 1)], min_val=0, max_val=EDGES - WIN)
                        act.dma_start(windows[1][:, bass.ds(t * WC, WC), :].rearrange("p c w -> p (c w)"),
                                      dst_pairs[bass.ds(at, WIN), :].rearrange("(p c) w -> p (c w)", c=WC)
                                      ).then_inc(s_win[1].sem, 16)
                    act.wait_ge(s_deg.sem, s_deg.at(1))
                    act.activation(root[:, :], deg1[:, :], ACT.Sqrt).then_inc(s_root.sem, 1)
                    act.wait_ge(s_win[1].sem, s_win[1].at(16 * TILES))
            s_const.end(1)
            for s in range(R):
                s_trow[s].end(16 * -(-(GROUPS - s) // R))
                s_place[s].end(16 * CH * -(-(GROUPS - s) // R))

            with nc.Block() as block:
                @block.sync
                def _(sp):
                    with sp.Fori(0, TILES) as t:
                        at = sp.value_load(first_edge[0:1, 0, bass.ds(t, 1)], min_val=0, max_val=EDGES - WIN)
                        sp.dma_start(windows[0][:, bass.ds(t * WC, WC), :].rearrange("p c w -> p (c w)"),
                                     src_pairs[bass.ds(at, WIN), :].rearrange("(p c) w -> p (c w)", c=WC)
                                     ).then_inc(s_win[0].sem, 16)
                    sp.wait_ge(s_win[0].sem, s_win[0].at(16 * TILES))

                @block.vector
                def _(dve):
                    for n, (e, k) in enumerate(((T, 1), (S, 0))):
                        dve.wait_ge(s_win[k].sem, s_win[k].at(16 * TILES))
                        dve.tensor_copy(e.other[:, :].unsqueeze(2), windows[k][:, :, 1:2])
                        dve.tensor_copy(e.own[:, :].unsqueeze(2), windows[k][:, :, 0:1])
                        dve.tensor_copy(own[k][:, :].unsqueeze(2), windows[k][:, :, 0:1]).then_inc(s_bin.sem, 1)
                        dve.wait_ge(s_bin.sem, s_bin.at(n + 1))
                        dve.tensor_tensor(e.rel[:, :], own[k][:, :], tile_start[:, :], ALU.subtract)
            s_bin.end(2)

        LAG = 2

        def tiles_of(s):
            return -(-(TILES - s) // NR)

        def table_tile(tab, g):
            n = NPAD if tab.shape[0] >= NPAD else (TILES - 1) * TILE
            return tab[0:n, :].rearrange("(g p j) d -> g p (j d)", p=P, j=J)[bass.ds(g, 1)].rearrange(
                "g p n -> p (g n)")

        def tile_loads(sp, loads, used, s_in=s_in):
            def step(g, s, turn):
                if not_first(turn):
                    sp.wait_ge(used.sem, used.at(g - NR + 1))
                for tab, ring in loads:
                    if tab is x and isinstance(g, int) and g == TILES - 1:
                        part = x_end.rearrange("(p j) d -> p (j d)", j=J)
                    else:
                        part = table_tile(tab, g)
                    sp.dma_start(ring[s][:, :], part).then_inc(s_in[s].sem, 16)
            ring_cycle(sp, TILES - 1, NR, step)
            step(TILES - 1, (TILES - 1) % NR, (TILES - 1) // NR)

        def tile_stores(act, stores, g, s, s_out=s_out):
            for tab, ring in stores:
                if tab is out and isinstance(g, int) and g == TILES - 1:
                    act.dma_start(out[(TILES - 1) * TILE:N, :].rearrange("(p j) d -> p (j d)", j=J),
                                  ring[s][0:LAST_P, :]).then_inc(s_out[s].sem, 16)
                else:
                    act.dma_start(table_tile(tab, g), ring[s][:, :]).then_inc(s_out[s].sem, 16)

        def end_tiles(loads, stores, signals, s_in=s_in, s_out=s_out):
            for s in range(NR):
                s_in[s].end(16 * len(loads) * tiles_of(s))
                s_out[s].end(16 * len(stores) * tiles_of(s))
            for sig in signals:
                sig.end(TILES)

        def norm_phase(m, hn, loads, stores, resid, before=None, after=None, pool_first=None,
                       project=None, stored_resid=False):
            cen = m.ring("cen", NR, [P, J * D])
            sqr = m.ring("sqr", NR, [P, J * D])
            rowsum, mean, sumsq, std, rstd = (m.ring(name, NR, [P, J]) for name in (
                "rowsum", "mean", "sumsq", "std", "rstd"))
            if project:
                hT = m.ring("hT", 2, [P, J * D])
                lin, leaky, ex = (m.ring(name, NR, [P, J]) for name in ("lin", "leaky", "ex"))
            ready = s_ready if after or project else s_hn

            with nc.Block() as block:
                @block.sync
                def _(sp):
                    tile_loads(sp, loads, ready)

                @block.gpsimd
                def _(pool):
                    def step(g, s, turn):
                        if pool_first:
                            pool.wait_ge(s_in[s].sem, s_in[s].at(16 * len(loads) * (turn + 1)))
                            if not_first(turn):
                                pool.wait_ge(s_x.sem, s_x.at(g - NR + 1))
                            pool_first(pool, g, s)
                        pool.wait_ge(s_mean.sem, s_mean.at(g + 1))
                        if not_first(turn):
                            pool.wait_ge(s_hn.sem, s_hn.at(g - NR + 1))
                        pool.tensor_tensor(rows3(cen[s]), rows3(resid[s]), bc(mean[s][:, :]),
                                           ALU.add).then_inc(s_cen.sem, 1)
                    ring_cycle(pool, TILES, NR, step)

                @block.vector
                def _(dve):
                    def part_a(g, s, turn):
                        dve.wait_ge(s_in[s].sem, s_in[s].at(16 * len(loads) * (turn + 1)))
                        if stored_resid and not_first(turn):
                            dve.wait_ge(s_out[s].sem, s_out[s].at(16 * len(stores) * turn))
                        if before:
                            before(dve, g, s)
                            dve.wait_ge(s_x.sem, s_x.at(g + 1))
                        dve.tensor_reduce(rowsum[s][:, :], rows3(resid[s]), AX_X, ALU.add).then_inc(s_sum.sem, 1)
                        dve.wait_ge(s_sum.sem, s_sum.at(g + 1))
                        dve.tensor_scalar(mean[s][:, :], rowsum[s][:, :], -1.0 / D, None,
                                          ALU.mult).then_inc(s_mean.sem, 1)

                    def squares_sum(g, s, turn):
                        dve.wait_ge(s_sqr.sem, s_sqr.at(g + 1))
                        dve.tensor_reduce(sumsq[s][:, :], rows3(sqr[s]), AX_X, ALU.add).then_inc(s_ssq.sem, 1)

                    def part_b(g, s, turn):
                        dve.wait_ge(s_std.sem, s_std.at(g + 1))
                        dve.reciprocal(rstd[s][:, :], std[s][:, :]).then_inc(s_rstd.sem, 1)
                        dve.wait_ge(s_rstd.sem, s_rstd.at(g + 1))
                        if not_first(turn):
                            dve.wait_ge(s_out[s].sem, s_out[s].at(16 * len(stores) * turn))
                        dve.scalar_tensor_tensor(rows3(hn[s]), rows3(cen[s]), 0.0, bc(rstd[s][:, :]),
                                                 ALU.max, ALU.mult).then_inc(s_hn.sem, 1)
                        if after:
                            dve.wait_ge(s_hn.sem, s_hn.at(g + 1))
                            after(dve, g, s)

                    def part_c(g, s, turn):
                        hw, as_, _ = project
                        if not_first(turn):
                            dve.wait_ge(s_out[s].sem, s_out[s].at(16 * len(stores) * turn))
                        dve.wait_ge(s_m1.sem, s_m1.at(g + 1))
                        half = psum[:, 4 * (s % 2) + 2, 0:4 * (D + 2)].rearrange("p (r w) -> p r w", w=D + 2)
                        dve.tensor_copy(rows3(hw[s], A)[:, 4:8, :], half[:, :, 0:A])
                        dve.tensor_copy(as_[s][:, 4:8].unsqueeze(2), half[:, :, A:A + 1]).then_inc(s_t3b.sem, 1)
                        dve.wait_ge(s_t3b.sem, s_t3b.at(g + 1))
                        dve.wait_ge(s_t3.sem, s_t3.at(g + 1))
                        dve.tensor_tensor(lin[s][:, :].unsqueeze(2), rows3(hw[s], A)[:, :, D:A],
                                          as_[s][:, :].unsqueeze(2), ALU.add).then_inc(s_lin.sem, 1)
                        dve.wait_ge(s_lin.sem, s_lin.at(g + 1))
                        dve.scalar_tensor_tensor(leaky[s][:, :], lin[s][:, :], SLOPE, lin[s][:, :],
                                                 ALU.mult, ALU.max).then_inc(s_leaky.sem, 1)

                    def part_d(g, s, turn):
                        hw, _, att = project
                        dve.wait_ge(s_ex.sem, s_ex.at(g + 1))
                        dve.tensor_tensor(rows3(att[s], A)[:, :, 0:D], rows3(hw[s], A)[:, :, 0:D], bc(ex[s][:, :]),
                                          ALU.mult)
                        dve.tensor_copy(rows3(att[s], A)[:, :, D:A],
                                        ex[s][:, :].unsqueeze(2)).then_inc(s_ready.sem, 1)

                    def behind(part, g, s, turn, n):
                        if not isinstance(turn, int) or g >= n:
                            part(g - n, (s - n) % NR, turn - (1 if s < n else 0))

                    def both(g, s, turn):
                        ahead = s + LAG
                        if not isinstance(turn, int) or g + LAG < TILES:
                            part_a(g + LAG, ahead % NR, turn + ahead // NR)
                        if not isinstance(turn, int) or g + 1 < TILES:
                            squares_sum(g + 1, (s + 1) % NR, turn)
                        part_b(g, s, turn)
                        if project:
                            behind(part_c, g, s, turn, 2)
                            behind(part_d, g, s, turn, 3)

                    for g in range(LAG):
                        part_a(g, g, 0)
                    squares_sum(0, 0, 0)
                    turns = (TILES - LAG) // NR
                    for g in range(NR):
                        both(g, g, 0)
                    with dve.Fori(1, turns) as turn:
                        for s in range(NR):
                            both(turn * NR + s, s, turn)
                    for g in range(turns * NR, TILES):
                        both(g, g % NR, g // NR)
                    if project:
                        for g in (TILES - 2, TILES - 1):
                            part_c(g, g % NR, g // NR)
                        for g in (TILES - 3, TILES - 2, TILES - 1):
                            part_d(g, g % NR, g // NR)

                @block.tensor
                def _(pe):
                    def transposes(g, s):
                        pe.wait_ge(s_hn.sem, s_hn.at(g + 1))
                        if not (isinstance(g, int) and g < 2):
                            pe.wait_ge(s_trc.sem, s_trc.at(g - 1))
                        for k in range(J // 2):
                            last = pe.transpose(psum[:, 4 * (s % 2), k * P:(k + 1) * P], hn[s][:, k * P:(k + 1) * P],
                                                ident[:, :])
                        last.then_inc(s_tr.sem, 1)

                    def products(g, s):
                        pe.wait_ge(s_trc.sem, s_trc.at(g + 1))
                        if not (isinstance(g, int) and g < 2):
                            pe.wait_ge(s_t3.sem, s_t3.at(g - 1))
                            pe.wait_ge(s_t3b.sem, s_t3b.at(g - 1))
                        for k in range(J // 2):
                            o = (k % 2) * 2 * (D + 2)
                            last = pe.matmul(psum[:, 4 * (s % 2) + 1 + k // 2, o:o + 2 * (D + 2)],
                                             hT[s % 2][:, k * P:(k + 1) * P], w3_sb[:, :], start=True, stop=True)
                        last.then_inc(s_m1.sem, 1)

                    def step(g, s, turn):
                        if not isinstance(turn, int) or g + 1 < TILES:
                            transposes(g + 1, (s + 1) % NR)
                        products(g, s)
                    if project:
                        transposes(0, 0)
                    if project:
                        ring_cycle(pe, TILES, NR, step)

                @block.scalar
                def _(act):
                    def square(g, s, turn):
                        act.wait_ge(s_cen.sem, s_cen.at(g + 1))
                        if not_first(turn):
                            act.wait_ge(s_ssq.sem, s_ssq.at(g - NR + 1))
                        act.activation(sqr[s][:, :], cen[s][:, :], ACT.Square).then_inc(s_sqr.sem, 1)

                    def root(g, s, turn):
                        act.wait_ge(s_ssq.sem, s_ssq.at(g + 1))
                        act.activation(std[s][:, :], sumsq[s][:, :], ACT.Sqrt, bias=eps[:, :],
                                       scale=1.0 / D).then_inc(s_std.sem, 1)

                    def products(g, s, turn):
                        hw, as_, _ = project
                        act.wait_ge(s_tr.sem, s_tr.at(g + 1))
                        if not (isinstance(g, int) and g < 2):
                            act.wait_ge(s_m1.sem, s_m1.at(g - 1))
                        act.copy(hT[s % 2][:, :], psum[:, 4 * (s % 2), :]).then_inc(s_trc.sem, 1)

                    def evacuate(g, s, turn):
                        hw, as_, _ = project
                        if not_first(turn):
                            act.wait_ge(s_out[s].sem, s_out[s].at(16 * len(stores) * turn))
                        act.wait_ge(s_m1.sem, s_m1.at(g + 1))
                        half = psum[:, 4 * (s % 2) + 1, 0:4 * (D + 2)].rearrange("p (r w) -> p r w", w=D + 2)
                        act.copy(rows3(hw[s], A)[:, 0:4, :], half[:, :, 0:A])
                        act.copy(as_[s][:, 0:4].unsqueeze(2), half[:, :, A:A + 1]).then_inc(s_t3.sem, 1)

                    def exps(g, s, turn):
                        act.wait_ge(s_leaky.sem, s_leaky.at(g + 1))
                        act.activation(ex[s][:, :], leaky[s][:, :], ACT.Exp).then_inc(s_ex.sem, 1)

                    def store(g, s, turn):
                        act.wait_ge(ready.sem, ready.at(g + 1))
                        tile_stores(act, stores, g, s)

                    def behind(part, g, s, turn, n):
                        if not isinstance(turn, int) or g >= n:
                            part(g - n, (s - n) % NR, turn - (1 if s < n else 0))

                    def step(g, s, turn):
                        ahead = s + LAG
                        if not isinstance(g, int) or g + LAG < TILES:
                            square(g + LAG, ahead % NR, turn + ahead // NR)
                        if not isinstance(turn, int) or g + 1 < TILES:
                            root(g + 1, (s + 1) % NR, turn)
                        if project:
                            products(g, s, turn)
                            behind(evacuate, g, s, turn, 1)
                            behind(exps, g, s, turn, 2)
                            behind(store, g, s, turn, 3)
                        else:
                            store(g, s, turn)
                    for g in range(LAG):
                        square(g, g, 0)
                    root(0, 0, 0)
                    turns = (TILES - LAG) // NR
                    for g in range(NR):
                        step(g, g, 0)
                    with act.Fori(1, turns) as turn:
                        for s in range(NR):
                            step(turn * NR + s, s, turn)
                    for g in range(turns * NR, TILES):
                        step(g, g % NR, g // NR)
                    if project:
                        evacuate(TILES - 1, (TILES - 1) % NR, (TILES - 1) // NR)
                        for g in (TILES - 2, TILES - 1):
                            exps(g, g % NR, 0)
                        for g in (TILES - 3, TILES - 2, TILES - 1):
                            store(g, g % NR, 0)
                    for s in range(NR):
                        act.wait_ge(s_out[s].sem, s_out[s].at(16 * len(stores) * tiles_of(s)))

            end_tiles(loads, stores, [s_hn, s_sum, s_mean, s_cen, s_sqr, s_ssq, s_std, s_rstd]
                      + [s_ready] * bool(after or project) + [s_x] * bool(before)
                      + [s_pre] * bool(pool_first)
                      + [s_tr, s_trc, s_m1, s_t3, s_t3b, s_lin, s_leaky, s_ex] * bool(project))

        def plain_phase(loads, stores, compute, more=(), s_in=s_in, s_out=s_out, s_ready=s_ready):
            with nc.Block() as block:
                @block.sync
                def _(sp):
                    tile_loads(sp, loads, s_ready, s_in)

                @block.vector
                def _(dve):
                    def step(g, s, turn):
                        dve.wait_ge(s_in[s].sem, s_in[s].at(16 * len(loads) * (turn + 1)))
                        if not_first(turn):
                            dve.wait_ge(s_out[s].sem, s_out[s].at(16 * len(stores) * turn))
                        compute(dve, g, s)
                    ring_cycle(dve, TILES, NR, step)

                @block.scalar
                def _(act):
                    def step(g, s, turn):
                        act.wait_ge(s_ready.sem, s_ready.at(g + 1))
                        tile_stores(act, stores, g, s, s_out)
                    ring_cycle(act, TILES - 1, NR, step)
                    step(TILES - 1, (TILES - 1) % NR, (TILES - 1) // NR)
                    for s in range(NR):
                        act.wait_ge(s_out[s].sem, s_out[s].at(16 * len(stores) * tiles_of(s)))
            end_tiles(loads, stores, [s_ready, *more], s_in, s_out)


        def edges_of(s):
            return -(-(GROUPS - s) // R)

        q = GeneralSignals(signal)

        def edge_phase(name, gathers, by, target, width, make=None, mark=False, count=False):
            NG = len(gathers) * CH
            gwidth = max(c + w for _, _, c, w in gathers)

            with Memory(nc, name) as m:
                g_idx = m.ring("g_idx", R, [P, len(gathers), CH], i32)
                s_idx = m.ring("s_idx", R, [P, CH], i32)
                got = m.ring("got", R, [P, CH, gwidth])
                same = m.ring("same", R, [P, CH, GROUP])
                sums = m.ring("sums", R, [P, CH, width])
                rowb = m.ring("rowb", R, [P, GROUP])
                vals = m.ring("vals", R, [P, CH, width]) if make else got
                if mark:
                    junk = m.tile("junk", [P, CH, GROUP])
                    n_before = m.tile("n_before", [P, CH])
                    shift = m.tile("shift", [P, CH])
                if count:
                    hot_hi = m.ring("hot_hi", 2, [P, HI], fp16)
                    hot_lo = m.ring("hot_lo", 2, [P, P], fp16)
                    deg1, some, out1, rdeg, root, rroot = (m.tile(n, [P, HI]) for n in (
                        "deg1", "some", "out1", "rdeg", "root", "rroot"))
                if make == "mlp":
                    pairT = m.tile("pairT", [P, GROUP])
                    h1T = m.tile("h1T", [A, GROUP])
                    gate = m.tile("gate", [P, CH, D])
                if make == "attend":
                    lin, leaky, ex = (m.tile(n, [P, CH]) for n in ("lin", "leaky", "ex"))
                rows_used = q.vals if make else q.summed
                block = m.stack.enter_context(nc.Block())

                def cols(t, g):
                    return t[:, bass.ds(g * CH, CH)]

                def col(t, g, i):
                    return t[:, bass.ds(g * CH + i, 1)]

                @block.sync
                def _(sp):
                    def step(g, s, turn):
                        if not_first(turn):
                            sp.wait_ge(q.same.sem, q.same.at(g - R + 1))
                            if mark:
                                sp.wait_ge(q.snew.sem, q.snew.at(g - R + 1))
                        sp.dma_start(rowb[s][:, :], by.row.rearrange("(g e) -> g e", e=GROUP)[
                            bass.ds(g, 1), :].to_broadcast([P, GROUP])).then_inc(q.row[s].sem, 16)
                    ring_cycle(sp, GROUPS, R, step)

                @block.gpsimd
                def _(pool):
                    def gather(g, s, turn):
                        pool.wait_ge(q.gidx.sem, q.gidx.at(g + 1))
                        if not_first(turn):
                            pool.wait_ge(rows_used.sem, rows_used.at(g - R + 1))
                            if make == "mlp":
                                pool.wait_ge(q.tr.sem, q.tr.at(g - R + 1))
                        passed(pool, g)
                        for k, (ends, tab, c, w) in enumerate(gathers):
                            for i in range(CH):
                                pool.indirect_dma_start(got[s][:, i, c:c + w], None, tab,
                                                        bass.IndirectOffsetOnAxis(ap=g_idx[s][:, k, i:i + 1], axis=0)
                                                        ).then_inc(q.got[s].sem, 16)

                    def scatter(g, s, turn):
                        pool.wait_ge(q.sidx.sem, q.sidx.at(g + 1))
                        pool.wait_ge(q.sums.sem, q.sums.at(g + 1))
                        if not_zero(g):
                            pool.wait_ge(q.scat.sem, q.scat.at(16 * CH * g))
                        passed(pool, g)
                        for i in range(CH):
                            pool.indirect_dma_start(target, bass.IndirectOffsetOnAxis(ap=s_idx[s][:, i:i + 1], axis=0),
                                                    sums[s][:, i, :], None, compute_op=ALU.add
                                                    ).then_inc(q.scat.sem, 16)

                    def step(g, s, turn):
                        ahead = s + AHEAD
                        if not isinstance(g, int) or g + AHEAD < GROUPS:
                            gather(g + AHEAD, ahead % R, turn + ahead // R)
                        scatter(g, s, turn)
                    for g in range(AHEAD):
                        gather(g, g, 0)
                    turns = (GROUPS - AHEAD) // R
                    for g in range(R):
                        step(g, g, 0)
                    with pool.Fori(1, turns) as turn:
                        for s in range(R):
                            step(turn * R + s, s, turn)
                    for g in range(turns * R, GROUPS):
                        step(g, g % R, g // R)
                    pool.wait_ge(q.scat.sem, q.scat.at(16 * CH * GROUPS))

                @block.vector
                def _(dve):
                    def gather_index(g, s, turn):
                        if not_first(turn):
                            dve.wait_ge(q.got[s].sem, q.got[s].at(16 * NG * turn))
                        for k, (ends, _, _, _) in enumerate(gathers):
                            last = dve.tensor_scalar(g_idx[s][:, k, :], cols(ends.gather, g), 0.0, None, ALU.add)
                        last.then_inc(q.gidx.sem, 1)

                    def equal_ends(g, s, turn):
                        dve.wait_ge(q.row[s].sem, q.row[s].at(16 * (turn + 1)))
                        if not_first(turn):
                            dve.wait_ge(q.summed.sem, q.summed.at(g - R + 1))
                        for i in range(CH):
                            last = dve.tensor_scalar(same[s][:, i, :], rowb[s][:, :], col(by.col, g, i), None,
                                                     ALU.is_equal)
                        last.then_inc(q.same.sem, 1)

                    def scatter_index(g, s, turn):
                        if mark:
                            for i in range(CH):
                                last = dve.scalar_tensor_tensor(junk[:, i, :], rowb[s][:, :], col(by.col, g, i),
                                                                earlier[:, i, :], ALU.is_equal, ALU.mult,
                                                                accum_out=n_before[:, i:i + 1])
                            last.then_inc(q.before.sem, 1)
                            dve.wait_ge(q.before.sem, q.before.at(g + 1))
                            dve.scalar_tensor_tensor(shift[:, :], n_before[:, :], 1.0, cols(by.to_dump, g),
                                                     ALU.min, ALU.mult).then_inc(q.shift.sem, 1)
                            dve.wait_ge(q.shift.sem, q.shift.at(g + 1))
                            dve.tensor_tensor(cols(by.scatter, g), cols(by.col, g), shift[:, :],
                                              ALU.add).then_inc(q.snew.sem, 1)
                            dve.wait_ge(q.snew.sem, q.snew.at(g + 1))
                        if not_first(turn):
                            dve.wait_ge(q.scat.sem, q.scat.at(16 * CH * (g - R + 1)))
                        dve.tensor_scalar(s_idx[s][:, :], cols(by.scatter, g), 0.0, None, ALU.add).then_inc(q.sidx.sem, 1)

                    def one_hots(g):
                        for i in range(CH):
                            for k, ends in enumerate((S, T)):
                                if not_zero(g) or i:
                                    dve.wait_ge(q.cnt.sem, q.cnt.at(2 * CH * g + 2 * i + k - 1))
                                dve.tensor_scalar(hot_lo[k][:, :], iota_lo[:, :], col(ends.lo, g, i), None, ALU.is_equal)
                                dve.tensor_scalar(hot_hi[k][:, :], iota_hi[:, :], col(ends.hi, g, i), None,
                                                  ALU.is_equal).then_inc(q.hot.sem, 1)

                    def values(g, s, turn):
                        if not_first(turn):
                            dve.wait_ge(q.summed.sem, q.summed.at(g - R + 1))
                        if make == "mlp":
                            dve.wait_ge(q.gate.sem, q.gate.at(g + 1))
                            inter = psum[:, 2, :].rearrange("p (c w) -> p c w", c=CH)[:, :, 0:D]
                            dve.tensor_tensor(vals[s][:, :, :], inter, gate[:, :, :], ALU.mult).then_inc(q.vals.sem, 1)
                        if make == "attend":
                            dve.wait_ge(q.got[s].sem, q.got[s].at(16 * NG * (turn + 1)))
                            dve.tensor_tensor(lin[:, :].unsqueeze(2), got[s][:, :, D:A], got[s][:, :, A:A + 1],
                                              ALU.add).then_inc(q.lin.sem, 1)
                            dve.wait_ge(q.lin.sem, q.lin.at(g + 1))
                            dve.scalar_tensor_tensor(leaky[:, :], lin[:, :], SLOPE, lin[:, :],
                                                     ALU.mult, ALU.max).then_inc(q.leaky.sem, 1)
                            dve.wait_ge(q.ex.sem, q.ex.at(g + 1))
                            dve.tensor_tensor(vals[s][:, :, 0:D], got[s][:, :, 0:D],
                                              ex[:, :].unsqueeze(2).to_broadcast([P, CH, D]), ALU.mult)
                            dve.tensor_copy(vals[s][:, :, D:A], ex[:, :].unsqueeze(2)).then_inc(q.vals.sem, 1)

                    def step(g, s, turn):
                        ahead = s + IDX_AHEAD
                        if not isinstance(g, int) or g + IDX_AHEAD < GROUPS:
                            gather_index(g + IDX_AHEAD, ahead % R, turn + ahead // R)
                        equal_ends(g, s, turn)
                        scatter_index(g, s, turn)
                        if count:
                            one_hots(g)
                        if make:
                            values(g, s, turn)
                    if make == "mlp":
                        dve.memset(h1T[D:A, :], 1.0).then_inc(q.ones.sem, 1)
                    for g in range(IDX_AHEAD):
                        gather_index(g, g, 0)
                    turns = (GROUPS - IDX_AHEAD) // R
                    for g in range(R):
                        step(g, g, 0)
                    with dve.Fori(1, turns) as turn:
                        for s in range(R):
                            step(turn * R + s, s, turn)
                    for g in range(turns * R, GROUPS):
                        step(g, g % R, g // R)
                    if count:
                        dve.wait_ge(q.cnt.sem, q.cnt.at(2 * CH * GROUPS))
                        dve.tensor_scalar(out1[:, :], counts_out[:, 0:HI], 1.0, None, ALU.max)
                        dve.tensor_scalar(some[:, :], counts_in[:, 0:HI], 1.0, None, ALU.min)
                        dve.tensor_scalar(deg1[:, :], counts_in[:, 0:HI], 1.0, None, ALU.max).then_inc(q.lin.sem, 1)
                        dve.wait_ge(q.lin.sem, q.lin.at(1))
                        dve.reciprocal(rcnt[:, :], out1[:, :])
                        dve.reciprocal(rdeg[:, :], deg1[:, :])
                        dve.wait_ge(q.ex.sem, q.ex.at(1))
                        dve.reciprocal(rroot[:, :], root[:, :]).then_inc(q.lin.sem, 1)
                        dve.wait_ge(q.lin.sem, q.lin.at(2))
                        dve.tensor_tensor(dinv[:, :], rroot[:, :], some[:, :], ALU.mult)
                        dve.tensor_tensor(dinv2[:, :], rdeg[:, :], some[:, :], ALU.mult)

                @block.tensor
                def _(pe):
                    def mlp(g, s, turn):
                        pe.wait_ge(q.got[s].sem, q.got[s].at(16 * NG * (turn + 1)))
                        if not_zero(g):
                            pe.wait_ge(q.trc.sem, q.trc.at(g))
                        for i in range(CH):
                            last = pe.transpose(psum[:, 0, i * P:(i + 1) * P], got[s][:, i, :], ident[:, :])
                        last.then_inc(q.tr.sem, 1)
                        pe.wait_ge(q.trc.sem, q.trc.at(g + 1))
                        if not_zero(g):
                            pe.wait_ge(q.m1c.sem, q.m1c.at(g))
                        pe.matmul(psum[0:D, 1, :], w1_sb[:, :], pairT[:, :], start=True, stop=True).then_inc(q.m1.sem, 1)
                        pe.wait_ge(q.m1c.sem, q.m1c.at(g + 1))
                        if not not_zero(g):
                            pe.wait_ge(q.ones.sem, q.ones.at(1))
                        if not_zero(g):
                            pe.wait_ge(q.vals.sem, q.vals.at(g))
                        for i in range(CH):
                            last = pe.matmul(psum[:, 2, i * P:(i + 1) * P], h1T[:, i * P:(i + 1) * P], w2_sb[:, :],
                                             start=True, stop=True)
                        last.then_inc(q.m2.sem, 1)

                    def count_chunks(g):
                        for i in range(CH):
                            for k, counts in enumerate((counts_out, counts_in)):
                                pe.wait_ge(q.hot.sem, q.hot.at(2 * CH * g + 2 * i + k + 1))
                                first = not not_zero(g) and i == 0
                                end = isinstance(g, int) and g == GROUPS - 1 and i == CH - 1
                                pe.matmul(counts[:, 0:512], hot_lo[k][:, :], hot_hi[k][:, 0:512], start=first, stop=end)
                                pe.matmul(counts[:, 512:HI], hot_lo[k][:, :], hot_hi[k][:, 512:HI],
                                          start=first, stop=end).then_inc(q.cnt.sem, 1)

                    def step(g, s, turn):
                        if make == "mlp":
                            mlp(g, s, turn)
                        if count:
                            count_chunks(g)
                        if make:
                            pe.wait_ge(q.vals.sem, q.vals.at(g + 1))
                        else:
                            pe.wait_ge(q.got[s].sem, q.got[s].at(16 * NG * (turn + 1)))
                        pe.wait_ge(q.same.sem, q.same.at(g + 1))
                        if not_zero(g):
                            pe.wait_ge(q.sums.sem, q.sums.at(g))
                        for j in range(CH):
                            for i in range(CH):
                                last = pe.matmul(psum[:, 3, j * width:(j + 1) * width],
                                                 same[s][:, i, j * LANES:(j + 1) * LANES], vals[s][:, i, 0:width],
                                                 start=i == 0, stop=i == CH - 1)
                        last.then_inc(q.summed.sem, 1)
                    ring_cycle(pe, GROUPS, R, step)

                @block.scalar
                def _(act):
                    def step(g, s, turn):
                        if make == "mlp":
                            act.wait_ge(q.tr.sem, q.tr.at(g + 1))
                            if not_zero(g):
                                act.wait_ge(q.m1.sem, q.m1.at(g))
                            act.copy(pairT[:, :], psum[:, 0, :]).then_inc(q.trc.sem, 1)
                            act.wait_ge(q.m1.sem, q.m1.at(g + 1))
                            if not_zero(g):
                                act.wait_ge(q.m2.sem, q.m2.at(g))
                            act.activation(h1T[0:D, :], psum[0:D, 1, :], ACT.Relu, bias=b1_sb[:, :]).then_inc(q.m1c.sem, 1)
                            act.wait_ge(q.m2.sem, q.m2.at(g + 1))
                            if not_zero(g):
                                act.wait_ge(q.vals.sem, q.vals.at(g))
                            pre = psum[:, 2, :].rearrange("p (c w) -> p c w", c=CH)[:, :, D:2 * D]
                            act.activation(gate[:, :, :], pre, ACT.Sigmoid).then_inc(q.gate.sem, 1)
                        if make == "attend":
                            act.wait_ge(q.leaky.sem, q.leaky.at(g + 1))
                            if not_zero(g):
                                act.wait_ge(q.vals.sem, q.vals.at(g))
                            act.activation(ex[:, :], leaky[:, :], ACT.Exp).then_inc(q.ex.sem, 1)
                        act.wait_ge(q.summed.sem, q.summed.at(g + 1))
                        if not_first(turn):
                            act.wait_ge(q.scat.sem, q.scat.at(16 * CH * (g - R + 1)))
                        act.copy(sums[s][:, :, :].rearrange("p c w -> p (c w)"),
                                 psum[:, 3, 0:CH * width]).then_inc(q.sums.sem, 1)
                    ring_cycle(act, GROUPS, R, step)
                    if count:
                        act.wait_ge(q.lin.sem, q.lin.at(1))
                        act.activation(root[:, :], deg1[:, :], ACT.Sqrt).then_inc(q.ex.sem, 1)
            for s in range(R):
                q.row[s].end(16 * edges_of(s))
                q.got[s].end(16 * NG * edges_of(s))
            q.scat.end(16 * CH * GROUPS)
            for sig in ([q.gidx, q.sidx, q.same, q.summed, q.sums] + [q.before, q.shift, q.snew] * bool(mark)
                        + [q.vals] * bool(make) + [q.tr, q.trc, q.m1, q.m1c, q.m2, q.gate] * (make == "mlp")
                        + [q.lin, q.leaky, q.ex] * (make == "attend")):
                sig.end(GROUPS)
            if count:
                q.hot.end(2 * CH * GROUPS)
                q.cnt.end(2 * CH * GROUPS)
                q.lin.end(2)
                q.ex.end(1)
            if make == "mlp":
                q.ones.end(1)

        f = FastSignals(signal)
        BATCHES = [(0, CH), (CH, WC)]
        BANKS = J // 2

        def tile_phase(name, ends, gathers, width, stores_of, make=None, add=None, y_of=False):
            NG = len(gathers) * WC
            gwidth = max(c + w for _, _, c, w in gathers)
            mlp = make == "mlp"
            nbuf = 1 if mlp else 2
            lag = 1 if mlp else 2
            vw = A if mlp else width

            with Memory(nc, name) as m:
                g_idx = m.ring("g_idx", WR, [P, len(gathers), WC], i32)
                got = m.ring("got", WR, [P, WC, gwidth])
                hot = m.ring("hot", WR, [P, WC, J, P], bf16)
                pieces = m.ring("pieces", WR, [P, WC, 3, vw], bf16)
                rest = m.ring("rest", WR, [P, WC, vw])
                sums = m.ring("sums", WR, [P, J * width])
                vals = m.ring("vals", WR, [P, WC, vw]) if make else got
                if add is not None:
                    basis = m.ring("basis", WR, [P, J * width])
                    total = m.ring("total", WR, [P, J * width])
                if y_of:
                    y = m.ring("y", WR, [P, J * D])
                if mlp:
                    pairT = m.tile("pairT", [P, WIN])
                    h1T = m.tile("h1T", [A, WIN])
                    gate = m.ring("gate", 2, [P, CH, D])
                    wide = [psum[:, 4, :], psum[:, 6, :]]
                    edges_out, edges_out1, rout = (m.ring(n, 2, [P, J]) for n in ("edges_out", "edges_out1", "rout"))
                if make == "attend":
                    lin, leaky, ex = (m.tile(n, [P, WC]) for n in ("lin", "leaky", "ex"))
                stores = stores_of(total if add is not None else sums, y if y_of else None)
                rows_used, per_tile = {None: (f.rest, 1), "mlp": (f.tr, 2), "attend": (f.vals, 1)}[make]
                block = m.stack.enter_context(nc.Block())

                def bank_of(s, b):
                    return (s % nbuf) * BANKS + b

                @block.sync
                def _(sp):
                    def step(g, s, turn):
                        if not_first(turn):
                            sp.wait_ge(f.fin.sem, f.fin.at(g - WR + 1))
                        sp.dma_start(basis[s][:, :], table_tile(add, g)).then_inc(f.base[s].sem, 16)
                    if add is not None:
                        ring_cycle(sp, TILES, WR, step)

                @block.gpsimd
                def _(pool):
                    def gather(g, s, turn):
                        pool.wait_ge(f.gidx.sem, f.gidx.at(g + 1))
                        if not_first(turn):
                            pool.wait_ge(rows_used.sem, rows_used.at(per_tile * (g - WR + 1)))
                        passed(pool, g)
                        for k, (_, tab, c, w) in enumerate(gathers):
                            for i in range(WC):
                                pool.indirect_dma_start(got[s][:, i, c:c + w], None, tab,
                                                        bass.IndirectOffsetOnAxis(ap=g_idx[s][:, k, i:i + 1], axis=0)
                                                        ).then_inc(f.got[s].sem, 16)
                    ring_cycle(pool, TILES, WR, gather)

                @block.vector
                def _(dve):
                    def gather_index(g, s, turn):
                        if not_first(turn):
                            dve.wait_ge(f.got[s].sem, f.got[s].at(16 * NG * turn))
                        for k, (which, _, _, _) in enumerate(gathers):
                            last = dve.tensor_scalar(g_idx[s][:, k, :], which[:, bass.ds(g * WC, WC)], 0.0, None, ALU.add)
                        last.then_inc(f.gidx.sem, 1)

                    def one_hot(g, s, turn):
                        if not_first(turn):
                            dve.wait_ge(f.acc.sem, f.acc.at(BANKS * (g - WR + 1)))
                        for c in range(WC):
                            last = dve.tensor_scalar(hot[s][:, c, :, :].rearrange("p j q -> p (j q)"),
                                                     iota_jp[:, :, :].rearrange("p j q -> p (j q)"),
                                                     ends.rel[:, bass.ds(g * WC + c, 1)], None, ALU.is_equal)
                        last.then_inc(f.hot.sem, 1)

                    def values(g, s, turn):
                        if mlp:
                            for n, (c0, c1) in enumerate(BATCHES):
                                dve.wait_ge(f.gate.sem, f.gate.at(2 * g + n + 1))
                                inter = wide[n][:, 0:(c1 - c0) * P].rearrange("p (c w) -> p c w", w=P)[:, :, 0:D]
                                dve.tensor_tensor(vals[s][:, c0:c1, 0:D], inter, gate[n][:, 0:c1 - c0, :],
                                                  ALU.mult).then_inc(f.vals.sem, 1)
                        if make == "attend":
                            dve.wait_ge(f.got[s].sem, f.got[s].at(16 * NG * (turn + 1)))
                            dve.tensor_tensor(lin[:, :].unsqueeze(2), got[s][:, :, D:A], got[s][:, :, A:A + 1],
                                              ALU.add).then_inc(f.lin.sem, 1)
                            dve.wait_ge(f.lin.sem, f.lin.at(g + 1))
                            dve.scalar_tensor_tensor(leaky[:, :], lin[:, :], SLOPE, lin[:, :],
                                                     ALU.mult, ALU.max).then_inc(f.leaky.sem, 1)
                            dve.wait_ge(f.ex.sem, f.ex.at(g + 1))
                            dve.tensor_tensor(vals[s][:, :, 0:D], got[s][:, :, 0:D],
                                              ex[:, :].unsqueeze(2).to_broadcast([P, WC, D]), ALU.mult)
                            dve.tensor_copy(vals[s][:, :, D:A], ex[:, :].unsqueeze(2)).then_inc(f.vals.sem, 1)

                    def split(g, s, turn):
                        dve.wait_ge(f.high.sem, f.high.at(g + 1))
                        dve.tensor_tensor(rest[s][:, :, :], vals[s][:, :, 0:vw], pieces[s][:, :, 0, :],
                                          ALU.subtract).then_inc(f.rest.sem, 1)

                    def lowest(g, s, turn):
                        dve.wait_ge(f.mid.sem, f.mid.at(g + 1))
                        dve.tensor_tensor(pieces[s][:, :, 2, :], rest[s][:, :, :], pieces[s][:, :, 1, :],
                                          ALU.subtract).then_inc(f.pieces.sem, 1)

                    def finish(g, s, turn):
                        if not_first(turn):
                            dve.wait_ge(f.out[s].sem, f.out[s].at(16 * len(stores) * turn))
                        for b in range(BANKS):
                            dve.wait_ge(f.acc.sem, f.acc.at(BANKS * g + b + 1))
                            three = psum[:, bank_of(s, b), 0:6 * vw].rearrange("p (j k w) -> p j w k", j=2, k=3)
                            if mlp:
                                dve.tensor_reduce(edges_out[s % 2][:, 2 * b:2 * b + 2].unsqueeze(2), three[:, :, D:A, :],
                                                  AX_X, ALU.add)
                            dve.tensor_reduce(rows3(sums[s], width)[:, 2 * b:2 * b + 2, :], three[:, :, 0:width, :],
                                              AX_X, ALU.add).then_inc(f.red.sem, 1)
                        dve.wait_ge(f.red.sem, f.red.at(BANKS * (g + 1)))
                        if mlp:
                            dve.tensor_scalar(edges_out1[s % 2][:, :], edges_out[s % 2][:, :], 1.0, None,
                                              ALU.max).then_inc(f.lin.sem, 1)
                            dve.wait_ge(f.lin.sem, f.lin.at(g + 1))
                            dve.reciprocal(rout[s % 2][:, :], edges_out1[s % 2][:, :]).then_inc(f.leaky.sem, 1)
                            dve.wait_ge(f.leaky.sem, f.leaky.at(g + 1))
                            dve.tensor_scalar(rcnt[:, bass.ds(g * J, J)], rout[s % 2][:, :], 0.0, None,
                                              ALU.add).then_inc(f.fin.sem, 1)
                        elif y_of:
                            dve.tensor_tensor(rows3(y[s]), rows3(sums[s]), bc(dinv2[:, bass.ds(g * J, J)]),
                                              ALU.mult).then_inc(f.fin.sem, 1)
                        elif add is not None:
                            dve.wait_ge(f.base[s].sem, f.base[s].at(16 * (turn + 1)))
                            dve.tensor_tensor(total[s][:, :], basis[s][:, :], sums[s][:, :],
                                              ALU.add).then_inc(f.fin.sem, 1)
                        else:
                            dve.sem_inc(f.fin.sem, 1)

                    def step(g, s, turn):
                        ahead = s + IDX_AHEAD
                        if not isinstance(turn, int) or g + IDX_AHEAD < TILES:
                            gather_index(g + IDX_AHEAD, ahead % WR, turn + ahead // WR)
                        one_hot(g, s, turn)
                        values(g, s, turn)
                        split(g, s, turn)
                        if not isinstance(turn, int) or g >= lag:
                            finish(g - lag, (s - lag) % WR, turn - (1 if s < lag else 0))
                        lowest(g, s, turn)

                    if mlp:
                        dve.memset(h1T[D:A, :], 1.0)
                        for s in range(WR):
                            last = dve.memset(vals[s][:, :, D:A], 1.0)
                        last.then_inc(f.ones.sem, 1)
                    for g in range(IDX_AHEAD):
                        gather_index(g, g, 0)
                    for g in range(WR):
                        step(g, g, 0)
                    turns = (TILES - IDX_AHEAD) // WR
                    with dve.Fori(1, turns) as turn:
                        for s in range(WR):
                            step(turn * WR + s, s, turn)
                    for g in range(turns * WR, TILES):
                        step(g, g % WR, g // WR)
                    for g in range(TILES - lag, TILES):
                        finish(g, g % WR, g // WR)

                @block.tensor
                def _(pe):
                    def accumulate(g, s, turn, b):
                        if b == 0:
                            pe.wait_ge(f.hot.sem, f.hot.at(g + 1))
                            pe.wait_ge(f.pieces.sem, f.pieces.at(g + 1))
                        if not (isinstance(g, int) and g < nbuf):
                            pe.wait_ge(f.red.sem, f.red.at(BANKS * (g - nbuf) + b + 1))
                        for j in (2 * b, 2 * b + 1):
                            o = (j % 2) * 3 * vw
                            for c in range(WC):
                                last = pe.matmul(psum[:, bank_of(s, b), o:o + 3 * vw], hot[s][:, c, j, :],
                                                 pieces[s][:, c, :, :].rearrange("p k w -> p (k w)"),
                                                 start=c == 0, stop=c == WC - 1)
                        last.then_inc(f.acc.sem, 1)

                    def transposes(g, s, turn, n):
                        c0, c1 = BATCHES[n]
                        if n == 0:
                            pe.wait_ge(f.got[s].sem, f.got[s].at(16 * NG * (turn + 1)))
                        if not_zero(g):
                            pe.wait_ge(f.vals.sem, f.vals.at(2 * g + n - 1))
                        for c in range(c0, c1):
                            last = pe.transpose(wide[n][:, (c - c0) * P:(c - c0 + 1) * P], got[s][:, c, :], ident[:, :])
                        last.then_inc(f.tr.sem, 1)

                    def first_product(g, n):
                        c0, c1 = BATCHES[n]
                        pe.wait_ge(f.trc.sem, f.trc.at(2 * g + n + 1))
                        if not_zero(g):
                            pe.wait_ge(f.m1c.sem, f.m1c.at(2 * g + n - 1))
                        pe.matmul(psum[0:D, 5 + 2 * n, 0:(c1 - c0) * P], w1_sb[:, :], pairT[:, c0 * P:c1 * P], start=True,
                                  stop=True).then_inc(f.m1.sem, 1)

                    def second_products(g, n):
                        c0, c1 = BATCHES[n]
                        pe.wait_ge(f.m1c.sem, f.m1c.at(2 * g + n + 1))
                        if not not_zero(g) and n == 0:
                            pe.wait_ge(f.ones.sem, f.ones.at(1))
                        for c in range(c0, c1):
                            last = pe.matmul(wide[n][:, (c - c0) * P:(c - c0 + 1) * P], h1T[:, c * P:(c + 1) * P], w2_sb[:, :],
                                             start=True, stop=True)
                        last.then_inc(f.m2.sem, 1)

                    def mlp_step(g, s, turn):
                        before = lambda b: ((not isinstance(turn, int) or g >= 1) and
                                            accumulate(g - 1, (s - 1) % WR, None, b))
                        transposes(g, s, turn, 0)
                        transposes(g, s, turn, 1)
                        before(0)
                        first_product(g, 0)
                        before(1)
                        first_product(g, 1)
                        second_products(g, 0)
                        before(2)
                        second_products(g, 1)
                        before(3)

                    def sum_step(g, s, turn):
                        for b in range(BANKS):
                            accumulate(g, s, turn, b)
                    ring_cycle(pe, TILES, WR, mlp_step if mlp else sum_step)
                    if mlp:
                        sum_step(TILES - 1, (TILES - 1) % WR, None)

                @block.scalar
                def _(act):
                    def store(g, s):
                        act.wait_ge(f.fin.sem, f.fin.at(g + 1))
                        for tab, ring in stores:
                            act.dma_start(table_tile(tab, g), ring[s][:, :]).then_inc(f.out[s].sem, 16)

                    def step(g, s, turn):
                        if mlp:
                            for n, (c0, c1) in enumerate(BATCHES):
                                act.wait_ge(f.tr.sem, f.tr.at(2 * g + n + 1))
                                if not_zero(g):
                                    act.wait_ge(f.m1.sem, f.m1.at(2 * g + n - 1))
                                act.copy(pairT[:, c0 * P:c1 * P], wide[n][:, 0:(c1 - c0) * P]).then_inc(f.trc.sem, 1)
                            for n, (c0, c1) in enumerate(BATCHES):
                                act.wait_ge(f.m1.sem, f.m1.at(2 * g + n + 1))
                                if not_zero(g):
                                    act.wait_ge(f.m2.sem, f.m2.at(2 * g + n - 1))
                                act.activation(h1T[0:D, c0 * P:c1 * P], psum[0:D, 5 + 2 * n, 0:(c1 - c0) * P], ACT.Relu,
                                               bias=b1_sb[:, :]).then_inc(f.m1c.sem, 1)
                            for n, (c0, c1) in enumerate(BATCHES):
                                act.wait_ge(f.m2.sem, f.m2.at(2 * g + n + 1))
                                if not_zero(g):
                                    act.wait_ge(f.vals.sem, f.vals.at(2 * g + n - 1))
                                pre = wide[n][:, 0:(c1 - c0) * P].rearrange("p (c w) -> p c w", w=P)[:, :, D:2 * D]
                                act.activation(gate[n][:, 0:c1 - c0, :], pre, ACT.Sigmoid).then_inc(f.gate.sem, 1)
                        if make == "attend":
                            act.wait_ge(f.leaky.sem, f.leaky.at(g + 1))
                            if not_zero(g):
                                act.wait_ge(f.vals.sem, f.vals.at(g))
                            act.activation(ex[:, :], leaky[:, :], ACT.Exp).then_inc(f.ex.sem, 1)
                        if make:
                            act.wait_ge(f.vals.sem, f.vals.at(per_vals * (g + 1)))
                        else:
                            act.wait_ge(f.got[s].sem, f.got[s].at(16 * NG * (turn + 1)))
                        if not_first(turn):
                            act.wait_ge(f.acc.sem, f.acc.at(BANKS * (g - WR + 1)))
                        act.copy(pieces[s][:, :, 0, :], vals[s][:, :, 0:vw]).then_inc(f.high.sem, 1)
                        act.wait_ge(f.rest.sem, f.rest.at(g + 1))
                        act.copy(pieces[s][:, :, 1, :], rest[s][:, :, :]).then_inc(f.mid.sem, 1)
                        if not isinstance(turn, int) or g >= lag:
                            store(g - lag, (s - lag) % WR)
                    per_vals = 2 if mlp else 1
                    ring_cycle(act, TILES, WR, step)
                    for g in range(TILES - lag, TILES):
                        store(g, g % WR)
                    for s in range(WR):
                        act.wait_ge(f.out[s].sem, f.out[s].at(16 * len(stores) * -(-(TILES - s) // WR)))

            for s in range(WR):
                turns = -(-(TILES - s) // WR)
                f.got[s].end(16 * NG * turns)
                f.out[s].end(16 * len(stores) * turns)
                f.base[s].end(16 * turns * (add is not None))
            for sig in ([f.gidx, f.hot, f.high, f.rest, f.mid, f.pieces, f.fin]
                        + [f.vals, f.lin, f.leaky, f.ex] * (make == "attend") + [f.lin, f.leaky] * mlp
                        + [f.vals, f.tr, f.trc, f.m1, f.m1c, f.m2, f.gate] * 2 * mlp):
                sig.end(TILES)
            f.acc.end(BANKS * TILES)
            f.red.end(BANKS * TILES)
            f.ones.end(mlp)

        def degrees(t, g):
            return bc(t[:, bass.ds(g * J, J)])

        def either(fast, general):
            is_it = nc.values_load(is_fast[0:1, 0:1], min_val=0, max_val=1)
            with nc.If(is_it > 0):
                fast()
            with nc.Else():
                general()

        with Memory(nc, "n0") as m:
            xt, hn = (m.ring(k, NR, [P, J * D]) for k in ("x", "h"))
            norm_phase(m, hn, [(x, xt)], [(h_tab, hn)], xt)

        def layer0_fast():
            tile_phase("f0", S, [(S.own, h_tab, 0, D), (S.other, h_tab, D, D)], D,
                       lambda sums, y: [(pool_tab, sums)], make="mlp")

        def layer0_general():
            with nc.Block() as block:
                @block.scalar
                def _(act):
                    n = sum(zero_table(act, tab, q.zero) for tab in (pool_tab, *hop_tab))
                    for tab in (x2_tab, att_tab):
                        act.dma_start(tab[NPAD:ROWS, :].rearrange("(p r) d -> p (r d)", r=4),
                                      zeros[0:(ROWS - NPAD) // 4, 0:4 * tab.shape[1]]).then_inc(q.zero.sem, 16)
                    act.wait_ge(q.zero.sem, q.zero.at(16 * (n + 2)))
            edge_phase("e0", [(S, h_tab, 0, D), (T, h_tab, D, D)], S, pool_tab, D, make="mlp", mark=True, count=True)
        either(layer0_fast, layer0_general)

        with Memory(nc, "n1") as m:
            xt, pt, scaled, x1, hn, x1h, y = (m.ring(k, NR, [P, J * D]) for k in (
                "x", "p", "scaled", "x1", "h", "x1h", "y"))

            def pool_first(pool, g, s):
                pool.tensor_tensor(rows3(scaled[s]), rows3(pt[s]), degrees(rcnt, g), ALU.mult).then_inc(s_pre.sem, 1)

            def before(dve, g, s):
                dve.wait_ge(s_pre.sem, s_pre.at(g + 1))
                dve.tensor_tensor(x1[s][:, :], xt[s][:, :], scaled[s][:, :], ALU.add).then_inc(s_x.sem, 1)

            def after(dve, g, s):
                dve.scalar_tensor_tensor(x1h[s][:, :], hn[s][:, :], 1.0 / (HOPS + 1), x1[s][:, :], ALU.mult, ALU.add)
                dve.tensor_tensor(rows3(y[s]), rows3(hn[s]), degrees(dinv, g), ALU.mult).then_inc(s_ready.sem, 1)

            norm_phase(m, hn, [(x, xt), (pool_tab, pt)], [(x1_tab, x1h), (y_tab[0], y)], x1, before, after, pool_first)

        for k in range(HOPS):
            more = k < HOPS - 1

            def hop_fast():
                tile_phase(f"f1{k}", T, [(T.other, y_tab[k % 2], 0, D)], D,
                           lambda sums, y: [(hop_tab[k], sums)] + [(y_tab[(k + 1) % 2], y)] * more, y_of=more)

            def hop_general():
                edge_phase(f"e1{k}", [(S, y_tab[k % 2], 0, D)], T, hop_tab[k], D, mark=k == 0)
                if more:
                    with Memory(nc, f"n2{k}") as m:
                        hop, y = (m.ring(n, NR, [P, J * D]) for n in ("hop", "y"))

                        def compute(dve, g, s):
                            dve.tensor_tensor(rows3(y[s]), rows3(hop[s]), degrees(dinv2, g),
                                              ALU.mult).then_inc(q.ready.sem, 1)
                        plain_phase([(hop_tab[k], hop)], [(y_tab[(k + 1) % 2], y)], compute,
                                    s_in=q.in_, s_out=q.out, s_ready=q.ready)
            either(hop_fast, hop_general)

        with Memory(nc, "n3") as m:
            x1, h0, h1, h2, two, three, mixed, x2, hn = (m.ring(k, NR if k not in ("three", "mixed") else 2, [P, J * D])
                                                         for k in ("x1", "h0", "h1", "h2", "two", "three", "mixed", "x2", "h"))

            def pool_first(pool, g, s):
                pool.tensor_tensor(two[s][:, :], h0[s][:, :], h1[s][:, :], ALU.add).then_inc(s_pre.sem, 1)

            def before(dve, g, s):
                dve.wait_ge(s_pre.sem, s_pre.at(g + 1))
                dve.tensor_tensor(three[s % 2][:, :], two[s][:, :], h2[s][:, :], ALU.add).then_inc(s_u.sem, 1)
                dve.wait_ge(s_u.sem, s_u.at(g + 1))
                dve.scalar_tensor_tensor(rows3(mixed[s % 2]), rows3(three[s % 2]), 1.0 / (HOPS + 1), degrees(dinv, g),
                                         ALU.mult, ALU.mult).then_inc(s_v.sem, 1)
                dve.wait_ge(s_v.sem, s_v.at(g + 1))
                dve.tensor_tensor(x2[s][:, :], mixed[s % 2][:, :], x1[s][:, :], ALU.add).then_inc(s_x.sem, 1)

            norm_phase(m, hn, [(x1_tab, x1), (hop_tab[0], h0), (hop_tab[1], h1), (hop_tab[2], h2)],
                       [(x2_tab, x2), (h_tab, hn)], x2, before, pool_first=pool_first, stored_resid=True)
            s_u.end(TILES)
            s_v.end(TILES)

        either(lambda: tile_phase("f2", S, [(S.other, h_tab, 0, D)], D, lambda total, y: [(x2_tab, total)], add=x2_tab),
               lambda: edge_phase("e2", [(T, h_tab, 0, D)], S, x2_tab, D))

        with Memory(nc, "n4") as m:
            x3, hn = (m.ring(k, NR, [P, J * D]) for k in ("x3", "h"))
            hw, att = (m.ring(k, NR, [P, J * A]) for k in ("hw", "att"))
            as_ = m.ring("as", NR, [P, J])
            norm_phase(m, hn, [(x2_tab, x3)], [(hw_tab, hw), (as_tab, as_), (att_tab, att)], x3,
                       project=(hw, as_, att))

        either(lambda: tile_phase("f3", S, [(S.other, hw_tab, 0, A), (S.own, as_tab, A, 1)], A,
                                  lambda total, y: [(att_tab, total)], make="attend", add=att_tab),
               lambda: edge_phase("e3", [(T, hw_tab, 0, A), (S, as_tab, A, 1)], S, att_tab, A, make="attend"))

        with Memory(nc, "n5") as m:
            x3, share, y = (m.ring(k, NR, [P, J * D]) for k in ("x3", "share", "y"))
            att = m.ring("att", NR, [P, J * A])
            rden = m.ring("rden", NR, [P, J])

            def compute(dve, g, s):
                dve.reciprocal(rden[s][:, :].unsqueeze(2), rows3(att[s], A)[:, :, D:A]).then_inc(s_u.sem, 1)
                dve.wait_ge(s_u.sem, s_u.at(g + 1))
                dve.tensor_tensor(rows3(share[s]), rows3(att[s], A)[:, :, 0:D], bc(rden[s][:, :]),
                                  ALU.mult).then_inc(s_v.sem, 1)
                dve.wait_ge(s_v.sem, s_v.at(g + 1))
                dve.tensor_tensor(y[s][:, :], x3[s][:, :], share[s][:, :], ALU.add).then_inc(s_ready.sem, 1)

            plain_phase([(x2_tab, x3), (att_tab, att)], [(out, y)], compute, more=[s_u, s_v])


_INS = ["x", "src", "dst", "L0_gnn_W1", "L0_gnn_b1", "L0_gnn_W2", "L0_gnn_b2", "L0_gnn_Wg", "L0_gnn_bg",
        "L3_gnn_W", "L3_gnn_a"]


def kernel(**inputs):
    import numpy as _np
    import concourse.bacc as _bacc
    from concourse import mybir as _mybir
    from concourse.bass_utils import run_bass_kernel_spmd as _run

    nc = _bacc.Bacc("TRN2", target_bir_lowering=False, num_devices=1)
    arrays, args = {}, []
    for name in _INS:
        a = _np.ascontiguousarray(inputs[name])
        arrays[f"in_{name}_dram"] = a
        args.append(nc.dram_tensor(f"in_{name}_dram", a.shape, _mybir.dt.from_np(a.dtype), kind="ExternalInput").ap())
    shape = _np.asarray(inputs["x"]).shape
    args.append(nc.dram_tensor("out_0_dram", shape, _mybir.dt.float32, kind="ExternalOutput").ap())
    gnn_kernel(nc, *args)
    r = _run(nc, [arrays], core_ids=[0])
    return r.results[0]["out_0_dram"]
```

```python
import concourse.bass as bass
from concourse import mybir
from contextlib import ExitStack

P = 128
D = 64
J = 8
TILE = P * J
LANES = 128
CH = 4
GROUP = CH * LANES
R = 4
AHEAD = 2
IDX_AHEAD = 3
WC = 5
WIN = WC * LANES
BINC = 28
WR = 4
NR = 6
EPS = 1e-5
SLOPE = 0.2
HOPS = 3

fp32 = mybir.dt.float32
fp16 = mybir.dt.float16
bf16 = mybir.dt.bfloat16
i32 = mybir.dt.int32
ALU = mybir.AluOpType
ACT = mybir.ActivationFunctionType
AX_X = mybir.AxisListType.X


class Signal:

    def __init__(self, sem):
        self.sem, self.base = sem, 0

    def at(self, n):
        return n + self.base

    def end(self, n):
        self.base += n


def ring_cycle(eng, n, slots, step, peeled=1):
    turns = n // slots
    for g in range(min(peeled * slots, n)):
        step(g, g % slots, g // slots)
    if turns > peeled:
        with eng.Fori(peeled, turns) as turn:
            for s in range(slots):
                step(turn * slots + s, s, turn)
    for g in range(max(turns, peeled) * slots, n):
        step(g, g % slots, g // slots)


def not_first(turn):
    return not (isinstance(turn, int) and turn == 0)


class NormSignals:

    def __init__(self, signal):
        self.x = signal("n_x")
        self.sum = signal("n_sum")
        self.mean = signal("n_mean")
        self.cen = signal("n_cen")
        self.sqr = signal("n_sqr")
        self.ssq = signal("n_ssq")
        self.hn = signal("n_hn")
        self.ready = signal("n_ready")
        self.pre = signal("n_pre")
        self.u = signal("n_u")
        self.v = signal("n_v")

    def each_tile(self):
        return [self.x, self.sum, self.mean, self.cen, self.sqr, self.ssq, self.hn, self.ready, self.pre,
                self.u, self.v]


class NormTransfers(NormSignals):

    def __init__(self, signal, signals, name, slots):
        (self.x, self.sum, self.mean, self.cen, self.sqr, self.ssq, self.hn, self.ready, self.pre,
         self.u, self.v) = signals.each_tile()
        self.std = signal(f"{name}_std")
        self.rstd = signal(f"{name}_rstd")
        self.in_ = [signal(f"{name}_in{s}") for s in range(slots)]
        self.out = [signal(f"{name}_out{s}") for s in range(slots)]


class GeneralSignals:

    def __init__(self, signal):
        self.gidx = signal("g_gidx")
        self.sidx = signal("g_sidx")
        self.same = signal("g_same")
        self.before = signal("g_before")
        self.shift = signal("g_shift")
        self.snew = signal("g_snew")
        self.vals = signal("g_vals")
        self.summed = signal("g_summed")
        self.sums = signal("g_sums")
        self.scat = signal("g_scat")
        self.tr = signal("g_tr")
        self.trc = signal("g_trc")
        self.m1 = signal("g_m1")
        self.m1c = signal("g_m1c")
        self.m2 = signal("g_m2")
        self.gate = signal("g_gate")
        self.hot = signal("g_hot")
        self.cnt = signal("g_cnt")
        self.lin = signal("g_lin")
        self.leaky = signal("g_leaky")
        self.ex = signal("g_ex")
        self.ones = signal("g_ones")
        self.ready = signal("g_ready")
        self.zero = signal("g_zero")
        self.row = [signal(f"g_row{s}") for s in range(R)]
        self.got = [signal(f"g_got{s}") for s in range(R)]


class FastSignals:

    def __init__(self, signal, norm):
        self.gidx = signal("f_gidx")
        self.hot = signal("f_hot")
        self.vals = signal("f_vals")
        self.high = signal("f_high")
        self.rest = signal("f_rest")
        self.mid = signal("f_mid")
        self.pieces = signal("f_pieces")
        self.acc = signal("f_acc")
        self.red = signal("f_red")
        self.fin = signal("f_fin")
        self.tr = signal("f_tr")
        self.trc = signal("f_trc")
        self.m1 = signal("f_m1")
        self.m1c = signal("f_m1c")
        self.m2 = signal("f_m2")
        self.gate = signal("f_gate")
        self.lin = signal("f_lin")
        self.leaky = signal("f_leaky")
        self.ex = signal("f_ex")
        self.ones = signal("f_ones")
        self.got = [signal(f"f_got{s}") for s in range(WR)]
        self.hot_q = self.tr
        self.picked = self.m1
        self.hot_j = self.m1c
        self.masked = self.m2
        self.own_a = self.gate
        self.q_row = [signal(f"f_q_row{s}") for s in range(2)]
        self.base = norm.in_
        self.out = norm.out


class Memory:

    def __init__(self, nc, name):
        self.nc, self.name, self.stack = nc, name, ExitStack()

    def __enter__(self):
        self.stack.__enter__()
        return self

    def __exit__(self, *why):
        return self.stack.__exit__(*why)

    def tile(self, name, shape, dt=fp32):
        return self.stack.enter_context(self.nc.sbuf_tensor(f"{self.name}_{name}", shape, dt))

    def ring(self, name, slots, shape, dt=fp32):
        return [self.tile(f"{name}{s}", shape, dt) for s in range(slots)]


def not_zero(g):
    return not (isinstance(g, int) and g == 0)


def gnn_kernel(nc, x, src, dst, W1, b1, W2, b2, Wg, bg, W3, a3, out):
    N = x.shape[0]
    E = src.shape[0]
    TILES = -(-N // TILE)
    NPAD = TILES * TILE
    LAST_P = (N - (TILES - 1) * TILE) // J
    assert (N - (TILES - 1) * TILE) % J == 0
    GROUPS = -(-E // GROUP)
    CHUNKS = GROUPS * CH
    assert GROUPS <= P and E > (CHUNKS - 2) * LANES
    HI = TILES * J
    EDGES = CHUNKS * LANES
    assert CHUNKS % BINC == 0 and TILES <= P and TILES % 2 == 0 and TILE == 1024 and E > (CHUNKS - 2) * LANES
    BINS = CHUNKS // BINC
    SPARE = N + 2 * LANES
    ROWS = SPARE + CH * LANES
    FULL = E // LANES
    REST = E - FULL * LANES
    A = D + 1

    with ExitStack() as ctx:
        def sb(name, shape, dt=fp32):
            return ctx.enter_context(nc.sbuf_tensor(name, shape, dt))

        def ps(name, shape, dt=fp32):
            return ctx.enter_context(nc.psum_tensor(name, shape, dt))

        def signal(name):
            return Signal(ctx.enter_context(nc.semaphore(name)))

        def table(name, rows, width):
            return nc.dram_tensor(name, (rows, width), fp32, kind="Internal").ap()

        h_tab = table("h_tab", NPAD, D)
        y_tab = [table(f"y_tab{k}", NPAD, D) for k in range(2)]
        x1_tab = table("x1_tab", NPAD, D)
        x2_tab = table("x2_tab", ROWS, D)
        pool_tab = table("pool_tab", ROWS, D)
        hop_tab = [table(f"hop_tab{k}", ROWS, D) for k in range(HOPS)]
        hw_tab = table("hw_tab", NPAD, A)
        as_tab = table("as_tab", NPAD, 1)
        att_tab = table("att_tab", ROWS, A)
        x_end = table("x_end", TILE, D)
        tile_rows = [nc.dram_tensor(f"{e}_tile_row", (CHUNKS * LANES,), fp16, kind="Internal").ap() for e in ("src", "dst")]
        src_q = nc.dram_tensor("src_q", (TILES * WIN,), fp16, kind="Internal").ap()
        src_pairs = nc.dram_tensor("src_pairs", (EDGES, 2), i32, kind="Internal").ap()
        dst_pairs = nc.dram_tensor("dst_pairs", (EDGES, 2), i32, kind="Internal").ap()
        src_row = nc.dram_tensor("src_row", (CHUNKS * LANES,), fp32, kind="Internal").ap()
        dst_row = nc.dram_tensor("dst_row", (CHUNKS * LANES,), fp32, kind="Internal").ap()

        def tile_of(tab, g):
            return tab[0:NPAD, :].rearrange("(g p j) d -> g p (j d)", p=P, j=J)[bass.ds(g, 1)].rearrange(
                "g p n -> p (g n)")

        ident = sb("ident", [P, P])
        zeros = sb("zeros", [P, 56 * D])
        eps = sb("eps", [P, 1])
        three_halves = sb("three_halves", [P, J])
        iota_hi = sb("iota_hi", [P, HI], fp16)
        iota_lo = sb("iota_lo", [P, P], fp16)
        earlier = sb("earlier", [P, CH, GROUP])
        dump = sb("dump", [P, CH])
        w1_sb = sb("w1_sb", [P, D])
        b1_sb = sb("b1_sb", [D, 1])
        w2_sb = sb("w2_sb", [A, 2 * D])
        w2T = sb("w2T", [D, A])
        wg_sb = sb("wg_sb", [D, D])
        bg_pad = sb("bg_pad", [A, D])
        w3_sb = sb("w3_sb", [P, 2 * (D + 2)])
        w3_in = sb("w3_in", [P, D])
        w3T = sb("w3T", [D, P])
        a3_sb = sb("a3_sb", [D, 2])

        class Ends:

            def __init__(self, name, dram, row):
                self.dram, self.row = dram, row
                self.col = sb(f"{name}_col", [P, CHUNKS])
                self.gather = sb(f"{name}_gather", [P, CHUNKS], i32)
                self.scatter = sb(f"{name}_scatter", [P, CHUNKS], i32)
                self.to_dump = sb(f"{name}_to_dump", [P, CHUNKS])
                self.hi = sb(f"{name}_hi", [P, CHUNKS])
                self.lo = sb(f"{name}_lo", [P, CHUNKS])
                self.rel = sb(f"{name}_rel", [P, TILES * WC])
                self.own = sb(f"{name}_own", [P, TILES * WC], i32)
                self.other = sb(f"{name}_other", [P, TILES * WC], i32)

        S = Ends("src", src, src_row)
        T = Ends("dst", dst, dst_row)
        src_j = sb("src_j", [P, TILES * WC])
        src_inside = sb("src_inside", [P, TILES * WC])
        as_all = sb("as_all", [P, HI])
        base = sb("base", [P, CHUNKS])
        part = sb("part", [P, 1])
        tile_id = sb("tile_id", [P, CHUNKS])
        pairs = sb("pairs", [P, CHUNKS, 2], i32)
        first_edge = sb("first_edge", [1, 2, P], i32)
        is_fast = sb("is_fast", [1, 1], i32)
        iota_jp = sb("iota_jp", [P, J, P], fp16)
        rcnt = sb("rcnt", [P, HI])
        dinv = sb("dinv", [P, HI])
        dinv2 = sb("dinv2", [P, HI])

        psum = ps("psum", [P, 8, 512])
        counts_out = psum[:, 4:6, :].rearrange("p b n -> p (b n)")
        counts_in = psum[:, 6:8, :].rearrange("p b n -> p (b n)")

        s_const = signal("s_const")
        s_iota = signal("s_iota")
        s_rows = signal("s_rows")
        s_wts = signal("s_wts")
        s_rowf = signal("s_rowf")
        s_pt = signal("s_pt")
        s_dc = signal("s_dc")
        s_passed = signal("s_passed")
        s_bin = signal("s_bin")
        s_binld = [signal(f"s_binld{k}") for k in range(2)]
        s_sort = signal("s_sort")
        s_bpe = signal("s_bpe")
        s_tcnt = signal("s_tcnt")
        s_kept = signal("s_kept")
        s_onehot = signal("s_onehot")
        s_cnt = signal("s_cnt")
        s_deg = signal("s_deg")
        s_root = signal("s_root")
        s_eqt = signal("s_eqt")
        s_rank = signal("s_rank")
        s_base = signal("s_base")
        s_pos = signal("s_pos")
        s_place = [signal(f"s_place{s}") for s in range(R)]
        s_win = [signal(f"s_win{k}") for k in range(2)]
        s_trow = [signal(f"s_trow{s}") for s in range(R)]
        s_tr = signal("s_tr")
        s_trc = signal("s_trc")
        s_m1 = signal("s_m1")
        s_lin = signal("s_lin")
        s_leaky = signal("s_leaky")
        s_ex = signal("s_ex")
        s_guess = signal("s_guess")
        s_newton = signal("s_newton")
        every_norm = NormSignals(signal)
        n_signals = NormTransfers(signal, every_norm, "n", NR)
        g_norm = NormTransfers(signal, every_norm, "gn", NR)
        f_norm = NormTransfers(signal, every_norm, "fn", WR)
        s_t3 = signal("s_t3")
        s_t3b = signal("s_t3b")

        def passed(pool, n):
            if not isinstance(n, int):
                pool.sem_inc(s_passed.sem, 1)

        def zero_table(eng, tab, done):
            rows, n, at, step, width = ROWS, 0, 0, 56, D
            while rows - at >= P:
                k = min(step, (rows - at) // P)
                eng.dma_start(tab[at:at + P * k, :].rearrange("(p r) d -> p (r d)", p=P),
                              zeros[:, 0:k * width]).then_inc(done.sem, 16)
                at += P * k
                n += 1
            if rows > at:
                eng.dma_start(tab[at:rows, :], zeros[0:rows - at, 0:width]).then_inc(done.sem, 16)
                n += 1
            return n

        def bc(ap):
            return ap.unsqueeze(2).to_broadcast([P, ap.shape[1], D])

        def rows3(t, w=D):
            return t[:, :].rearrange("p (j d) -> p j d", d=w)

        with Memory(nc, "prep") as m, nc.Block() as block:
            bits = m.ring("bits", 4, [P, CHUNKS], i32)
            for e, name in ((S, "src"), (T, "dst")):
                e.rows_i = m.tile(f"{name}_rows_i", [GROUPS, CH, LANES], i32)
                e.rows_f = m.tile(f"{name}_rows_f", [GROUPS, CH, LANES])

            @block.gpsimd
            def _(pool):
                pool.iota(S.rows_i[:, :, :], [[0, CH], [1, LANES]], base=N - (GROUPS - 2) * LANES,
                          channel_multiplier=LANES).then_inc(s_iota.sem, 1)
                pool.iota(T.rows_i[:, :, :], [[0, CH], [1, LANES]], base=N - (GROUPS - 2) * LANES,
                          channel_multiplier=LANES).then_inc(s_iota.sem, 1)
                pool.memset(ident[:, :], 0.0).then_inc(s_const.sem, 1)
                pool.memset(bg_pad[:, :], 0.0).then_inc(s_const.sem, 1)
                pool.memset(w3_sb[:, :], 0.0).then_inc(s_const.sem, 1)
                pool.memset(earlier[:, :, :], 1.0).then_inc(s_const.sem, 1)
                pool.memset(zeros[:, :], 0.0).then_inc(s_const.sem, 1)
                pool.iota(iota_jp[:, :, :], [[1, J], [J, P]], base=0, channel_multiplier=0,
                          allow_small_or_imprecise_dtypes=True).then_inc(s_const.sem, 1)
                pool.memset(three_halves[:, :], 1.5)
                pool.memset(eps[:, :], EPS).then_inc(s_const.sem, 1)
                pool.iota(iota_hi[:, :], [[1, HI]], base=0, channel_multiplier=0,
                          allow_small_or_imprecise_dtypes=True).then_inc(s_const.sem, 1)
                pool.iota(iota_lo[:, :], [[1, P]], base=0, channel_multiplier=0,
                          allow_small_or_imprecise_dtypes=True).then_inc(s_const.sem, 1)
                pool.iota(dump[:, :], [[LANES, CH]], base=SPARE, channel_multiplier=1,
                          allow_small_or_imprecise_dtypes=True).then_inc(s_const.sem, 1)
                pool.wait_ge(s_const.sem, s_const.at(10))
                pool.affine_select(out=ident[:, :], in_=ident[:, :], compare_op=ALU.not_equal, fill=1.0,
                                   base=0, pattern=[[-1, P]], channel_multiplier=1).then_inc(s_const.sem, 1)
                for i in range(CH):
                    pool.affine_select(out=earlier[:, i, :], in_=earlier[:, i, :], compare_op=ALU.is_gt, fill=0.0,
                                       base=LANES * i, pattern=[[-1, GROUP]],
                                       channel_multiplier=1).then_inc(s_const.sem, 1)

            tile_rows_i = m.ring("tile_rows_i", 2, [GROUPS, CH, LANES], i32)
            tile_rows_f = m.ring("tile_rows_f", 2, [GROUPS, CH, LANES], fp16)
            dst_pair_rows = m.tile("dst_pair_rows", [GROUPS, CH, LANES, 2], i32)
            tid_i = m.tile("tid_i", [P, CHUNKS], i32)

            @block.sync
            def _(sp):
                sp.wait_ge(s_iota.sem, s_iota.at(2))
                for e in (S, T):
                    whole = FULL // GROUPS
                    sp.dma_start(e.rows_i[:, 0:whole, :], e.dram[0:whole * GROUPS * LANES].rearrange(
                        "(t c m) -> c t m", c=GROUPS, m=LANES)).then_inc(s_rows.sem, 16)
                    more = FULL - whole * GROUPS
                    sp.dma_start(e.rows_i[0:more, whole, :], e.dram[whole * GROUPS * LANES:FULL * LANES].rearrange(
                        "(c m) -> c m", m=LANES)).then_inc(s_rows.sem, 16)
                    sp.dma_start(e.rows_i[more:more + 1, whole, 0:REST], e.dram[FULL * LANES:E].rearrange(
                        "(c m) -> c m", c=1)).then_inc(s_rows.sem, 16)
                sp.wait_ge(s_const.sem, s_const.at(10))
                sp.dma_start(w1_sb[:, :], W1).then_inc(s_wts.sem, 16)
                sp.dma_start(b1_sb[:, :], b1.rearrange("(p o) -> p o", o=1)).then_inc(s_wts.sem, 16)
                sp.dma_start(w2_sb[0:D, 0:D], W2).then_inc(s_wts.sem, 16)
                sp.dma_start(w2_sb[D:A, 0:D], b2.rearrange("(o n) -> o n", o=1)).then_inc(s_wts.sem, 16)
                sp.dma_start(wg_sb[:, :], Wg).then_inc(s_wts.sem, 16)
                sp.dma_start(bg_pad[D:A, :], bg.rearrange("(o n) -> o n", o=1)).then_inc(s_wts.sem, 16)
                for k in range(2):
                    sp.dma_start(w3_in[k * D:(k + 1) * D, :], W3).then_inc(s_wts.sem, 16)
                    sp.dma_start(w3_sb[k * D:(k + 1) * D, k * (D + 2):k * (D + 2) + D], W3).then_inc(s_wts.sem, 16)
                for k in range(2):
                    sp.dma_start(a3_sb[:, k:k + 1], a3[(1 - k) * D:(2 - k) * D].rearrange(
                        "(p o) -> p o", o=1)).then_inc(s_wts.sem, 16)
                sp.wait_ge(s_dc.sem, s_dc.at(2))
                for e in (S, T):
                    sp.dma_start(e.row.rearrange("(t c m) -> c t m", c=GROUPS, m=LANES),
                                 e.rows_f[:, :, :]).then_inc(s_rowf.sem, 16)
                sp.wait_ge(s_bin.sem, s_bin.at(2))
                for k in range(2):
                    sp.dma_start(tile_rows[k].rearrange("(t c m) -> c t m", c=GROUPS, m=LANES),
                                 tile_rows_f[k][:, :, :]).then_inc(s_rowf.sem, 16)
                sp.dma_start(dst_pairs.rearrange("(t c m) w -> c t (m w)", c=GROUPS, m=LANES),
                             dst_pair_rows[:, :, :, :].rearrange("c t m w -> c t (m w)")).then_inc(s_rowf.sem, 16)
                sp.dma_start(x_end.rearrange("(p j) d -> p (j d)", j=J), zeros[:, 0:J * D]).then_inc(s_rowf.sem, 16)
                sp.wait_ge(s_rowf.sem, s_rowf.at(96))
                sp.dma_start(x_end[0:N - (TILES - 1) * TILE, :], x[(TILES - 1) * TILE:N, :]).then_inc(s_rowf.sem, 16)
                sp.wait_ge(s_rowf.sem, s_rowf.at(112))

            @block.tensor
            def _(pe):
                pe.wait_ge(s_const.sem, s_const.at(11))
                pe.wait_ge(s_dc.sem, s_dc.at(2))
                for n, e in enumerate((S, T)):
                    for t in range(CH):
                        last = pe.transpose(psum[:, n, t * GROUPS:(t + 1) * GROUPS], e.rows_f[:, t, :],
                                            ident[0:GROUPS, 0:GROUPS])
                    last.then_inc(s_pt.sem, 1)
                pe.wait_ge(s_wts.sem, s_wts.at(16 * 12))
                pe.transpose(psum[0:D, 2, 0:A], w2_sb[:, 0:D], ident[0:A, 0:A]).then_inc(s_pt.sem, 1)
                pe.transpose(psum[0:D, 3, 0:P], w3_in[:, :], ident[:, :]).then_inc(s_pt.sem, 1)
                pe.wait_ge(s_trc.sem, s_trc.at(2))
                pe.matmul(psum[0:A, 4, 0:D], w2T[:, :], wg_sb[:, :], start=True, stop=True).then_inc(s_pt.sem, 1)
                pe.matmul(psum[:, 5, 0:2], w3T[:, :], a3_sb[:, :], start=True, stop=True).then_inc(s_pt.sem, 1)

            @block.scalar
            def _(act):
                act.wait_ge(s_pt.sem, s_pt.at(3))
                act.copy(w2T[:, :], psum[0:D, 2, 0:A]).then_inc(s_trc.sem, 1)
                act.wait_ge(s_pt.sem, s_pt.at(4))
                act.copy(w3T[:, :], psum[0:D, 3, 0:P]).then_inc(s_trc.sem, 1)
                act.wait_ge(s_pt.sem, s_pt.at(6))
                for k in range(2):
                    o = k * (D + 2) + D
                    act.copy(w3_sb[k * D:(k + 1) * D, o:o + 2], psum[k * D:(k + 1) * D, 5, 0:2])

            @block.vector
            def _(dve):
                dve.wait_ge(s_rows.sem, s_rows.at(16 * 6))
                for e in (S, T):
                    dve.tensor_copy(e.rows_f[:, :, :], e.rows_i[:, :, :]).then_inc(s_dc.sem, 1)
                n = 2
                dve.wait_ge(s_const.sem, s_const.at(15))
                for k, e in enumerate((S, T)):
                    dve.wait_ge(s_pt.sem, s_pt.at(k + 1))
                    dve.tensor_copy(e.col[:, :], psum[:, k, 0:CHUNKS])
                    dve.tensor_copy(e.gather[:, :], psum[:, k, 0:CHUNKS]).then_inc(s_dc.sem, 1)
                    n += 1
                    dve.wait_ge(s_dc.sem, s_dc.at(n))
                    dve.tensor_scalar(bits[0][:, :], e.gather[:, :], 10, 3, ALU.logical_shift_right,
                                      ALU.logical_shift_left)
                    dve.tensor_scalar(bits[1][:, :], e.gather[:, :], 7, None, ALU.bitwise_and)
                    dve.tensor_scalar(bits[2][:, :], e.gather[:, :], 3, P - 1, ALU.logical_shift_right,
                                      ALU.bitwise_and)
                    dve.tensor_tensor(e.to_dump[:, :].rearrange("p (g c) -> p g c", c=CH),
                                      dump[:, :].unsqueeze(1).to_broadcast([P, GROUPS, CH]),
                                      e.col[:, :].rearrange("p (g c) -> p g c", c=CH),
                                      ALU.subtract).then_inc(s_dc.sem, 1)
                    n += 1
                    dve.wait_ge(s_dc.sem, s_dc.at(n))
                    dve.tensor_tensor(bits[3][:, :], bits[0][:, :], bits[1][:, :], ALU.bitwise_or)
                    dve.tensor_copy(e.lo[:, :], bits[2][:, :]).then_inc(s_dc.sem, 1)
                    n += 1
                    dve.wait_ge(s_dc.sem, s_dc.at(n))
                    dve.tensor_copy(e.hi[:, :], bits[3][:, :]).then_inc(s_dc.sem, 1)
                    n += 1
                    dve.wait_ge(s_dc.sem, s_dc.at(n))
                for k, e in enumerate((S, T)):
                    dve.tensor_scalar(tile_rows_i[k][:, :, :], e.rows_i[:, :, :], 10, None, ALU.logical_shift_right)
                dve.tensor_scalar(tid_i[:, :], S.gather[:, :], 10, None, ALU.logical_shift_right)
                dve.tensor_copy(pairs[:, :, 0:1], S.gather[:, :].unsqueeze(2))
                dve.tensor_copy(pairs[:, :, 1:2], T.gather[:, :].unsqueeze(2))
                dve.tensor_copy(dst_pair_rows[:, :, :, 0], T.rows_i[:, :, :])
                dve.tensor_copy(dst_pair_rows[:, :, :, 1], S.rows_i[:, :, :]).then_inc(s_bin.sem, 1)
                dve.wait_ge(s_bin.sem, s_bin.at(1))
                dve.tensor_copy(tile_id[:, :], tid_i[:, :])
                for k in range(2):
                    last = dve.tensor_copy(tile_rows_f[k][:, :, :], tile_rows_i[k][:, :, :])
                last.then_inc(s_bin.sem, 1)
                dve.wait_ge(s_pt.sem, s_pt.at(5))
                dve.tensor_tensor(w2_sb[:, D:2 * D], psum[0:A, 4, 0:D], bg_pad[:, :], ALU.add)
        s_pt.end(6)
        s_trc.end(2)
        s_bin.end(2)
        s_const.end(15)
        s_dc.end(10)

        counts_m = Memory(nc, "counts")
        with counts_m as m:
            edge_b = m.ring("edge_b", 2, [P, BINC * LANES], fp16)
            is_tile = m.ring("is_tile", 2, [P, BINC, LANES], bf16)
            cnt_step = m.ring("cnt_step", 2, [P, BINC])
            is_less = m.ring("is_less", 2, [P, BINC * LANES], bf16)
            less = m.tile("less", [P, 2, BINS])
            less_step = m.ring("less_step", 2, [P, 2])
            cnt = m.tile("cnt", [P, CHUNKS])
            scan = m.ring("scan", 2, [P, CHUNKS])
            bound = m.tile("bound", [P, 2])
            before = m.tile("before", [P, P])
            totals = m.tile("totals", [P, 4])
            starts = m.tile("starts", [P, 2])
            clamped = m.tile("clamped", [P, 2])
            over = m.tile("over", [P, 4])
            worst = m.tile("worst", [P, 1])
            worst1 = m.tile("worst1", [1, 1])
            flag = m.tile("flag", [1, 1])
            edges_now = m.tile("edges_now", [GROUPS, GROUP])
            edges_next = m.tile("edges_next", [GROUPS, GROUP])
            rise = m.tile("rise", [GROUPS, GROUP])

            with nc.Block() as block:
                @block.gpsimd
                def _(pool):
                    pool.iota(part[:, :], [[0, 1]], base=0, channel_multiplier=1,
                              allow_small_or_imprecise_dtypes=True).then_inc(s_const.sem, 1)
                    pool.iota(bound[:, :], [[1, 2]], base=0, channel_multiplier=1,
                              allow_small_or_imprecise_dtypes=True).then_inc(s_const.sem, 1)
                    pool.memset(before[:, :], 1.0).then_inc(s_const.sem, 1)
                    pool.memset(over[:, :], 0.0).then_inc(s_const.sem, 1)
                    pool.memset(edges_next[:, :], 1e9).then_inc(s_const.sem, 1)
                    pool.wait_ge(s_const.sem, s_const.at(5))
                    pool.affine_select(out=before[:, :], in_=before[:, :], compare_op=ALU.is_gt, fill=0.0,
                                       base=0, pattern=[[1, P]], channel_multiplier=-1).then_inc(s_const.sem, 1)

                @block.sync
                def _(sp):
                    sp.dma_start(edges_now[:, :], dst_row.rearrange("(p m) -> p m", m=GROUP)).then_inc(s_sort.sem, 16)
                    sp.wait_ge(s_const.sem, s_const.at(5))
                    sp.dma_start(edges_next[0:GROUPS - 1, :], dst_row[1:1 + (GROUPS - 1) * GROUP].rearrange(
                        "(p m) -> p m", m=GROUP)).then_inc(s_sort.sem, 16)
                    sp.dma_start(edges_next[GROUPS - 1:GROUPS, 0:GROUP - 1], dst_row[1 + (GROUPS - 1) * GROUP:EDGES]
                                 .rearrange("(p m) -> p m", p=1)).then_inc(s_sort.sem, 16)

                    def step(b, s, turn, row, before_this):
                        if not (before_this == 0 and not not_first(turn)):
                            sp.wait_ge(s_tcnt.sem, s_tcnt.at(before_this + b - 1))
                        sp.dma_start(edge_b[s][:, :], row.rearrange("(g e) -> g e", e=BINC * LANES)[
                            bass.ds(b, 1), :].to_broadcast([P, BINC * LANES])).then_inc(s_binld[s].sem, 16)
                    ring_cycle(sp, BINS, 2, lambda b, s, turn: step(b, s, turn, tile_rows[0], 0))
                    ring_cycle(sp, BINS, 2, lambda b, s, turn: step(b, s, turn, tile_rows[1], BINS))

                @block.vector
                def _(dve):
                    dve.wait_ge(s_const.sem, s_const.at(6))

                    def count_src(b, s, turn):
                        dve.wait_ge(s_binld[s].sem, s_binld[s].at(16 * (turn + 1)))
                        dve.tensor_scalar(is_tile[s][:, :, :].rearrange("p c e -> p (c e)"), edge_b[s][:, :],
                                          part[:, :], None, ALU.is_equal).then_inc(s_tcnt.sem, 1)
                        dve.wait_ge(s_tcnt.sem, s_tcnt.at(b + 1))
                        dve.tensor_reduce(cnt_step[s][:, :], is_tile[s][:, :, :], AX_X, ALU.add).then_inc(s_bin.sem, 1)
                        dve.wait_ge(s_bin.sem, s_bin.at(b + 1))
                        dve.tensor_scalar(cnt[:, bass.ds(b * BINC, BINC)], cnt_step[s][:, :], 0.0, None,
                                          ALU.add).then_inc(s_kept.sem, 1)

                    def count_dst(b, s, turn):
                        dve.wait_ge(s_binld[s].sem, s_binld[s].at(16 * (turn + 1) + 16 * (BINS // 2)))
                        if not (isinstance(b, int) and b < 1):
                            dve.wait_ge(s_tcnt.sem, s_tcnt.at(BINS + b))
                        for k in range(2):
                            last = dve.tensor_scalar(is_less[k][:, :], edge_b[s][:, :], bound[:, k:k + 1], 0.0,
                                                     ALU.is_lt, ALU.add, accum_out=less_step[s][:, k:k + 1])
                        last.then_inc(s_tcnt.sem, 1)
                        dve.wait_ge(s_tcnt.sem, s_tcnt.at(BINS + b + 1))
                        dve.tensor_scalar(less[:, :, bass.ds(b, 1)], less_step[s][:, :].unsqueeze(2), 0.0, None,
                                          ALU.add).then_inc(s_kept.sem, 1)
                    ring_cycle(dve, BINS, 2, count_src)
                    ring_cycle(dve, BINS, 2, count_dst)

                    n = BINS
                    dve.wait_ge(s_sort.sem, s_sort.at(48))
                    dve.wait_ge(s_kept.sem, s_kept.at(2 * BINS))
                    dve.tensor_tensor(rise[:, :], edges_now[:, :], edges_next[:, :], ALU.subtract)
                    dve.tensor_scalar(scan[0][:, :], cnt[:, :], 0.0, None, ALU.add)
                    dve.tensor_reduce(totals[:, 0:1], cnt[:, :], AX_X, ALU.add)
                    dve.tensor_reduce(totals[:, 1:3].unsqueeze(2), less[:, :, :], AX_X, ALU.add).then_inc(s_bin.sem, 1)
                    n += 1
                    dve.wait_ge(s_bin.sem, s_bin.at(n))
                    dve.tensor_reduce(over[0:GROUPS, 2:3], rise[:, :], AX_X, ALU.max)
                    cur, d = 0, 1
                    while d < CHUNKS:
                        a, b = scan[cur], scan[1 - cur]
                        dve.tensor_scalar(b[:, 0:d], a[:, 0:d], 0.0, None, ALU.add)
                        dve.tensor_tensor(b[:, d:CHUNKS], a[:, d:CHUNKS], a[:, 0:CHUNKS - d],
                                          ALU.add).then_inc(s_bin.sem, 1)
                        n += 1
                        dve.wait_ge(s_bin.sem, s_bin.at(n))
                        cur, d = 1 - cur, 2 * d
                    dve.tensor_tensor(scan[1 - cur][:, :], scan[cur][:, :], cnt[:, :], ALU.subtract)
                    dve.tensor_scalar(over[:, 0:1], totals[:, 0:1], -float(WIN), None, ALU.add)
                    dve.scalar_tensor_tensor(over[:, 1:2], totals[:, 2:3], -float(WIN), totals[:, 1:2],
                                             ALU.add, ALU.subtract)
                    dve.wait_ge(s_bpe.sem, s_bpe.at(1))
                    dve.tensor_copy(starts[:, 0:1], psum[:, 0, 0:1])
                    dve.tensor_copy(starts[:, 1:2], totals[:, 1:2]).then_inc(s_bin.sem, 1)
                    n += 1
                    dve.wait_ge(s_bin.sem, s_bin.at(n))
                    dve.tensor_scalar(base[:, :], scan[1 - cur][:, :], starts[:, 0:1], None, ALU.add)
                    dve.tensor_scalar(clamped[:, :], starts[:, :], float(EDGES - WIN), None, ALU.min)
                    dve.tensor_reduce(worst[:, :], over[:, :], AX_X, ALU.max).then_inc(s_bin.sem, 1)
                    n += 1
                    dve.wait_ge(s_bpe.sem, s_bpe.at(2))
                    for k in range(2):
                        dve.tensor_copy(first_edge[0:1, k, :], psum[0:1, 1, k * P:(k + 1) * P])
                    dve.tensor_reduce(worst1[:, :], psum[0:1, 1, 2 * P:3 * P], AX_X, ALU.max).then_inc(s_bin.sem, 1)
                    n += 1
                    dve.wait_ge(s_bin.sem, s_bin.at(n))
                    dve.tensor_scalar(flag[:, :], worst1[:, :], 0.0, None, ALU.is_le).then_inc(s_bin.sem, 1)
                    n += 1
                    dve.wait_ge(s_bin.sem, s_bin.at(n))
                    dve.tensor_copy(is_fast[:, :], flag[:, :])
                    s_bin.steps = n

                @block.tensor
                def _(pe):
                    pe.wait_ge(s_const.sem, s_const.at(6))
                    pe.wait_ge(s_bin.sem, s_bin.at(BINS + 1))
                    pe.matmul(psum[:, 0, 0:1], before[:, :], totals[:, 0:1], start=True, stop=True).then_inc(s_bpe.sem, 1)
                    steps = (CHUNKS - 1).bit_length()
                    pe.wait_ge(s_bin.sem, s_bin.at(BINS + 1 + steps + 2))
                    for k in range(2):
                        pe.matmul(psum[0:1, 1, k * P:(k + 1) * P], clamped[:, k:k + 1], ident[:, :], start=True, stop=True)
                    pe.matmul(psum[0:1, 1, 2 * P:3 * P], worst[:, :], ident[:, :], start=True,
                              stop=True).then_inc(s_bpe.sem, 1)
        s_const.end(6)
        s_sort.end(48)
        for k in range(2):
            s_binld[k].end(16 * BINS)
        s_tcnt.end(2 * BINS)
        s_kept.end(2 * BINS)
        s_bin.end(s_bin.steps)
        s_bpe.end(2)

        with Memory(nc, "place") as m:
            hot_hi = m.ring("hot_hi", CH, [P, HI], fp16)
            hot_lo = m.ring("hot_lo", CH, [P, P], fp16)
            deg1, some, rdeg, root, rroot = (m.tile(n, [P, HI]) for n in ("deg1", "some", "rdeg", "root", "rroot"))
            tile_b = m.ring("tile_b", R, [P, GROUP], fp16)
            is_mine = m.ring("is_mine", R, [P, GROUP])
            junk = m.ring("junk", 2, [P, CH, LANES])
            rank = m.ring("rank", R, [P, CH])
            base_now = m.ring("base_now", R, [P, CH])
            place = m.ring("place", R, [P, CH], i32)
            pair = m.ring("pair", R, [P, CH, 2], i32)
            windows = m.ring("windows", 2, [P, TILES * WC, 2], i32)
            own = m.ring("own", 2, [P, TILES * WC])
            tile_start = m.tile("tile_start", [P, TILES * WC])
            own_q, own_j = (m.tile(n, [P, TILES * WC], i32) for n in ("own_q", "own_j"))
            own_q16 = m.tile("own_q16", [P, TILES * WC], fp16)
            from_0 = m.tile("from_0", [P, TILES * WC])

            with nc.Block() as block:
                @block.sync
                def _(sp):
                    def step(g, s, turn):
                        if not_first(turn):
                            sp.wait_ge(s_rank.sem, s_rank.at(g - R + 1))
                        sp.dma_start(tile_b[s][:, :], tile_rows[0].rearrange("(g e) -> g e", e=GROUP)[
                            bass.ds(g, 1), :].to_broadcast([P, GROUP])).then_inc(s_trow[s].sem, 16)
                    ring_cycle(sp, GROUPS, R, step)

                @block.vector
                def _(dve):
                    def degree_rows(g):
                        for i in range(CH):
                            if not_zero(g):
                                dve.wait_ge(s_cnt.sem, s_cnt.at(CH * (g - 1) + i + 1))
                            dve.tensor_scalar(hot_lo[i][:, :], iota_lo[:, :], T.lo[:, bass.ds(g * CH + i, 1)], None,
                                              ALU.is_equal)
                            dve.tensor_scalar(hot_hi[i][:, :], iota_hi[:, :], T.hi[:, bass.ds(g * CH + i, 1)], None,
                                              ALU.is_equal).then_inc(s_onehot.sem, 1)

                    def step(g, s, turn):
                        degree_rows(g)
                        dve.wait_ge(s_trow[s].sem, s_trow[s].at(16 * (turn + 1)))
                        if not_first(turn):
                            dve.wait_ge(s_base.sem, s_base.at(g - R + 1))
                        dve.tensor_scalar(base_now[s][:, :], base[:, bass.ds(g * CH, CH)], 0.0, None, ALU.add)
                        dve.tensor_scalar(is_mine[s][:, :], tile_b[s][:, :], part[:, :], None,
                                          ALU.is_equal).then_inc(s_eqt.sem, 1)
                        for i in range(CH):
                            last = dve.scalar_tensor_tensor(junk[s % 2][:, i, :], tile_b[s][:, i * LANES:(i + 1) * LANES],
                                                            tile_id[:, bass.ds(g * CH + i, 1)], earlier[:, 0, 0:LANES],
                                                            ALU.is_equal, ALU.mult, accum_out=rank[s][:, i:i + 1])
                        last.then_inc(s_rank.sem, 1)
                        dve.wait_ge(s_rank.sem, s_rank.at(g + 1))
                        if not_first(turn):
                            dve.wait_ge(s_place[s].sem, s_place[s].at(16 * CH * turn))
                        dve.tensor_scalar(pair[s][:, :, :], pairs[:, bass.ds(g * CH, CH), :], 0.0, None, ALU.add)
                        dve.wait_ge(s_base.sem, s_base.at(g + 1))
                        dve.tensor_tensor(place[s][:, :], psum[:, s, 0:CH], rank[s][:, :], ALU.add).then_inc(s_pos.sem, 1)
                    ring_cycle(dve, GROUPS, R, step)
                    dve.wait_ge(s_cnt.sem, s_cnt.at(CH * GROUPS))
                    dve.tensor_scalar(some[:, :], counts_in[:, 0:HI], 1.0, None, ALU.min)
                    dve.tensor_scalar(deg1[:, :], counts_in[:, 0:HI], 1.0, None, ALU.max).then_inc(s_deg.sem, 1)
                    dve.wait_ge(s_deg.sem, s_deg.at(1))
                    dve.reciprocal(rdeg[:, :], deg1[:, :])
                    dve.wait_ge(s_root.sem, s_root.at(1))
                    dve.reciprocal(rroot[:, :], root[:, :]).then_inc(s_deg.sem, 1)
                    dve.wait_ge(s_deg.sem, s_deg.at(2))
                    dve.tensor_tensor(dinv[:, :], rroot[:, :], some[:, :], ALU.mult)
                    dve.tensor_tensor(dinv2[:, :], rdeg[:, :], some[:, :], ALU.mult)

                @block.tensor
                def _(pe):
                    def step(g, s, turn):
                        for i in range(CH):
                            pe.wait_ge(s_onehot.sem, s_onehot.at(CH * g + i + 1))
                            first = not not_zero(g) and i == 0
                            end = isinstance(g, int) and g == GROUPS - 1 and i == CH - 1
                            pe.matmul(counts_in[:, 0:512], hot_lo[i][:, :], hot_hi[i][:, 0:512], start=first,
                                      stop=end)
                            pe.matmul(counts_in[:, 512:HI], hot_lo[i][:, :], hot_hi[i][:, 512:HI], start=first,
                                      stop=end).then_inc(s_cnt.sem, 1)
                        pe.wait_ge(s_eqt.sem, s_eqt.at(g + 1))
                        if not_first(turn):
                            pe.wait_ge(s_pos.sem, s_pos.at(g - R + 1))
                        for i in range(CH):
                            last = pe.matmul(psum[:, s, i:i + 1], is_mine[s][:, i * LANES:(i + 1) * LANES],
                                             base_now[s][:, i:i + 1], start=True, stop=True)
                        last.then_inc(s_base.sem, 1)
                    ring_cycle(pe, GROUPS, R, step)

                @block.gpsimd
                def _(pool):
                    pool.iota(tile_start[:, :], [[TILE, TILES], [0, WC]], base=0, channel_multiplier=0,
                              allow_small_or_imprecise_dtypes=True).then_inc(s_const.sem, 1)

                    def step(g, s, turn):
                        pool.wait_ge(s_pos.sem, s_pos.at(g + 1))
                        passed(pool, g)
                        for i in range(CH):
                            pool.indirect_dma_start(src_pairs, bass.IndirectOffsetOnAxis(ap=place[s][:, i:i + 1], axis=0),
                                                    pair[s][:, i, :], None).then_inc(s_place[s].sem, 16)
                    ring_cycle(pool, GROUPS, R, step)
                    for s in range(R):
                        pool.wait_ge(s_place[s].sem, s_place[s].at(16 * CH * -(-(GROUPS - s) // R)))

                @block.scalar
                def _(act):
                    with act.Fori(0, TILES) as t:
                        at = act.value_load(first_edge[0:1, 1, bass.ds(t, 1)], min_val=0, max_val=EDGES - WIN)
                        act.dma_start(windows[1][:, bass.ds(t * WC, WC), :].rearrange("p c w -> p (c w)"),
                                      dst_pairs[bass.ds(at, WIN), :].rearrange("(p c) w -> p (c w)", c=WC)
                                      ).then_inc(s_win[1].sem, 16)
                    act.wait_ge(s_deg.sem, s_deg.at(1))
                    act.activation(root[:, :], deg1[:, :], ACT.Sqrt).then_inc(s_root.sem, 1)
                    act.wait_ge(s_win[1].sem, s_win[1].at(16 * TILES))
            s_const.end(1)
            for s in range(R):
                s_trow[s].end(16 * -(-(GROUPS - s) // R))
                s_place[s].end(16 * CH * -(-(GROUPS - s) // R))

            with nc.Block() as block:
                def src_windows(eng, first, last):
                    with eng.Fori(first, last) as t:
                        at = eng.value_load(first_edge[0:1, 0, bass.ds(t, 1)], min_val=0, max_val=EDGES - WIN)
                        eng.dma_start(windows[0][:, bass.ds(t * WC, WC), :].rearrange("p c w -> p (c w)"),
                                      src_pairs[bass.ds(at, WIN), :].rearrange("(p c) w -> p (c w)", c=WC)
                                      ).then_inc(s_win[0].sem, 16)

                @block.sync
                def _(sp):
                    src_windows(sp, 0, TILES // 2)

                @block.scalar
                def _(act):
                    src_windows(act, TILES // 2, TILES)
                    act.wait_ge(s_bin.sem, s_bin.at(4))
                    act.dma_start(src_q.rearrange("(t p c) -> p t c", p=P, c=WC),
                                  own_q16[:, :].rearrange("p (t c) -> p t c", c=WC)).then_inc(s_rowf.sem, 16)
                    act.wait_ge(s_rowf.sem, s_rowf.at(16))

                @block.vector
                def _(dve):
                    for n, (e, k) in enumerate(((T, 1), (S, 0))):
                        dve.wait_ge(s_win[k].sem, s_win[k].at(16 * TILES))
                        dve.tensor_copy(e.other[:, :].unsqueeze(2), windows[k][:, :, 1:2])
                        dve.tensor_copy(e.own[:, :].unsqueeze(2), windows[k][:, :, 0:1])
                        dve.tensor_copy(own[k][:, :].unsqueeze(2), windows[k][:, :, 0:1]).then_inc(s_bin.sem, 1)
                        dve.wait_ge(s_bin.sem, s_bin.at(n + 1))
                        dve.tensor_tensor(e.rel[:, :], own[k][:, :], tile_start[:, :], ALU.subtract)
                    dve.tensor_scalar(own_q[:, :], S.own[:, :], 3, None, ALU.logical_shift_right)
                    dve.tensor_scalar(own_j[:, :], S.own[:, :], J - 1, None, ALU.bitwise_and).then_inc(s_bin.sem, 1)
                    dve.wait_ge(s_bin.sem, s_bin.at(3))
                    dve.tensor_copy(src_j[:, :], own_j[:, :])
                    dve.scalar_tensor_tensor(own_q16[:, :], tile_start[:, :], -1.0 / J, own_q[:, :], ALU.mult,
                                             ALU.add).then_inc(s_bin.sem, 1)
                    dve.wait_ge(s_bin.sem, s_bin.at(4))
                    dve.tensor_scalar(from_0[:, :], own_q16[:, :], 0.0, None, ALU.is_ge).then_inc(s_bin.sem, 1)
                    dve.wait_ge(s_bin.sem, s_bin.at(5))
                    dve.scalar_tensor_tensor(src_inside[:, :], own_q16[:, :], float(P), from_0[:, :], ALU.is_lt,
                                             ALU.mult)
            s_bin.end(5)
            s_rowf.end(16)

        LAG = 2
        NEWTON = 3
        MAGIC = float(0x5F3759DF)
        POOL_STEPS = 4 * NEWTON

        def guess_root(dve, sig, g, sumsq, var, minus_half, y):
            dve.tensor_scalar(var[:, :], sumsq[:, :], 1.0 / D, EPS, ALU.mult, ALU.add)
            dve.tensor_scalar(minus_half[:, :], sumsq[:, :], -0.5 / D, -0.5 * EPS, ALU.mult,
                              ALU.add).then_inc(sig.sem, 1)
            dve.wait_ge(sig.sem, sig.at(2 * g + 1))
            dve.tensor_scalar(y[:, :].bitcast(i32), var[:, :].bitcast(i32), -0.5, MAGIC, ALU.mult,
                              ALU.add).then_inc(sig.sem, 1)

        def newton_on_pool(pool, sig, g, guessed, minus_half, y0, square, term, factor, between, out_):
            ys = [y0, between[0], between[1], out_]
            for k in range(NEWTON):
                if k == 0:
                    pool.wait_ge(guessed.sem, guessed.at(2 * g + 2))
                else:
                    pool.wait_ge(sig.sem, sig.at(POOL_STEPS * g + 4 * k))
                pool.tensor_tensor(square[:, :], ys[k][:, :], ys[k][:, :], ALU.mult).then_inc(sig.sem, 1)
                pool.wait_ge(sig.sem, sig.at(POOL_STEPS * g + 4 * k + 1))
                pool.tensor_tensor(term[:, :], square[:, :], minus_half[:, :], ALU.mult).then_inc(sig.sem, 1)
                pool.wait_ge(sig.sem, sig.at(POOL_STEPS * g + 4 * k + 2))
                pool.tensor_tensor(factor[:, :], term[:, :], three_halves[:, :], ALU.add).then_inc(sig.sem, 1)
                pool.wait_ge(sig.sem, sig.at(POOL_STEPS * g + 4 * k + 3))
                pool.tensor_tensor(ys[k + 1][:, :], factor[:, :], ys[k][:, :], ALU.mult).then_inc(sig.sem, 1)

        def tiles_of(s, slots=NR):
            return -(-(TILES - s) // slots)

        def table_tile(tab, g):
            n = NPAD if tab.shape[0] >= NPAD else (TILES - 1) * TILE
            return tab[0:n, :].rearrange("(g p j) d -> g p (j d)", p=P, j=J)[bass.ds(g, 1)].rearrange(
                "g p n -> p (g n)")

        def tile_loads(sp, loads, used, w, slots=NR):
            def step(g, s, turn):
                if not_first(turn):
                    sp.wait_ge(used.sem, used.at(g - slots + 1))
                for tab, ring in loads:
                    if tab is x and isinstance(g, int) and g == TILES - 1:
                        part = x_end.rearrange("(p j) d -> p (j d)", j=J)
                    else:
                        part = table_tile(tab, g)
                    sp.dma_start(ring[s][:, :], part).then_inc(w.in_[s].sem, 16)
            ring_cycle(sp, TILES - 1, slots, step)
            step(TILES - 1, (TILES - 1) % slots, (TILES - 1) // slots)

        def tile_stores(act, stores, g, s, w):
            for tab, ring in stores:
                if tab is out and isinstance(g, int) and g == TILES - 1:
                    act.dma_start(out[(TILES - 1) * TILE:N, :].rearrange("(p j) d -> p (j d)", j=J),
                                  ring[s][0:LAST_P, :]).then_inc(w.out[s].sem, 16)
                else:
                    act.dma_start(table_tile(tab, g), ring[s][:, :]).then_inc(w.out[s].sem, 16)

        def end_tiles(loads, stores, signals, w, slots=NR):
            for s in range(slots):
                w.in_[s].end(16 * len(loads) * tiles_of(s, slots))
                w.out[s].end(16 * len(stores) * tiles_of(s, slots))
            for sig in signals:
                sig.end(TILES)

        class Norm:

            def __init__(self, loads, stores, x, h, new_x, after=None, stored_x=False, steps=(), pool_first=None):
                self.loads, self.stores, self.x, self.h = loads, stores, x, h
                self.pool_first = pool_first
                self.new_x, self.after, self.stored_x, self.steps = new_x, after, stored_x, list(steps)

        def norm_phase(m, hn, loads, stores, resid, before=None, after=None, pool_first=None,
                       project=None, stored_resid=False, w=n_signals):
            cen = m.ring("cen", NR, [P, J * D])
            sqr = m.ring("sqr", NR, [P, J * D])
            rowsum, mean, sumsq, std, rstd = (m.ring(name, NR, [P, J]) for name in (
                "rowsum", "mean", "sumsq", "std", "rstd"))
            if project:
                hT = m.ring("hT", 2, [P, J * D])
                lin, leaky, ex = (m.ring(name, NR, [P, J]) for name in ("lin", "leaky", "ex"))
                var, square_, term, factor, between0, between1 = (m.tile(n, [P, J]) for n in (
                    "var", "square", "term", "factor", "between0", "between1"))
                minus_half, guess = (m.ring(n, NR, [P, J]) for n in ("minus_half", "guess"))
            ready = w.ready if after or project else w.hn

            with nc.Block() as block:
                @block.sync
                def _(sp):
                    tile_loads(sp, loads, ready if before or after else w.cen, w)

                @block.gpsimd
                def _(pool):
                    def step(g, s, turn):
                        if pool_first:
                            pool.wait_ge(w.in_[s].sem, w.in_[s].at(16 * len(loads) * (turn + 1)))
                            if not_first(turn):
                                pool.wait_ge(w.x.sem, w.x.at(g - NR + 1))
                            pool_first(pool, g, s)
                        pool.wait_ge(w.mean.sem, w.mean.at(g + 1))
                        if not_first(turn):
                            pool.wait_ge(w.hn.sem, w.hn.at(g - NR + 1))
                        pool.tensor_tensor(rows3(cen[s]), rows3(resid[s]), bc(mean[s][:, :]),
                                           ALU.add).then_inc(w.cen.sem, 1)
                        if project and (not isinstance(g, int) or g >= 1):
                            root(g - 1, (s - 1) % NR)

                    def root(g, s):
                        if not (isinstance(g, int) and g < NR):
                            pool.wait_ge(w.hn.sem, w.hn.at(g - NR + 1))
                        newton_on_pool(pool, s_newton, g, s_guess, minus_half[s], guess[s], square_, term, factor,
                                       (between0, between1), rstd[s])
                    ring_cycle(pool, TILES, NR, step)
                    if project:
                        root(TILES - 1, (TILES - 1) % NR)

                @block.vector
                def _(dve):
                    def part_a(g, s, turn):
                        dve.wait_ge(w.in_[s].sem, w.in_[s].at(16 * len(loads) * (turn + 1)))
                        if stored_resid and not_first(turn):
                            dve.wait_ge(w.out[s].sem, w.out[s].at(16 * len(stores) * turn))
                        if before:
                            before(dve, g, s)
                            dve.wait_ge(w.x.sem, w.x.at(g + 1))
                        dve.tensor_reduce(rowsum[s][:, :], rows3(resid[s]), AX_X, ALU.add).then_inc(w.sum.sem, 1)
                        dve.wait_ge(w.sum.sem, w.sum.at(g + 1))
                        dve.tensor_scalar(mean[s][:, :], rowsum[s][:, :], -1.0 / D, None,
                                          ALU.mult).then_inc(w.mean.sem, 1)

                    def squares_sum(g, s, turn):
                        dve.wait_ge(w.sqr.sem, w.sqr.at(g + 1))
                        dve.tensor_reduce(sumsq[s][:, :], rows3(sqr[s]), AX_X, ALU.add).then_inc(w.ssq.sem, 1)
                        if project:
                            dve.wait_ge(w.ssq.sem, w.ssq.at(g + 1))
                            if not (isinstance(g, int) and g < NR):
                                dve.wait_ge(s_newton.sem, s_newton.at(POOL_STEPS * (g - NR + 1)))
                            guess_root(dve, s_guess, g, sumsq[s], var, minus_half[s], guess[s])

                    def part_b(g, s, turn):
                        if project:
                            dve.wait_ge(s_newton.sem, s_newton.at(POOL_STEPS * (g + 1)))
                        else:
                            dve.wait_ge(w.std.sem, w.std.at(g + 1))
                            dve.reciprocal(rstd[s][:, :], std[s][:, :]).then_inc(w.rstd.sem, 1)
                            dve.wait_ge(w.rstd.sem, w.rstd.at(g + 1))
                        if not_first(turn):
                            dve.wait_ge(w.out[s].sem, w.out[s].at(16 * len(stores) * turn))
                        dve.scalar_tensor_tensor(rows3(hn[s]), rows3(cen[s]), 0.0, bc(rstd[s][:, :]),
                                                 ALU.max, ALU.mult).then_inc(w.hn.sem, 1)
                        if after:
                            dve.wait_ge(w.hn.sem, w.hn.at(g + 1))
                            after(dve, g, s)

                    def part_c(g, s, turn):
                        hw, as_, _ = project
                        if not_first(turn):
                            dve.wait_ge(w.out[s].sem, w.out[s].at(16 * len(stores) * turn))
                        dve.wait_ge(s_m1.sem, s_m1.at(g + 1))
                        half = psum[:, 4 * (s % 2) + 2, 0:4 * (D + 2)].rearrange("p (r w) -> p r w", w=D + 2)
                        dve.tensor_copy(rows3(hw[s], A)[:, 4:8, :], half[:, :, 0:A])
                        dve.tensor_copy(as_[s][:, 4:8].unsqueeze(2), half[:, :, A:A + 1]).then_inc(s_t3b.sem, 1)
                        dve.wait_ge(s_t3b.sem, s_t3b.at(g + 1))
                        dve.wait_ge(s_t3.sem, s_t3.at(g + 1))
                        dve.tensor_scalar(as_all[:, bass.ds(g * J, J)], as_[s][:, :], 0.0, None, ALU.add)
                        dve.tensor_tensor(lin[s][:, :].unsqueeze(2), rows3(hw[s], A)[:, :, D:A],
                                          as_[s][:, :].unsqueeze(2), ALU.add).then_inc(s_lin.sem, 1)
                        dve.wait_ge(s_lin.sem, s_lin.at(g + 1))
                        dve.scalar_tensor_tensor(leaky[s][:, :], lin[s][:, :], SLOPE, lin[s][:, :],
                                                 ALU.mult, ALU.max).then_inc(s_leaky.sem, 1)

                    def part_d(g, s, turn):
                        hw, _, att = project
                        dve.wait_ge(s_ex.sem, s_ex.at(g + 1))
                        dve.tensor_tensor(rows3(att[s], A)[:, :, 0:D], rows3(hw[s], A)[:, :, 0:D], bc(ex[s][:, :]),
                                          ALU.mult)
                        dve.tensor_copy(rows3(att[s], A)[:, :, D:A],
                                        ex[s][:, :].unsqueeze(2)).then_inc(w.ready.sem, 1)

                    def behind(part, g, s, turn, n):
                        if not isinstance(turn, int) or g >= n:
                            part(g - n, (s - n) % NR, turn - (1 if s < n else 0))

                    def both(g, s, turn):
                        ahead = s + LAG
                        if not isinstance(turn, int) or g + LAG < TILES:
                            part_a(g + LAG, ahead % NR, turn + ahead // NR)
                        if not isinstance(turn, int) or g + 1 < TILES:
                            squares_sum(g + 1, (s + 1) % NR, turn)
                        part_b(g, s, turn)
                        if project:
                            behind(part_c, g, s, turn, 2)
                            behind(part_d, g, s, turn, 3)

                    for g in range(LAG):
                        part_a(g, g, 0)
                    squares_sum(0, 0, 0)
                    turns = (TILES - LAG) // NR
                    for g in range(NR):
                        both(g, g, 0)
                    with dve.Fori(1, turns) as turn:
                        for s in range(NR):
                            both(turn * NR + s, s, turn)
                    for g in range(turns * NR, TILES):
                        both(g, g % NR, g // NR)
                    if project:
                        for g in (TILES - 2, TILES - 1):
                            part_c(g, g % NR, g // NR)
                        for g in (TILES - 3, TILES - 2, TILES - 1):
                            part_d(g, g % NR, g // NR)

                @block.tensor
                def _(pe):
                    def transposes(g, s):
                        pe.wait_ge(w.hn.sem, w.hn.at(g + 1))
                        if not (isinstance(g, int) and g < 2):
                            pe.wait_ge(s_trc.sem, s_trc.at(g - 1))
                        for k in range(J // 2):
                            last = pe.transpose(psum[:, 4 * (s % 2), k * P:(k + 1) * P], hn[s][:, k * P:(k + 1) * P],
                                                ident[:, :])
                        last.then_inc(s_tr.sem, 1)

                    def products(g, s):
                        pe.wait_ge(s_trc.sem, s_trc.at(g + 1))
                        if not (isinstance(g, int) and g < 2):
                            pe.wait_ge(s_t3.sem, s_t3.at(g - 1))
                            pe.wait_ge(s_t3b.sem, s_t3b.at(g - 1))
                        for k in range(J // 2):
                            o = (k % 2) * 2 * (D + 2)
                            last = pe.matmul(psum[:, 4 * (s % 2) + 1 + k // 2, o:o + 2 * (D + 2)],
                                             hT[s % 2][:, k * P:(k + 1) * P], w3_sb[:, :], start=True, stop=True)
                        last.then_inc(s_m1.sem, 1)

                    def step(g, s, turn):
                        if not isinstance(turn, int) or g + 1 < TILES:
                            transposes(g + 1, (s + 1) % NR)
                        products(g, s)
                    if project:
                        transposes(0, 0)
                    if project:
                        ring_cycle(pe, TILES, NR, step)

                @block.scalar
                def _(act):
                    def square(g, s, turn):
                        act.wait_ge(w.cen.sem, w.cen.at(g + 1))
                        if not_first(turn):
                            act.wait_ge(w.ssq.sem, w.ssq.at(g - NR + 1))
                        act.activation(sqr[s][:, :], cen[s][:, :], ACT.Square).then_inc(w.sqr.sem, 1)

                    def root(g, s, turn):
                        act.wait_ge(w.ssq.sem, w.ssq.at(g + 1))
                        act.activation(std[s][:, :], sumsq[s][:, :], ACT.Sqrt, bias=eps[:, :],
                                       scale=1.0 / D).then_inc(w.std.sem, 1)

                    def products(g, s, turn):
                        hw, as_, _ = project
                        act.wait_ge(s_tr.sem, s_tr.at(g + 1))
                        if not (isinstance(g, int) and g < 2):
                            act.wait_ge(s_m1.sem, s_m1.at(g - 1))
                        act.copy(hT[s % 2][:, :], psum[:, 4 * (s % 2), :]).then_inc(s_trc.sem, 1)

                    def evacuate(g, s, turn):
                        hw, as_, _ = project
                        if not_first(turn):
                            act.wait_ge(w.out[s].sem, w.out[s].at(16 * len(stores) * turn))
                        act.wait_ge(s_m1.sem, s_m1.at(g + 1))
                        half = psum[:, 4 * (s % 2) + 1, 0:4 * (D + 2)].rearrange("p (r w) -> p r w", w=D + 2)
                        act.copy(rows3(hw[s], A)[:, 0:4, :], half[:, :, 0:A])
                        act.copy(as_[s][:, 0:4].unsqueeze(2), half[:, :, A:A + 1]).then_inc(s_t3.sem, 1)

                    def exps(g, s, turn):
                        act.wait_ge(s_leaky.sem, s_leaky.at(g + 1))
                        act.activation(ex[s][:, :], leaky[s][:, :], ACT.Exp).then_inc(s_ex.sem, 1)

                    def store(g, s, turn):
                        act.wait_ge(ready.sem, ready.at(g + 1))
                        tile_stores(act, stores, g, s, w)

                    def behind(part, g, s, turn, n):
                        if not isinstance(turn, int) or g >= n:
                            part(g - n, (s - n) % NR, turn - (1 if s < n else 0))

                    def step(g, s, turn):
                        ahead = s + LAG
                        if not isinstance(g, int) or g + LAG < TILES:
                            square(g + LAG, ahead % NR, turn + ahead // NR)
                        if not project and (not isinstance(turn, int) or g + 1 < TILES):
                            root(g + 1, (s + 1) % NR, turn)
                        if project:
                            products(g, s, turn)
                            behind(evacuate, g, s, turn, 1)
                            behind(exps, g, s, turn, 2)
                            behind(store, g, s, turn, 3)
                        else:
                            store(g, s, turn)
                    for g in range(LAG):
                        square(g, g, 0)
                    if not project:
                        root(0, 0, 0)
                    turns = (TILES - LAG) // NR
                    for g in range(NR):
                        step(g, g, 0)
                    with act.Fori(1, turns) as turn:
                        for s in range(NR):
                            step(turn * NR + s, s, turn)
                    for g in range(turns * NR, TILES):
                        step(g, g % NR, g // NR)
                    if project:
                        evacuate(TILES - 1, (TILES - 1) % NR, (TILES - 1) // NR)
                        for g in (TILES - 2, TILES - 1):
                            exps(g, g % NR, 0)
                        for g in (TILES - 3, TILES - 2, TILES - 1):
                            store(g, g % NR, 0)
                    for s in range(NR):
                        act.wait_ge(w.out[s].sem, w.out[s].at(16 * len(stores) * tiles_of(s)))

            s_newton.end(POOL_STEPS * TILES * bool(project))
            s_guess.end(2 * TILES * bool(project))
            end_tiles(loads, stores, [w.hn, w.sum, w.mean, w.cen, w.sqr, w.ssq] + [w.std, w.rstd] * (not project)
                      + [w.ready] * bool(after or project) + [w.x] * bool(before)
                      + [w.pre] * bool(pool_first)
                      + [s_tr, s_trc, s_m1, s_t3, s_t3b, s_lin, s_leaky, s_ex] * bool(project), w)

        def plain_phase(loads, stores, compute, more=(), w=n_signals, ready=n_signals.ready):
            with nc.Block() as block:
                @block.sync
                def _(sp):
                    tile_loads(sp, loads, ready, w)

                @block.vector
                def _(dve):
                    def step(g, s, turn):
                        dve.wait_ge(w.in_[s].sem, w.in_[s].at(16 * len(loads) * (turn + 1)))
                        if not_first(turn):
                            dve.wait_ge(w.out[s].sem, w.out[s].at(16 * len(stores) * turn))
                        compute(dve, g, s)
                    ring_cycle(dve, TILES, NR, step)

                @block.scalar
                def _(act):
                    def step(g, s, turn):
                        act.wait_ge(ready.sem, ready.at(g + 1))
                        tile_stores(act, stores, g, s, w)
                    ring_cycle(act, TILES - 1, NR, step)
                    step(TILES - 1, (TILES - 1) % NR, (TILES - 1) // NR)
                    for s in range(NR):
                        act.wait_ge(w.out[s].sem, w.out[s].at(16 * len(stores) * tiles_of(s)))
            end_tiles(loads, stores, [ready, *more], w)

        def edges_of(s):
            return -(-(GROUPS - s) // R)

        q = GeneralSignals(signal)

        def edge_phase(name, gathers, by, target, width, make=None, mark=False, count=False):
            NG = len(gathers) * CH
            gwidth = max(c + w for _, _, c, w in gathers)

            with Memory(nc, name) as m:
                g_idx = m.ring("g_idx", R, [P, len(gathers), CH], i32)
                s_idx = m.ring("s_idx", R, [P, CH], i32)
                got = m.ring("got", R, [P, CH, gwidth])
                same = m.ring("same", R, [P, CH, GROUP])
                sums = m.ring("sums", R, [P, CH, width])
                rowb = m.ring("rowb", R, [P, GROUP])
                vals = m.ring("vals", R, [P, CH, width]) if make else got
                if mark:
                    junk = m.tile("junk", [P, CH, GROUP])
                    n_before = m.tile("n_before", [P, CH])
                    shift = m.tile("shift", [P, CH])
                if count:
                    hot_hi = m.ring("hot_hi", 2, [P, HI], fp16)
                    hot_lo = m.ring("hot_lo", 2, [P, P], fp16)
                    deg1, some, out1, rdeg, root, rroot = (m.tile(n, [P, HI]) for n in (
                        "deg1", "some", "out1", "rdeg", "root", "rroot"))
                if make == "mlp":
                    pairT = m.tile("pairT", [P, GROUP])
                    h1T = m.tile("h1T", [A, GROUP])
                    gate = m.tile("gate", [P, CH, D])
                if make == "attend":
                    lin, leaky, ex = (m.tile(n, [P, CH]) for n in ("lin", "leaky", "ex"))
                rows_used = q.vals if make else q.summed
                block = m.stack.enter_context(nc.Block())

                def cols(t, g):
                    return t[:, bass.ds(g * CH, CH)]

                def col(t, g, i):
                    return t[:, bass.ds(g * CH + i, 1)]

                @block.sync
                def _(sp):
                    def step(g, s, turn):
                        if not_first(turn):
                            sp.wait_ge(q.same.sem, q.same.at(g - R + 1))
                            if mark:
                                sp.wait_ge(q.snew.sem, q.snew.at(g - R + 1))
                        sp.dma_start(rowb[s][:, :], by.row.rearrange("(g e) -> g e", e=GROUP)[
                            bass.ds(g, 1), :].to_broadcast([P, GROUP])).then_inc(q.row[s].sem, 16)
                    ring_cycle(sp, GROUPS, R, step)

                @block.gpsimd
                def _(pool):
                    def gather(g, s, turn):
                        pool.wait_ge(q.gidx.sem, q.gidx.at(g + 1))
                        if not_first(turn):
                            pool.wait_ge(rows_used.sem, rows_used.at(g - R + 1))
                            if make == "mlp":
                                pool.wait_ge(q.tr.sem, q.tr.at(g - R + 1))
                        passed(pool, g)
                        for k, (ends, tab, c, w) in enumerate(gathers):
                            for i in range(CH):
                                pool.indirect_dma_start(got[s][:, i, c:c + w], None, tab,
                                                        bass.IndirectOffsetOnAxis(ap=g_idx[s][:, k, i:i + 1], axis=0)
                                                        ).then_inc(q.got[s].sem, 16)

                    def scatter(g, s, turn):
                        pool.wait_ge(q.sidx.sem, q.sidx.at(g + 1))
                        pool.wait_ge(q.sums.sem, q.sums.at(g + 1))
                        if not_zero(g):
                            pool.wait_ge(q.scat.sem, q.scat.at(16 * CH * g))
                        passed(pool, g)
                        for i in range(CH):
                            pool.indirect_dma_start(target, bass.IndirectOffsetOnAxis(ap=s_idx[s][:, i:i + 1], axis=0),
                                                    sums[s][:, i, :], None, compute_op=ALU.add
                                                    ).then_inc(q.scat.sem, 16)

                    def step(g, s, turn):
                        ahead = s + AHEAD
                        if not isinstance(g, int) or g + AHEAD < GROUPS:
                            gather(g + AHEAD, ahead % R, turn + ahead // R)
                        scatter(g, s, turn)
                    for g in range(AHEAD):
                        gather(g, g, 0)
                    turns = (GROUPS - AHEAD) // R
                    for g in range(R):
                        step(g, g, 0)
                    with pool.Fori(1, turns) as turn:
                        for s in range(R):
                            step(turn * R + s, s, turn)
                    for g in range(turns * R, GROUPS):
                        step(g, g % R, g // R)
                    pool.wait_ge(q.scat.sem, q.scat.at(16 * CH * GROUPS))

                @block.vector
                def _(dve):
                    def gather_index(g, s, turn):
                        if not_first(turn):
                            dve.wait_ge(q.got[s].sem, q.got[s].at(16 * NG * turn))
                        for k, (ends, _, _, _) in enumerate(gathers):
                            last = dve.tensor_scalar(g_idx[s][:, k, :], cols(ends.gather, g), 0.0, None, ALU.add)
                        last.then_inc(q.gidx.sem, 1)

                    def equal_ends(g, s, turn):
                        dve.wait_ge(q.row[s].sem, q.row[s].at(16 * (turn + 1)))
                        if not_first(turn):
                            dve.wait_ge(q.summed.sem, q.summed.at(g - R + 1))
                        for i in range(CH):
                            last = dve.tensor_scalar(same[s][:, i, :], rowb[s][:, :], col(by.col, g, i), None,
                                                     ALU.is_equal)
                        last.then_inc(q.same.sem, 1)

                    def scatter_index(g, s, turn):
                        if mark:
                            for i in range(CH):
                                last = dve.scalar_tensor_tensor(junk[:, i, :], rowb[s][:, :], col(by.col, g, i),
                                                                earlier[:, i, :], ALU.is_equal, ALU.mult,
                                                                accum_out=n_before[:, i:i + 1])
                            last.then_inc(q.before.sem, 1)
                            dve.wait_ge(q.before.sem, q.before.at(g + 1))
                            dve.scalar_tensor_tensor(shift[:, :], n_before[:, :], 1.0, cols(by.to_dump, g),
                                                     ALU.min, ALU.mult).then_inc(q.shift.sem, 1)
                            dve.wait_ge(q.shift.sem, q.shift.at(g + 1))
                            dve.tensor_tensor(cols(by.scatter, g), cols(by.col, g), shift[:, :],
                                              ALU.add).then_inc(q.snew.sem, 1)
                            dve.wait_ge(q.snew.sem, q.snew.at(g + 1))
                        if not_first(turn):
                            dve.wait_ge(q.scat.sem, q.scat.at(16 * CH * (g - R + 1)))
                        dve.tensor_scalar(s_idx[s][:, :], cols(by.scatter, g), 0.0, None, ALU.add).then_inc(q.sidx.sem, 1)

                    def one_hots(g):
                        for i in range(CH):
                            for k, ends in enumerate((S, T)):
                                if not_zero(g) or i:
                                    dve.wait_ge(q.cnt.sem, q.cnt.at(2 * CH * g + 2 * i + k - 1))
                                dve.tensor_scalar(hot_lo[k][:, :], iota_lo[:, :], col(ends.lo, g, i), None, ALU.is_equal)
                                dve.tensor_scalar(hot_hi[k][:, :], iota_hi[:, :], col(ends.hi, g, i), None,
                                                  ALU.is_equal).then_inc(q.hot.sem, 1)

                    def values(g, s, turn):
                        if not_first(turn):
                            dve.wait_ge(q.summed.sem, q.summed.at(g - R + 1))
                        if make == "mlp":
                            dve.wait_ge(q.gate.sem, q.gate.at(g + 1))
                            inter = psum[:, 2, :].rearrange("p (c w) -> p c w", c=CH)[:, :, 0:D]
                            dve.tensor_tensor(vals[s][:, :, :], inter, gate[:, :, :], ALU.mult).then_inc(q.vals.sem, 1)
                        if make == "attend":
                            dve.wait_ge(q.got[s].sem, q.got[s].at(16 * NG * (turn + 1)))
                            dve.tensor_tensor(lin[:, :].unsqueeze(2), got[s][:, :, D:A], got[s][:, :, A:A + 1],
                                              ALU.add).then_inc(q.lin.sem, 1)
                            dve.wait_ge(q.lin.sem, q.lin.at(g + 1))
                            dve.scalar_tensor_tensor(leaky[:, :], lin[:, :], SLOPE, lin[:, :],
                                                     ALU.mult, ALU.max).then_inc(q.leaky.sem, 1)
                            dve.wait_ge(q.ex.sem, q.ex.at(g + 1))
                            dve.tensor_tensor(vals[s][:, :, 0:D], got[s][:, :, 0:D],
                                              ex[:, :].unsqueeze(2).to_broadcast([P, CH, D]), ALU.mult)
                            dve.tensor_copy(vals[s][:, :, D:A], ex[:, :].unsqueeze(2)).then_inc(q.vals.sem, 1)

                    def step(g, s, turn):
                        ahead = s + IDX_AHEAD
                        if not isinstance(g, int) or g + IDX_AHEAD < GROUPS:
                            gather_index(g + IDX_AHEAD, ahead % R, turn + ahead // R)
                        equal_ends(g, s, turn)
                        scatter_index(g, s, turn)
                        if count:
                            one_hots(g)
                        if make:
                            values(g, s, turn)
                    if make == "mlp":
                        dve.memset(h1T[D:A, :], 1.0).then_inc(q.ones.sem, 1)
                    for g in range(IDX_AHEAD):
                        gather_index(g, g, 0)
                    turns = (GROUPS - IDX_AHEAD) // R
                    for g in range(R):
                        step(g, g, 0)
                    with dve.Fori(1, turns) as turn:
                        for s in range(R):
                            step(turn * R + s, s, turn)
                    for g in range(turns * R, GROUPS):
                        step(g, g % R, g // R)
                    if count:
                        dve.wait_ge(q.cnt.sem, q.cnt.at(2 * CH * GROUPS))
                        dve.tensor_scalar(out1[:, :], counts_out[:, 0:HI], 1.0, None, ALU.max)
                        dve.tensor_scalar(some[:, :], counts_in[:, 0:HI], 1.0, None, ALU.min)
                        dve.tensor_scalar(deg1[:, :], counts_in[:, 0:HI], 1.0, None, ALU.max).then_inc(q.lin.sem, 1)
                        dve.wait_ge(q.lin.sem, q.lin.at(1))
                        dve.reciprocal(rcnt[:, :], out1[:, :])
                        dve.reciprocal(rdeg[:, :], deg1[:, :])
                        dve.wait_ge(q.ex.sem, q.ex.at(1))
                        dve.reciprocal(rroot[:, :], root[:, :]).then_inc(q.lin.sem, 1)
                        dve.wait_ge(q.lin.sem, q.lin.at(2))
                        dve.tensor_tensor(dinv[:, :], rroot[:, :], some[:, :], ALU.mult)
                        dve.tensor_tensor(dinv2[:, :], rdeg[:, :], some[:, :], ALU.mult)

                @block.tensor
                def _(pe):
                    def mlp(g, s, turn):
                        pe.wait_ge(q.got[s].sem, q.got[s].at(16 * NG * (turn + 1)))
                        if not_zero(g):
                            pe.wait_ge(q.trc.sem, q.trc.at(g))
                        for i in range(CH):
                            last = pe.transpose(psum[:, 0, i * P:(i + 1) * P], got[s][:, i, :], ident[:, :])
                        last.then_inc(q.tr.sem, 1)
                        pe.wait_ge(q.trc.sem, q.trc.at(g + 1))
                        if not_zero(g):
                            pe.wait_ge(q.m1c.sem, q.m1c.at(g))
                        pe.matmul(psum[0:D, 1, :], w1_sb[:, :], pairT[:, :], start=True, stop=True).then_inc(q.m1.sem, 1)
                        pe.wait_ge(q.m1c.sem, q.m1c.at(g + 1))
                        if not not_zero(g):
                            pe.wait_ge(q.ones.sem, q.ones.at(1))
                        if not_zero(g):
                            pe.wait_ge(q.vals.sem, q.vals.at(g))
                        for i in range(CH):
                            last = pe.matmul(psum[:, 2, i * P:(i + 1) * P], h1T[:, i * P:(i + 1) * P], w2_sb[:, :],
                                             start=True, stop=True)
                        last.then_inc(q.m2.sem, 1)

                    def count_chunks(g):
                        for i in range(CH):
                            for k, counts in enumerate((counts_out, counts_in)):
                                pe.wait_ge(q.hot.sem, q.hot.at(2 * CH * g + 2 * i + k + 1))
                                first = not not_zero(g) and i == 0
                                end = isinstance(g, int) and g == GROUPS - 1 and i == CH - 1
                                pe.matmul(counts[:, 0:512], hot_lo[k][:, :], hot_hi[k][:, 0:512], start=first, stop=end)
                                pe.matmul(counts[:, 512:HI], hot_lo[k][:, :], hot_hi[k][:, 512:HI],
                                          start=first, stop=end).then_inc(q.cnt.sem, 1)

                    def step(g, s, turn):
                        if make == "mlp":
                            mlp(g, s, turn)
                        if count:
                            count_chunks(g)
                        if make:
                            pe.wait_ge(q.vals.sem, q.vals.at(g + 1))
                        else:
                            pe.wait_ge(q.got[s].sem, q.got[s].at(16 * NG * (turn + 1)))
                        pe.wait_ge(q.same.sem, q.same.at(g + 1))
                        if not_zero(g):
                            pe.wait_ge(q.sums.sem, q.sums.at(g))
                        for j in range(CH):
                            for i in range(CH):
                                last = pe.matmul(psum[:, 3, j * width:(j + 1) * width],
                                                 same[s][:, i, j * LANES:(j + 1) * LANES], vals[s][:, i, 0:width],
                                                 start=i == 0, stop=i == CH - 1)
                        last.then_inc(q.summed.sem, 1)
                    ring_cycle(pe, GROUPS, R, step)

                @block.scalar
                def _(act):
                    def step(g, s, turn):
                        if make == "mlp":
                            act.wait_ge(q.tr.sem, q.tr.at(g + 1))
                            if not_zero(g):
                                act.wait_ge(q.m1.sem, q.m1.at(g))
                            act.copy(pairT[:, :], psum[:, 0, :]).then_inc(q.trc.sem, 1)
                            act.wait_ge(q.m1.sem, q.m1.at(g + 1))
                            if not_zero(g):
                                act.wait_ge(q.m2.sem, q.m2.at(g))
                            act.activation(h1T[0:D, :], psum[0:D, 1, :], ACT.Relu, bias=b1_sb[:, :]).then_inc(q.m1c.sem, 1)
                            act.wait_ge(q.m2.sem, q.m2.at(g + 1))
                            if not_zero(g):
                                act.wait_ge(q.vals.sem, q.vals.at(g))
                            pre = psum[:, 2, :].rearrange("p (c w) -> p c w", c=CH)[:, :, D:2 * D]
                            act.activation(gate[:, :, :], pre, ACT.Sigmoid).then_inc(q.gate.sem, 1)
                        if make == "attend":
                            act.wait_ge(q.leaky.sem, q.leaky.at(g + 1))
                            if not_zero(g):
                                act.wait_ge(q.vals.sem, q.vals.at(g))
                            act.activation(ex[:, :], leaky[:, :], ACT.Exp).then_inc(q.ex.sem, 1)
                        act.wait_ge(q.summed.sem, q.summed.at(g + 1))
                        if not_first(turn):
                            act.wait_ge(q.scat.sem, q.scat.at(16 * CH * (g - R + 1)))
                        act.copy(sums[s][:, :, :].rearrange("p c w -> p (c w)"),
                                 psum[:, 3, 0:CH * width]).then_inc(q.sums.sem, 1)
                    ring_cycle(act, GROUPS, R, step)
                    if count:
                        act.wait_ge(q.lin.sem, q.lin.at(1))
                        act.activation(root[:, :], deg1[:, :], ACT.Sqrt).then_inc(q.ex.sem, 1)
            for s in range(R):
                q.row[s].end(16 * edges_of(s))
                q.got[s].end(16 * NG * edges_of(s))
            q.scat.end(16 * CH * GROUPS)
            for sig in ([q.gidx, q.sidx, q.same, q.summed, q.sums] + [q.before, q.shift, q.snew] * bool(mark)
                        + [q.vals] * bool(make) + [q.tr, q.trc, q.m1, q.m1c, q.m2, q.gate] * (make == "mlp")
                        + [q.lin, q.leaky, q.ex] * (make == "attend")):
                sig.end(GROUPS)
            if count:
                q.hot.end(2 * CH * GROUPS)
                q.cnt.end(2 * CH * GROUPS)
                q.lin.end(2)
                q.ex.end(1)
            if make == "mlp":
                q.ones.end(1)

        f = FastSignals(signal, f_norm)
        BATCHES = [(0, CH), (CH, WC)]
        BANKS = 2
        PER_BANK = J // BANKS
        FIRST_BEHIND = 3
        CENTRE_BEHIND = 5

        def tile_phase(name, ends, gathers, width, stores_of=None, make=None, add=None, y_of=False, norm_of=None):
            w = f_norm
            NG = len(gathers) * WC
            gwidth = max(c + w for _, _, c, w in gathers)
            mlp = make == "mlp"
            nbuf = 2
            lag = 2
            vw = A if mlp else width

            with Memory(nc, name) as m:
                g_idx = m.ring("g_idx", WR, [P, len(gathers), WC], i32)
                got = m.ring("got", WR, [P, WC, gwidth])
                hots = 2 if norm_of else WR
                hot = m.ring("hot", hots, [P, WC, J, P], bf16)
                pieces = m.ring("pieces", WR, [P, WC, 3, vw], bf16)
                rest = m.ring("rest", WR, [P, WC, vw])
                sums = m.ring("sums", WR, [P, J * width]) if add is None else None
                vals = m.ring("vals", WR, [P, WC, vw]) if make else got
                if add is not None:
                    basis = m.ring("basis", WR, [P, J * width])
                    total = m.ring("total", WR, [P, J * width])
                if y_of:
                    y = m.ring("y", WR, [P, J * D])
                if mlp:
                    pairT = m.tile("pairT", [P, WIN])
                    h1T = m.tile("h1T", [A, WIN])
                    gate = m.ring("gate", 2, [P, CH, D])
                    wide = [psum[:, 4, :], psum[:, 6, :]]
                    edges_out1, rout = (m.ring(n, 2, [P, J]) for n in ("edges_out1", "rout"))
                if make == "attend":
                    lin, leaky, ex = (m.tile(n, [P, WC]) for n in ("lin", "leaky", "ex"))
                    q_row = m.ring("q_row", 2, [P, WIN], fp16)
                    hot_q = m.ring("hot_q", 2, [P, WIN], bf16)
                    hot_j = m.tile("hot_j", [P, WC, J])
                    masked = m.tile("masked", [P, WC, 3, J])
                    own_a, other_a = (m.tile(n, [P, WC]) for n in ("own_a", "other_a"))
                    as_rest = m.tile("as_rest", [P, HI])
                    as_pieces = m.tile("as_pieces", [P, TILES, 3, J], bf16)
                if norm_of:
                    norm = norm_of(m, sums, rout if mlp else None)
                    sq = lag + 1 + bool(norm.pool_first)
                    cen = m.ring("cen", WR, [P, J * D])
                    sqr = m.ring("sqr", 2, [P, J * D])
                    rowsum, mean, sumsq, std, rstd = (m.ring(n, WR, [P, J]) for n in (
                        "rowsum", "mean", "sumsq", "std", "rstd"))
                    stores = []
                else:
                    stores = stores_of(total if add is not None else sums, y if y_of else None)
                rows_used, per_tile = {None: (f.rest, 1), "mlp": (f.tr, 2), "attend": (f.vals, 1)}[make]
                peeled = 2 if norm_of else 1
                block = m.stack.enter_context(nc.Block())

                def bank_of(s, b):
                    return (s % nbuf) * BANKS + b

                @block.sync
                def _(sp):
                    def step(g, s, turn):
                        if not_first(turn):
                            sp.wait_ge(f.fin.sem, f.fin.at(g - WR + 1))
                        sp.dma_start(basis[s][:, :], table_tile(add, g)).then_inc(f.base[s].sem, 16)
                        if make == "attend" and (not isinstance(turn, int) or g + 1 < TILES):
                            q_load(g + 1, (s + 1) % 2)

                    def q_load(g, s):
                        if not (isinstance(g, int) and g < 2):
                            sp.wait_ge(f.hot_q.sem, f.hot_q.at(g - 1))
                        sp.dma_start(q_row[s][:, :], src_q.rearrange("(t e) -> t e", e=WIN)[
                            bass.ds(g, 1), :].to_broadcast([P, WIN])).then_inc(f.q_row[s].sem, 16)
                    if make == "attend":
                        q_load(0, 0)
                    if add is not None:
                        ring_cycle(sp, TILES, WR, step)
                    if norm_of:
                        tile_loads(sp, norm.loads, w.x, w, WR)

                @block.gpsimd
                def _(pool):
                    def gather(g, s, turn):
                        pool.wait_ge(f.gidx.sem, f.gidx.at(g + 1))
                        if not_first(turn):
                            pool.wait_ge(rows_used.sem, rows_used.at(per_tile * (g - WR + 1)))
                        passed(pool, g)
                        for k, (_, tab, c, w) in enumerate(gathers):
                            for i in range(WC):
                                pool.indirect_dma_start(got[s][:, i, c:c + w], None, tab,
                                                        bass.IndirectOffsetOnAxis(ap=g_idx[s][:, k, i:i + 1], axis=0)
                                                        ).then_inc(f.got[s].sem, 16)

                    def first_part(g, s, turn):
                        pool.wait_ge(w.in_[s].sem, w.in_[s].at(16 * len(norm.loads) * (turn + 1)))
                        if not_first(turn):
                            pool.wait_ge(w.x.sem, w.x.at(g - WR + 1))
                        norm.pool_first(pool, g, s)

                    def centre(g, s, turn):
                        pool.wait_ge(w.mean.sem, w.mean.at(g + 1))
                        if not_first(turn):
                            pool.wait_ge(w.hn.sem, w.hn.at(g - WR + 1))
                        pool.tensor_tensor(rows3(cen[s]), rows3(norm.x[s]), bc(mean[s][:, :]),
                                           ALU.add).then_inc(w.cen.sem, 1)

                    def behind(part, g, s, turn, n):
                        if not isinstance(turn, int) or g >= n:
                            part(g - n, (s - n) % WR, turn + (s - n) // WR)

                    def step(g, s, turn):
                        gather(g, s, turn)
                        if norm_of and norm.pool_first:
                            behind(first_part, g, s, turn, FIRST_BEHIND)
                            behind(centre, g, s, turn, CENTRE_BEHIND)
                    ring_cycle(pool, TILES, WR, step, peeled)
                    if norm_of and norm.pool_first:
                        for g in range(TILES - CENTRE_BEHIND, TILES):
                            if g >= TILES - FIRST_BEHIND:
                                first_part(g, g % WR, g // WR)
                            centre(g, g % WR, g // WR)

                @block.vector
                def _(dve):
                    def gather_index(g, s, turn):
                        if not_first(turn):
                            dve.wait_ge(f.got[s].sem, f.got[s].at(16 * NG * turn))
                        for k, (which, _, _, _) in enumerate(gathers):
                            last = dve.tensor_scalar(g_idx[s][:, k, :], which[:, bass.ds(g * WC, WC)], 0.0, None, ALU.add)
                        last.then_inc(f.gidx.sem, 1)

                    def one_hot(g, s, turn):
                        if not (isinstance(g, int) and g < hots):
                            dve.wait_ge(f.acc.sem, f.acc.at(BANKS * (g - hots + 1)))
                        for c in range(WC):
                            last = dve.tensor_scalar(hot[s % hots][:, c, :, :].rearrange("p j q -> p (j q)"),
                                                     iota_jp[:, :, :].rearrange("p j q -> p (j q)"),
                                                     ends.rel[:, bass.ds(g * WC + c, 1)], None, ALU.is_equal)
                        last.then_inc(f.hot.sem, 1)

                    def values(g, s, turn):
                        if mlp:
                            for n, (c0, c1) in enumerate(BATCHES):
                                dve.wait_ge(f.gate.sem, f.gate.at(2 * g + n + 1))
                                inter = wide[n][:, 0:(c1 - c0) * P].rearrange("p (c w) -> p c w", w=P)[:, :, 0:D]
                                dve.tensor_tensor(vals[s][:, c0:c1, 0:D], inter, gate[n][:, 0:c1 - c0, :],
                                                  ALU.mult).then_inc(f.vals.sem, 1)
                        if make == "attend":
                            dve.tensor_tensor(hot_j[:, :, :], iota_lo[:, 0:J].unsqueeze(1).to_broadcast([P, WC, J]),
                                              src_j[:, bass.ds(g * WC, WC)].unsqueeze(2).to_broadcast([P, WC, J]),
                                              ALU.is_equal).then_inc(f.hot_j.sem, 1)
                            dve.wait_ge(f.hot_j.sem, f.hot_j.at(g + 1))
                            dve.wait_ge(f.picked.sem, f.picked.at(g + 1))
                            dve.tensor_tensor(masked[:, :, :, :], psum[:, 4 + s % 2, 0:WC * 3 * J].rearrange(
                                "p (c k j) -> p c k j", k=3, j=J), hot_j[:, :, :].unsqueeze(2).to_broadcast(
                                [P, WC, 3, J]), ALU.mult).then_inc(f.masked.sem, 1)
                            dve.wait_ge(f.got[s].sem, f.got[s].at(16 * NG * (turn + 1)))
                            dve.tensor_tensor(other_a[:, :].unsqueeze(2), got[s][:, :, D:A],
                                              src_inside[:, bass.ds(g * WC, WC)].unsqueeze(2), ALU.mult)
                            dve.wait_ge(f.masked.sem, f.masked.at(g + 1))
                            dve.tensor_reduce(own_a[:, :].unsqueeze(2), masked[:, :, :, :].rearrange(
                                "p c k j -> p c (k j)"), AX_X, ALU.add).then_inc(f.own_a.sem, 1)
                            dve.wait_ge(f.own_a.sem, f.own_a.at(g + 1))
                            dve.tensor_tensor(lin[:, :], other_a[:, :], own_a[:, :], ALU.add).then_inc(f.lin.sem, 1)
                            dve.wait_ge(f.lin.sem, f.lin.at(g + 1))
                            dve.scalar_tensor_tensor(leaky[:, :], lin[:, :], SLOPE, lin[:, :],
                                                     ALU.mult, ALU.max).then_inc(f.leaky.sem, 1)
                            dve.wait_ge(f.ex.sem, f.ex.at(g + 1))
                            dve.tensor_tensor(vals[s][:, :, 0:D], got[s][:, :, 0:D],
                                              ex[:, :].unsqueeze(2).to_broadcast([P, WC, D]), ALU.mult)
                            dve.tensor_copy(vals[s][:, :, D:A], ex[:, :].unsqueeze(2)).then_inc(f.vals.sem, 1)

                    def one_hot_q(g, s, turn):
                        dve.wait_ge(f.q_row[s % 2].sem, f.q_row[s % 2].at(16 * (WR // 2 * turn + s // 2 + 1)))
                        if not (isinstance(g, int) and g < 2):
                            dve.wait_ge(f.picked.sem, f.picked.at(g - 1))
                        dve.tensor_scalar(hot_q[s % 2][:, :], q_row[s % 2][:, :], part[:, :], None,
                                          ALU.is_equal).then_inc(f.hot_q.sem, 1)

                    def split_a():
                        piece = [as_pieces[:, :, k, :] for k in range(3)]
                        whole = as_all[:, :].rearrange("p (t j) -> p t j", j=J)
                        left = as_rest[:, :].rearrange("p (t j) -> p t j", j=J)
                        dve.tensor_copy(piece[0], whole).then_inc(f.ones.sem, 1)
                        dve.wait_ge(f.ones.sem, f.ones.at(1))
                        dve.tensor_tensor(left, whole, piece[0], ALU.subtract).then_inc(f.ones.sem, 1)
                        dve.wait_ge(f.ones.sem, f.ones.at(2))
                        dve.tensor_copy(piece[1], left).then_inc(f.ones.sem, 1)
                        dve.wait_ge(f.ones.sem, f.ones.at(3))
                        dve.tensor_tensor(piece[2], left, piece[1], ALU.subtract).then_inc(f.ones.sem, 1)

                    def split(g, s, turn):
                        dve.wait_ge(f.high.sem, f.high.at(g + 1))
                        dve.tensor_tensor(rest[s][:, :, :], vals[s][:, :, 0:vw], pieces[s][:, :, 0, :],
                                          ALU.subtract).then_inc(f.rest.sem, 1)

                    def lowest(g, s, turn):
                        dve.wait_ge(f.mid.sem, f.mid.at(g + 1))
                        dve.tensor_tensor(pieces[s][:, :, 2, :], rest[s][:, :, :], pieces[s][:, :, 1, :],
                                          ALU.subtract).then_inc(f.pieces.sem, 1)

                    def finish(g, s, turn):
                        if stores and not_first(turn):
                            dve.wait_ge(f.out[s].sem, f.out[s].at(16 * len(stores) * turn))
                        for b in range(BANKS):
                            dve.wait_ge(f.acc.sem, f.acc.at(BANKS * g + b + 1))
                            js = slice(b * PER_BANK, (b + 1) * PER_BANK)
                            here = psum[:, bank_of(s, b), 0:PER_BANK * vw].rearrange("p (j w) -> p j w", w=vw)
                            if mlp:
                                dve.tensor_scalar(edges_out1[s % 2][:, js].unsqueeze(2), here[:, :, D:A], 1.0, None,
                                                  ALU.max)
                            if add is not None:
                                if b == 0:
                                    dve.wait_ge(f.base[s].sem, f.base[s].at(16 * (turn + 1)))
                                last = dve.tensor_tensor(rows3(total[s], width)[:, js, :], here[:, :, 0:width],
                                                         rows3(basis[s], width)[:, js, :], ALU.add)
                            else:
                                last = dve.tensor_scalar(rows3(sums[s], width)[:, js, :], here[:, :, 0:width], 0.0, None,
                                                         ALU.add)
                            last.then_inc(f.red.sem, 1)
                        dve.wait_ge(f.red.sem, f.red.at(BANKS * (g + 1)))
                        if mlp:
                            dve.reciprocal(rout[s % 2][:, :], edges_out1[s % 2][:, :]).then_inc(f.leaky.sem, 1)
                            dve.wait_ge(f.leaky.sem, f.leaky.at(g + 1))
                        elif y_of:
                            dve.tensor_tensor(rows3(y[s]), rows3(sums[s]), bc(dinv2[:, bass.ds(g * J, J)]),
                                              ALU.mult).then_inc(f.fin.sem, 1)
                        elif not norm_of:
                            dve.sem_inc(f.fin.sem, 1)

                    def centre(g, s, turn):
                        dve.wait_ge(w.in_[s].sem, w.in_[s].at(16 * len(norm.loads) * (turn + 1)))
                        if norm.stored_x and not_first(turn):
                            dve.wait_ge(w.out[s].sem, w.out[s].at(16 * len(norm.stores) * turn))
                        norm.new_x(dve, g, s)
                        dve.wait_ge(w.x.sem, w.x.at(g + 1))
                        dve.tensor_reduce(rowsum[s][:, :], rows3(norm.x[s]), AX_X, ALU.add).then_inc(w.sum.sem, 1)
                        dve.wait_ge(w.sum.sem, w.sum.at(g + 1))
                        dve.tensor_scalar(mean[s][:, :], rowsum[s][:, :], -1.0 / D, None,
                                          ALU.mult).then_inc(w.mean.sem, 1)
                        if not norm.pool_first:
                            dve.wait_ge(w.mean.sem, w.mean.at(g + 1))
                            dve.tensor_tensor(rows3(cen[s]), rows3(norm.x[s]), bc(mean[s][:, :]),
                                              ALU.add).then_inc(w.cen.sem, 1)

                    def squares_sum(g, s, turn):
                        dve.wait_ge(w.sqr.sem, w.sqr.at(g + 1))
                        dve.tensor_reduce(sumsq[s][:, :], rows3(sqr[s % 2]), AX_X, ALU.add).then_inc(w.ssq.sem, 1)

                    def normalise(g, s, turn):
                        dve.wait_ge(w.std.sem, w.std.at(g + 1))
                        dve.reciprocal(rstd[s][:, :], std[s][:, :]).then_inc(w.rstd.sem, 1)
                        dve.wait_ge(w.rstd.sem, w.rstd.at(g + 1))
                        if not_first(turn):
                            dve.wait_ge(w.out[s].sem, w.out[s].at(16 * len(norm.stores) * turn))
                        dve.scalar_tensor_tensor(rows3(norm.h[s]), rows3(cen[s]), 0.0, bc(rstd[s][:, :]),
                                                 ALU.max, ALU.mult).then_inc(w.hn.sem, 1)
                        if norm.after:
                            dve.wait_ge(w.hn.sem, w.hn.at(g + 1))
                            norm.after(dve, g, s)

                    def behind(part, g, s, turn, n):
                        if not isinstance(turn, int) or g >= n:
                            part(g - n, (s - n) % WR, turn + (s - n) // WR)

                    def step(g, s, turn):
                        ahead = s + IDX_AHEAD
                        if not isinstance(turn, int) or g + IDX_AHEAD < TILES:
                            gather_index(g + IDX_AHEAD, ahead % WR, turn + ahead // WR)
                        one_hot(g, s, turn)
                        if make == "attend" and (not isinstance(turn, int) or g + 1 < TILES):
                            one_hot_q(g + 1, (s + 1) % WR, turn + (s + 1) // WR)
                        if norm_of:
                            behind(squares_sum, g, s, turn, sq)
                            behind(normalise, g, s, turn, sq + 1)
                        values(g, s, turn)
                        split(g, s, turn)
                        behind(finish, g, s, turn, lag)
                        lowest(g, s, turn)
                        if norm_of:
                            behind(centre, g, s, turn, lag)

                    if mlp:
                        dve.memset(h1T[D:A, :], 1.0)
                        for s in range(WR):
                            last = dve.memset(vals[s][:, :, D:A], 1.0)
                        last.then_inc(f.ones.sem, 1)
                    for g in range(IDX_AHEAD):
                        gather_index(g, g, 0)
                    if make == "attend":
                        split_a()
                        one_hot_q(0, 0, 0)
                    for g in range(peeled * WR):
                        step(g, g % WR, g // WR)
                    turns = (TILES - IDX_AHEAD) // WR
                    with dve.Fori(peeled, turns) as turn:
                        for s in range(WR):
                            step(turn * WR + s, s, turn)
                    for g in range(turns * WR, TILES):
                        step(g, g % WR, g // WR)
                    for g in range(TILES - lag, TILES):
                        finish(g, g % WR, g // WR)
                    if norm_of:
                        for g in range(TILES - sq - 1, TILES):
                            if g >= TILES - lag:
                                centre(g, g % WR, g // WR)
                            if g >= TILES - sq:
                                squares_sum(g, g % WR, g // WR)
                            normalise(g, g % WR, g // WR)

                @block.tensor
                def _(pe):
                    def accumulate(g, s, turn, b):
                        if b == 0:
                            pe.wait_ge(f.hot.sem, f.hot.at(g + 1))
                            pe.wait_ge(f.pieces.sem, f.pieces.at(g + 1))
                        if not (isinstance(g, int) and g < nbuf):
                            pe.wait_ge(f.red.sem, f.red.at(BANKS * (g - nbuf) + b + 1))
                        for j in range(b * PER_BANK, (b + 1) * PER_BANK):
                            o = (j % PER_BANK) * vw
                            for c in range(WC):
                                for k in range(3):
                                    last = pe.matmul(psum[:, bank_of(s, b), o:o + vw], hot[s % hots][:, c, j, :],
                                                     pieces[s][:, c, k, :], start=c == 0 and k == 0,
                                                     stop=c == WC - 1 and k == 2)
                        last.then_inc(f.acc.sem, 1)

                    def transposes(g, s, turn, n):
                        c0, c1 = BATCHES[n]
                        if n == 0:
                            pe.wait_ge(f.got[s].sem, f.got[s].at(16 * NG * (turn + 1)))
                        if not_zero(g):
                            pe.wait_ge(f.vals.sem, f.vals.at(2 * g + n - 1))
                        for c in range(c0, c1):
                            last = pe.transpose(wide[n][:, (c - c0) * P:(c - c0 + 1) * P], got[s][:, c, :], ident[:, :])
                        last.then_inc(f.tr.sem, 1)

                    def first_product(g, n):
                        c0, c1 = BATCHES[n]
                        pe.wait_ge(f.trc.sem, f.trc.at(2 * g + n + 1))
                        if not_zero(g):
                            pe.wait_ge(f.m1c.sem, f.m1c.at(2 * g + n - 1))
                        pe.matmul(psum[0:D, 5 + 2 * n, 0:(c1 - c0) * P], w1_sb[:, :], pairT[:, c0 * P:c1 * P], start=True,
                                  stop=True).then_inc(f.m1.sem, 1)

                    def second_products(g, n):
                        c0, c1 = BATCHES[n]
                        pe.wait_ge(f.m1c.sem, f.m1c.at(2 * g + n + 1))
                        if not not_zero(g) and n == 0:
                            pe.wait_ge(f.ones.sem, f.ones.at(1))
                        for c in range(c0, c1):
                            last = pe.matmul(wide[n][:, (c - c0) * P:(c - c0 + 1) * P], h1T[:, c * P:(c + 1) * P], w2_sb[:, :],
                                             start=True, stop=True)
                        last.then_inc(f.m2.sem, 1)

                    def mlp_step(g, s, turn):
                        before = lambda b: ((not isinstance(turn, int) or g >= 1) and
                                            accumulate(g - 1, (s - 1) % WR, None, b))
                        transposes(g, s, turn, 0)
                        transposes(g, s, turn, 1)
                        first_product(g, 0)
                        first_product(g, 1)
                        second_products(g, 0)
                        second_products(g, 1)
                        before(0)
                        before(1)

                    def pick(g, s):
                        pe.wait_ge(f.hot_q.sem, f.hot_q.at(g + 1))
                        if not (isinstance(g, int) and g < 2):
                            pe.wait_ge(f.masked.sem, f.masked.at(g - 1))
                        for c in range(WC):
                            last = pe.matmul(psum[:, 4 + s % 2, c * 3 * J:(c + 1) * 3 * J],
                                             hot_q[s % 2][:, :].rearrange("q (p c) -> q c p", c=WC)[:, c, :],
                                             as_pieces[:, bass.ds(g, 1), :, :].rearrange("q t k j -> q (t k j)"),
                                             start=True, stop=True)
                        last.then_inc(f.picked.sem, 1)

                    def sum_step(g, s, turn):
                        if make == "attend" and (not isinstance(turn, int) or g + 1 < TILES):
                            pick(g + 1, (s + 1) % WR)
                        for b in range(BANKS):
                            accumulate(g, s, turn, b)
                    if make == "attend":
                        pe.wait_ge(f.ones.sem, f.ones.at(4))
                        pick(0, 0)
                    ring_cycle(pe, TILES, WR, mlp_step if mlp else sum_step)
                    if mlp:
                        sum_step(TILES - 1, (TILES - 1) % WR, None)

                @block.scalar
                def _(act):
                    def store(g, s):
                        act.wait_ge(f.fin.sem, f.fin.at(g + 1))
                        for tab, ring in stores:
                            act.dma_start(table_tile(tab, g), ring[s][:, :]).then_inc(f.out[s].sem, 16)

                    def square(g, s, turn):
                        act.wait_ge(w.cen.sem, w.cen.at(g + 1))
                        if not (isinstance(g, int) and g < 2):
                            act.wait_ge(w.ssq.sem, w.ssq.at(g - 1))
                        act.activation(sqr[s % 2][:, :], cen[s][:, :], ACT.Square).then_inc(w.sqr.sem, 1)

                    def root(g, s, turn):
                        act.wait_ge(w.ssq.sem, w.ssq.at(g + 1))
                        act.activation(std[s][:, :], sumsq[s][:, :], ACT.Sqrt, bias=eps[:, :],
                                       scale=1.0 / D).then_inc(w.std.sem, 1)

                    def norm_store(g, s, turn):
                        done = w.ready if norm.after else w.hn
                        act.wait_ge(done.sem, done.at(g + 1))
                        tile_stores(act, norm.stores, g, s, w)

                    def behind(part, g, s, turn, n):
                        if not isinstance(turn, int) or g >= n:
                            part(g - n, (s - n) % WR, turn + (s - n) // WR)

                    def step(g, s, turn):
                        if norm_of and not mlp:
                            behind(square, g, s, turn, sq)
                        if mlp:
                            for n, (c0, c1) in enumerate(BATCHES):
                                act.wait_ge(f.tr.sem, f.tr.at(2 * g + n + 1))
                                if not_zero(g):
                                    act.wait_ge(f.m1.sem, f.m1.at(2 * g + n - 1))
                                act.copy(pairT[:, c0 * P:c1 * P], wide[n][:, 0:(c1 - c0) * P]).then_inc(f.trc.sem, 1)
                            if norm_of:
                                behind(square, g, s, turn, sq)
                            for n, (c0, c1) in enumerate(BATCHES):
                                act.wait_ge(f.m1.sem, f.m1.at(2 * g + n + 1))
                                if not_zero(g):
                                    act.wait_ge(f.m2.sem, f.m2.at(2 * g + n - 1))
                                act.activation(h1T[0:D, c0 * P:c1 * P], psum[0:D, 5 + 2 * n, 0:(c1 - c0) * P], ACT.Relu,
                                               bias=b1_sb[:, :]).then_inc(f.m1c.sem, 1)
                            for n, (c0, c1) in enumerate(BATCHES):
                                act.wait_ge(f.m2.sem, f.m2.at(2 * g + n + 1))
                                if not_zero(g):
                                    act.wait_ge(f.vals.sem, f.vals.at(2 * g + n - 1))
                                pre = wide[n][:, 0:(c1 - c0) * P].rearrange("p (c w) -> p c w", w=P)[:, :, D:2 * D]
                                act.activation(gate[n][:, 0:c1 - c0, :], pre, ACT.Sigmoid).then_inc(f.gate.sem, 1)
                        if make == "attend":
                            act.wait_ge(f.leaky.sem, f.leaky.at(g + 1))
                            if not_zero(g):
                                act.wait_ge(f.vals.sem, f.vals.at(g))
                            act.activation(ex[:, :], leaky[:, :], ACT.Exp).then_inc(f.ex.sem, 1)
                        if make:
                            act.wait_ge(f.vals.sem, f.vals.at(per_vals * (g + 1)))
                        else:
                            act.wait_ge(f.got[s].sem, f.got[s].at(16 * NG * (turn + 1)))
                        if not_first(turn):
                            act.wait_ge(f.acc.sem, f.acc.at(BANKS * (g - WR + 1)))
                        act.copy(pieces[s][:, :, 0, :], vals[s][:, :, 0:vw]).then_inc(f.high.sem, 1)
                        act.wait_ge(f.rest.sem, f.rest.at(g + 1))
                        act.copy(pieces[s][:, :, 1, :], rest[s][:, :, :]).then_inc(f.mid.sem, 1)
                        if norm_of:
                            behind(root, g, s, turn, sq)
                            behind(norm_store, g, s, turn, sq + 1)
                        elif not isinstance(turn, int) or g >= lag:
                            store(g - lag, (s - lag) % WR)
                    per_vals = 2 if mlp else 1
                    ring_cycle(act, TILES, WR, step, peeled)
                    if norm_of:
                        for g in range(TILES - sq - 1, TILES):
                            if g >= TILES - sq:
                                square(g, g % WR, g // WR)
                                root(g, g % WR, g // WR)
                            norm_store(g, g % WR, g // WR)
                        for s in range(WR):
                            act.wait_ge(w.out[s].sem, w.out[s].at(16 * len(norm.stores) * tiles_of(s, WR)))
                    else:
                        for g in range(TILES - lag, TILES):
                            store(g, g % WR)
                        for s in range(WR):
                            act.wait_ge(f.out[s].sem, f.out[s].at(16 * len(stores) * tiles_of(s, WR)))

            for s in range(WR):
                turns = -(-(TILES - s) // WR)
                f.got[s].end(16 * NG * turns)
                f.out[s].end(16 * len(stores) * turns)
                f.base[s].end(16 * turns * (add is not None))
            for sig in ([f.gidx, f.hot, f.high, f.rest, f.mid, f.pieces] + [f.fin] * (not norm_of)
                        + [f.vals, f.lin, f.leaky, f.ex, f.hot_q, f.picked, f.hot_j, f.masked, f.own_a] * (make == "attend") + [f.leaky] * mlp
                        + [f.vals, f.tr, f.trc, f.m1, f.m1c, f.m2, f.gate] * 2 * mlp):
                sig.end(TILES)
            f.acc.end(BANKS * TILES)
            f.red.end(BANKS * TILES)
            for s in range(2):
                f.q_row[s].end(16 * (TILES // 2) * (make == "attend"))
            f.ones.end(1 if mlp else 4 if make == "attend" else 0)
            if norm_of:
                end_tiles(norm.loads, norm.stores, [w.x, w.sum, w.mean, w.cen, w.sqr, w.ssq, w.std, w.rstd, w.hn]
                          + [w.ready] * bool(norm.after) + norm.steps, w, WR)

        def degrees(t, g):
            return bc(t[:, bass.ds(g * J, J)])

        def either(fast, general):
            is_it = nc.values_load(is_fast[0:1, 0:1], min_val=0, max_val=1)
            shared = every_norm.each_tile()
            before = [sig.base for sig in shared]
            with nc.If(is_it > 0):
                fast()
            after_fast = [sig.base for sig in shared]
            for sig, count in zip(shared, before):
                sig.base = count
            with nc.Else():
                general()
            assert [sig.base for sig in shared] == after_fast

        with Memory(nc, "n0") as m:
            xt, hn = (m.ring(k, NR, [P, J * D]) for k in ("x", "h"))
            norm_phase(m, hn, [(x, xt)], [(h_tab, hn)], xt)

        def after_layer0(w, h, x1, x1h, y):
            def after(dve, g, s):
                dve.scalar_tensor_tensor(x1h[s][:, :], h[s][:, :], 1.0 / (HOPS + 1), x1[s][:, :], ALU.mult, ALU.add)
                dve.tensor_tensor(rows3(y[s]), rows3(h[s]), degrees(dinv, g), ALU.mult).then_inc(w.ready.sem, 1)
            return after

        def layer0_fast():
            def norm_of(m, sums, rout):
                xt, x1, h, x1h, y = (m.ring(k, WR, [P, J * D]) for k in ("x", "x1", "h", "x1h", "y"))
                scaled = m.ring("scaled", 2, [P, J * D])
                w = f_norm

                def new_x(dve, g, s):
                    dve.tensor_tensor(rows3(scaled[s % 2]), rows3(sums[s]), bc(rout[s % 2][:, :]),
                                      ALU.mult).then_inc(w.pre.sem, 1)
                    dve.wait_ge(w.pre.sem, w.pre.at(g + 1))
                    dve.tensor_tensor(x1[s][:, :], xt[s][:, :], scaled[s % 2][:, :], ALU.add).then_inc(w.x.sem, 1)
                return Norm([(x, xt)], [(x1_tab, x1h), (y_tab[0], y)], x1, h, new_x, after_layer0(w, h, x1, x1h, y),
                            steps=[w.pre])
            tile_phase("f0", S, [(S.own, h_tab, 0, D), (S.other, h_tab, D, D)], D, make="mlp", norm_of=norm_of)

        def layer0_general():
            with nc.Block() as block:
                @block.scalar
                def _(act):
                    n = sum(zero_table(act, tab, q.zero) for tab in (pool_tab, *hop_tab))
                    for tab in (x2_tab, att_tab):
                        act.dma_start(tab[NPAD:ROWS, :].rearrange("(p r) d -> p (r d)", r=4),
                                      zeros[0:(ROWS - NPAD) // 4, 0:4 * tab.shape[1]]).then_inc(q.zero.sem, 16)
                    act.wait_ge(q.zero.sem, q.zero.at(16 * (n + 2)))
            edge_phase("e0", [(S, h_tab, 0, D), (T, h_tab, D, D)], S, pool_tab, D, make="mlp", mark=True, count=True)
            with Memory(nc, "n1") as m:
                xt, pt, scaled, x1, h, x1h, y = (m.ring(k, NR, [P, J * D]) for k in (
                    "x", "p", "scaled", "x1", "h", "x1h", "y"))
                w = g_norm

                def pool_first(pool, g, s):
                    pool.tensor_tensor(rows3(scaled[s]), rows3(pt[s]), degrees(rcnt, g), ALU.mult).then_inc(w.pre.sem, 1)

                def before(dve, g, s):
                    dve.wait_ge(w.pre.sem, w.pre.at(g + 1))
                    dve.tensor_tensor(x1[s][:, :], xt[s][:, :], scaled[s][:, :], ALU.add).then_inc(w.x.sem, 1)
                norm_phase(m, h, [(x, xt), (pool_tab, pt)], [(x1_tab, x1h), (y_tab[0], y)], x1, before,
                           after_layer0(w, h, x1, x1h, y), pool_first, w=w)
        either(layer0_fast, layer0_general)

        def mixed_x(w, x1, h2, two, three, mixed, x2):
            def mix(dve, g, s):
                dve.tensor_tensor(three[s % 2][:, :], two[s][:, :], h2[s][:, :], ALU.add).then_inc(w.u.sem, 1)
                dve.wait_ge(w.u.sem, w.u.at(g + 1))
                dve.scalar_tensor_tensor(rows3(mixed[s % 2]), rows3(three[s % 2]), 1.0 / (HOPS + 1), degrees(dinv, g),
                                         ALU.mult, ALU.mult).then_inc(w.v.sem, 1)
                dve.wait_ge(w.v.sem, w.v.at(g + 1))
                dve.tensor_tensor(x2[s][:, :], mixed[s % 2][:, :], x1[s][:, :], ALU.add).then_inc(w.x.sem, 1)
            return mix

        def first_hops():
            for k in range(HOPS - 1):
                tile_phase(f"f1{k}", T, [(T.other, y_tab[k % 2], 0, D)], D,
                           lambda sums, y: [(hop_tab[k], sums), (y_tab[(k + 1) % 2], y)], y_of=True)

        def last_hop():
            def norm_of(m, sums, rout):
                x1, h0, h1, x2, h = (m.ring(k, WR, [P, J * D]) for k in ("x1", "h0", "h1", "x2", "h"))
                two = m.ring("two", WR, [P, J * D])
                three, mixed = (m.ring(k, 2, [P, J * D]) for k in ("three", "mixed"))
                w = f_norm
                mix = mixed_x(w, x1, sums, two, three, mixed, x2)

                def pool_first(pool, g, s):
                    pool.tensor_tensor(two[s][:, :], h0[s][:, :], h1[s][:, :], ALU.add).then_inc(w.pre.sem, 1)

                def new_x(dve, g, s):
                    dve.wait_ge(w.pre.sem, w.pre.at(g + 1))
                    mix(dve, g, s)
                return Norm([(x1_tab, x1), (hop_tab[0], h0), (hop_tab[1], h1)], [(x2_tab, x2), (h_tab, h)], x2, h,
                            new_x, stored_x=True, steps=[w.pre, w.u, w.v], pool_first=pool_first)
            k = HOPS - 1
            tile_phase(f"f1{k}", T, [(T.other, y_tab[k % 2], 0, D)], D, norm_of=norm_of)

        def layer1_fast():
            first_hops()
            last_hop()

        def layer1_general():
            for k in range(HOPS):
                edge_phase(f"e1{k}", [(S, y_tab[k % 2], 0, D)], T, hop_tab[k], D, mark=k == 0)
                if k < HOPS - 1:
                    with Memory(nc, f"n2{k}") as m:
                        hop, y = (m.ring(n, NR, [P, J * D]) for n in ("hop", "y"))

                        def compute(dve, g, s):
                            dve.tensor_tensor(rows3(y[s]), rows3(hop[s]), degrees(dinv2, g),
                                              ALU.mult).then_inc(q.ready.sem, 1)
                        plain_phase([(hop_tab[k], hop)], [(y_tab[(k + 1) % 2], y)], compute, w=g_norm, ready=q.ready)
            with Memory(nc, "n3") as m:
                x1, h0, h1, h2, two, three, mixed, x2, h = (m.ring(k, NR if k not in ("three", "mixed") else 2, [P, J * D])
                                                            for k in ("x1", "h0", "h1", "h2", "two", "three", "mixed",
                                                                      "x2", "h"))
                w = g_norm
                mix = mixed_x(w, x1, h2, two, three, mixed, x2)

                def pool_first(pool, g, s):
                    pool.tensor_tensor(two[s][:, :], h0[s][:, :], h1[s][:, :], ALU.add).then_inc(w.pre.sem, 1)

                def before(dve, g, s):
                    dve.wait_ge(w.pre.sem, w.pre.at(g + 1))
                    mix(dve, g, s)
                norm_phase(m, h, [(x1_tab, x1), (hop_tab[0], h0), (hop_tab[1], h1), (hop_tab[2], h2)],
                           [(x2_tab, x2), (h_tab, h)], x2, before, pool_first=pool_first, stored_resid=True, w=w)
                w.u.end(TILES)
                w.v.end(TILES)
        either(layer1_fast, layer1_general)

        either(lambda: tile_phase("f2", S, [(S.other, h_tab, 0, D)], D, lambda total, y: [(x2_tab, total)], add=x2_tab),
               lambda: edge_phase("e2", [(T, h_tab, 0, D)], S, x2_tab, D))

        with Memory(nc, "n4") as m:
            x3, hn = (m.ring(k, NR, [P, J * D]) for k in ("x3", "h"))
            hw, att = (m.ring(k, NR, [P, J * A]) for k in ("hw", "att"))
            as_ = m.ring("as", NR, [P, J])
            norm_phase(m, hn, [(x2_tab, x3)], [(hw_tab, hw), (as_tab, as_), (att_tab, att)], x3,
                       project=(hw, as_, att))

        either(lambda: tile_phase("f3", S, [(S.other, hw_tab, 0, A)], A,
                                  lambda total, y: [(att_tab, total)], make="attend", add=att_tab),
               lambda: edge_phase("e3", [(T, hw_tab, 0, A), (S, as_tab, A, 1)], S, att_tab, A, make="attend"))

        with Memory(nc, "n5") as m:
            x3, share, y = (m.ring(k, NR, [P, J * D]) for k in ("x3", "share", "y"))
            att = m.ring("att", NR, [P, J * A])
            rden = m.ring("rden", NR, [P, J])

            w = n_signals

            def compute(dve, g, s):
                dve.reciprocal(rden[s][:, :].unsqueeze(2), rows3(att[s], A)[:, :, D:A]).then_inc(w.u.sem, 1)
                dve.wait_ge(w.u.sem, w.u.at(g + 1))
                dve.tensor_tensor(rows3(share[s]), rows3(att[s], A)[:, :, 0:D], bc(rden[s][:, :]),
                                  ALU.mult).then_inc(w.v.sem, 1)
                dve.wait_ge(w.v.sem, w.v.at(g + 1))
                dve.tensor_tensor(y[s][:, :], x3[s][:, :], share[s][:, :], ALU.add).then_inc(w.ready.sem, 1)

            plain_phase([(x2_tab, x3), (att_tab, att)], [(out, y)], compute, more=[w.u, w.v])


_INS = ["x", "src", "dst", "L0_gnn_W1", "L0_gnn_b1", "L0_gnn_W2", "L0_gnn_b2", "L0_gnn_Wg", "L0_gnn_bg",
        "L3_gnn_W", "L3_gnn_a"]


def kernel(**inputs):
    import numpy as _np
    import concourse.bacc as _bacc
    from concourse import mybir as _mybir
    from concourse.bass_utils import run_bass_kernel_spmd as _run

    nc = _bacc.Bacc("TRN2", target_bir_lowering=False, num_devices=1)
    arrays, args = {}, []
    for name in _INS:
        a = _np.ascontiguousarray(inputs[name])
        arrays[f"in_{name}_dram"] = a
        args.append(nc.dram_tensor(f"in_{name}_dram", a.shape, _mybir.dt.from_np(a.dtype), kind="ExternalInput").ap())
    shape = _np.asarray(inputs["x"]).shape
    args.append(nc.dram_tensor("out_0_dram", shape, _mybir.dt.float32, kind="ExternalOutput").ap())
    gnn_kernel(nc, *args)
    r = _run(nc, [arrays], core_ids=[0])
    return r.results[0]["out_0_dram"]
```
